# Optimizing a Trainium2 kernel written in Bass

```python
import numpy as np
import jax
import jax.numpy as jnp

def _softmax(x, axis=-1):
    return jax.nn.softmax(x, axis=axis)

def _gelu(x):
    return jax.nn.gelu(x, approximate=True)

def _silu(x):
    return jax.nn.silu(x)

def _sigmoid(x):
    return jax.nn.sigmoid(x)

def _layernorm(x, axis=-1, eps=1e-05):
    m = jnp.mean(x, axis=axis, keepdims=True)
    v = jnp.var(x, axis=axis, keepdims=True)
    return (x - m) / jnp.sqrt(v + eps)

def _scatter_add(tgt, idx, src, axis=0):
    return tgt.at[idx].add(src)

def _segment_sum(src, seg, n):
    return jax.ops.segment_sum(src, seg, n)
kernel_name = 'mk_hybrid_d1_jaxref_r4_b861d9'

def setup_inputs(seed: int=0):
    np.random.seed(seed)
    _w = jnp.asarray

    def _L0_attn_a_setup():
        import jax, jax.numpy as jnp
        import numpy as np
        D_HEAD = 128
        ROTARY_BASE = 10000.0
        NEG = 1e+30

        def frac_rope(x, base=ROTARY_BASE):
            rot, skip = jnp.split(x, 2, axis=-1)
            T, W = (rot.shape[-2], rot.shape[-1])
            pos = jnp.arange(T)[:, None]
            dims = jnp.arange(W // 2)
            ang = jnp.power(base, -dims / (W // 2))[None, :]
            rad = pos * ang
            cos = jnp.cos(rad).astype(x.dtype)
            sin = jnp.sin(rad).astype(x.dtype)
            even, odd = jnp.split(rot, 2, axis=-1)
            r_even = even * cos - odd * sin
            r_odd = even * sin + odd * cos
            return jnp.concatenate([r_even, r_odd, skip], axis=-1)
        key = jax.random.key(seed)
        B, T, M, D = (4, 512, 256, D_HEAD)
        H = M // D
        ks = jax.random.split(key, 5)
        scale = M ** (-0.5)
        x = jax.random.normal(ks[0], (B, T, M), dtype=jnp.float32)
        wq = jax.random.normal(ks[1], (M, H, D), dtype=jnp.float32) * scale
        wk = jax.random.normal(ks[2], (M, H, D), dtype=jnp.float32) * scale
        wv = jax.random.normal(ks[3], (M, H, D), dtype=jnp.float32) * scale
        wo = jax.random.normal(ks[4], (H, D, M), dtype=jnp.float32) * scale
        return {'x': x, 'wq': wq, 'wk': wk, 'wv': wv, 'wo': wo}
    _L0_attn_a_in = _L0_attn_a_setup()

    def _L0_attn_b_setup():
        import jax, jax.numpy as jnp
        import numpy as np
        B, T, D = (4, 512, 256)
        H, DK = (8, 64)
        EPS = 1e-06

        def _xavier(key, shape):
            fan_in, fan_out = (shape[1], shape[0])
            lim = float(np.sqrt(6.0 / (fan_in + fan_out)))
            return jax.random.uniform(key, shape, jnp.float32, -lim, lim)

        def _phi(u):
            return jax.nn.elu(u) + 1.0
        key = jax.random.key(seed)
        ks = jax.random.split(key, 7)
        x = jax.random.normal(ks[0], (B, T, D), jnp.float32)
        W_Q = _xavier(ks[1], (H * DK, D))
        W_K = _xavier(ks[2], (H * DK, D))
        W_V = _xavier(ks[3], (H * DK, D))
        W_g_w = _xavier(ks[4], (H * DK, D))
        W_g_b = jax.random.normal(ks[5], (H * DK,), jnp.float32) * 0.02
        W_O = _xavier(ks[6], (D, H * DK))
        decay_log = jnp.zeros((H,), jnp.float32)
        return {'x': x, 'W_Q': W_Q, 'W_K': W_K, 'W_V': W_V, 'W_g_w': W_g_w, 'W_g_b': W_g_b, 'W_O': W_O, 'decay_log': decay_log}
    _L0_attn_b_in = _L0_attn_b_setup()

    def _L0_ffn_setup():
        import jax, jax.numpy as jnp
        import numpy as np
        DIM = 256
        HIDDEN = 768
        SCALE = 1.0 / 127.0

        def _dequant(w_int, dtype):
            return w_int.astype(dtype) * jnp.asarray(SCALE, dtype)
        key = jax.random.key(seed)
        k_x, k_g, k_u, k_d = jax.random.split(key, 4)
        x = jax.random.normal(k_x, (4, 512, DIM), dtype=jnp.float32)
        w_gate = jax.random.randint(k_g, (HIDDEN, DIM), -127, 128, dtype=jnp.int32)
        w_up = jax.random.randint(k_u, (HIDDEN, DIM), -127, 128, dtype=jnp.int32)
        w_down = jax.random.randint(k_d, (DIM, HIDDEN), -127, 128, dtype=jnp.int32)
        return {'x': x, 'w_gate': w_gate, 'w_up': w_up, 'w_down': w_down}
    _L0_ffn_in = _L0_ffn_setup()
    _d = {'L0_attn_a_x': _L0_attn_a_in['x'], 'L0_attn_a_wq': _L0_attn_a_in['wq'], 'L0_attn_a_wk': _L0_attn_a_in['wk'], 'L0_attn_a_wv': _L0_attn_a_in['wv'], 'L0_attn_a_wo': _L0_attn_a_in['wo'], 'L0_attn_b_W_Q': _L0_attn_b_in['W_Q'], 'L0_attn_b_W_K': _L0_attn_b_in['W_K'], 'L0_attn_b_W_V': _L0_attn_b_in['W_V'], 'L0_attn_b_W_g_w': _L0_attn_b_in['W_g_w'], 'L0_attn_b_W_g_b': _L0_attn_b_in['W_g_b'], 'L0_attn_b_W_O': _L0_attn_b_in['W_O'], 'L0_attn_b_decay_log': _L0_attn_b_in['decay_log'], 'L0_ffn_w_gate': _L0_ffn_in['w_gate'], 'L0_ffn_w_up': _L0_ffn_in['w_up'], 'L0_ffn_w_down': _L0_ffn_in['w_down']}
    _x0 = _d['L0_attn_a_x']
    _d['L0_attn_a_x'] = jax.random.normal(jax.random.fold_in(jax.random.key(seed), 1), (8, 1024, 256), dtype=_x0.dtype)
    del _x0
    return _d

def reference(L0_attn_a_x, L0_attn_a_wq, L0_attn_a_wk, L0_attn_a_wv, L0_attn_a_wo, L0_attn_b_W_Q, L0_attn_b_W_K, L0_attn_b_W_V, L0_attn_b_W_g_w, L0_attn_b_W_g_b, L0_attn_b_W_O, L0_attn_b_decay_log, L0_ffn_w_gate, L0_ffn_w_up, L0_ffn_w_down):

    def _L0_attn_a_ref(x, wq, wk, wv, wo):
        import jax, jax.numpy as jnp
        import numpy as np
        D_HEAD = 128
        ROTARY_BASE = 10000.0
        NEG = 1e+30

        def frac_rope(x, base=ROTARY_BASE):
            rot, skip = jnp.split(x, 2, axis=-1)
            T, W = (rot.shape[-2], rot.shape[-1])
            pos = jnp.arange(T)[:, None]
            dims = jnp.arange(W // 2)
            ang = jnp.power(base, -dims / (W // 2))[None, :]
            rad = pos * ang
            cos = jnp.cos(rad).astype(x.dtype)
            sin = jnp.sin(rad).astype(x.dtype)
            even, odd = jnp.split(rot, 2, axis=-1)
            r_even = even * cos - odd * sin
            r_odd = even * sin + odd * cos
            return jnp.concatenate([r_even, r_odd, skip], axis=-1)
        T = x.shape[1]
        q = jnp.einsum('btm,mhd->bhtd', x, wq)
        k = jnp.einsum('btm,mhd->bhtd', x, wk)
        v = jnp.einsum('btm,mhd->bhtd', x, wv)
        q = frac_rope(q) * D_HEAD ** (-0.5)
        k = frac_rope(k) * D_HEAD ** (-0.5)
        s = jnp.einsum('bhid,bhjd->bhij', q, k)
        i = jnp.arange(T)[:, None]
        j = jnp.arange(T)[None, :]
        s = s - NEG * jnp.less(i, j).astype(s.dtype)
        p = jax.nn.softmax(s, axis=-1)
        o = jnp.einsum('bhij,bhjd->bhid', p, v)
        return jnp.einsum('bhid,hdm->bim', o, wo)

    def _L0_attn_b_ref(x, W_Q, W_K, W_V, W_g_w, W_g_b, W_O, decay_log):
        import jax, jax.numpy as jnp
        import numpy as np
        B, T, D = (4, 512, 256)
        H, DK = (8, 64)
        EPS = 1e-06

        def _xavier(key, shape):
            fan_in, fan_out = (shape[1], shape[0])
            lim = float(np.sqrt(6.0 / (fan_in + fan_out)))
            return jax.random.uniform(key, shape, jnp.float32, -lim, lim)

        def _phi(u):
            return jax.nn.elu(u) + 1.0
        b, t, d = x.shape
        q = _phi((x @ W_Q.T).reshape(b, t, H, DK))
        k = _phi((x @ W_K.T).reshape(b, t, H, DK))
        v = (x @ W_V.T).reshape(b, t, H, DK)
        gamma = jax.nn.sigmoid(decay_log)
        g4 = gamma[None, :, None, None]
        g3 = gamma[None, :, None]
        qT = jnp.moveaxis(q, 1, 0)
        kT = jnp.moveaxis(k, 1, 0)
        vT = jnp.moveaxis(v, 1, 0)
        S0 = jnp.zeros((b, H, DK, DK), x.dtype)
        z0 = jnp.zeros((b, H, DK), x.dtype)

        def step(carry, inp):
            S, z = carry
            qt, kt, vt = inp
            S = g4 * S + jnp.einsum('bhi,bhj->bhij', kt, vt)
            z = g3 * z + kt
            num = jnp.einsum('bhij,bhi->bhj', S, qt)
            den = jnp.sum(z * qt, axis=-1, keepdims=True) + EPS
            return ((S, z), num / den)
        _, ys = jax.lax.scan(step, (S0, z0), (qT, kT, vT))
        outputs = jnp.moveaxis(ys, 0, 1)
        gate = jax.nn.sigmoid(x @ W_g_w.T + W_g_b).reshape(b, t, H, DK)
        y = (outputs * gate).reshape(b, t, H * DK)
        return y @ W_O.T

    def _L0_ffn_ref(x, w_gate, w_up, w_down):
        import jax, jax.numpy as jnp
        import numpy as np
        DIM = 256
        HIDDEN = 768
        SCALE = 1.0 / 127.0

        def _dequant(w_int, dtype):
            return w_int.astype(dtype) * jnp.asarray(SCALE, dtype)
        wg = _dequant(w_gate, x.dtype)
        wu = _dequant(w_up, x.dtype)
        wd = _dequant(w_down, x.dtype)
        gate = jnp.einsum('bsd,hd->bsh', x, wg)
        up = jnp.einsum('bsd,hd->bsh', x, wu)
        h = jax.nn.silu(gate) * up
        return jnp.einsum('bsh,dh->bsd', h, wd)
    x = L0_attn_a_x
    x = x + _L0_attn_a_ref(_layernorm(x, axis=-1), L0_attn_a_wq, L0_attn_a_wk, L0_attn_a_wv, L0_attn_a_wo)
    x = x + _L0_ffn_ref(_layernorm(x, axis=-1), L0_ffn_w_gate, L0_ffn_w_up, L0_ffn_w_down)
    x = x + _L0_attn_b_ref(_layernorm(x, axis=-1), L0_attn_b_W_Q, L0_attn_b_W_K, L0_attn_b_W_V, L0_attn_b_W_g_w, L0_attn_b_W_g_b, L0_attn_b_W_O, L0_attn_b_decay_log)
    x = x + _L0_ffn_ref(_layernorm(x, axis=-1), L0_ffn_w_gate, L0_ffn_w_up, L0_ffn_w_down)
    return x

_drawn_inputs = setup_inputs


def setup_inputs(seed=0):
    import zlib

    import numpy as np

    out = dict(_drawn_inputs(seed))
    spreads = {'L0_attn_b_decay_log': (0.0, 2.0)}
    factors = {'L0_attn_a_wq': 4.05,
     'L0_attn_a_wk': 4.001,
     'L0_attn_b_W_Q': 64.0,
     'L0_attn_b_W_K': 64.0,
     'L0_attn_b_W_V': 8.0,
     'L0_attn_b_W_g_w': 23.165,
     'L0_attn_b_W_g_b': 64.0,
     'L0_attn_b_W_O': 8.0}
    for name, (base, spread) in spreads.items():
        noise = np.random.default_rng([zlib.crc32(name.encode()), seed]).standard_normal(out[name].shape)
        drawn = base * np.exp(spread * noise) if base else spread * noise
        out[name] = jnp.asarray(drawn.astype(out[name].dtype))
    for name, factor in factors.items():
        out[name] = (out[name] * factor).astype(out[name].dtype)
    return out
```

```python
import concourse.bass as bass
from concourse import mybir
from contextlib import ExitStack
import numpy as np

F32 = mybir.dt.float32
F32R = mybir.dt.float32r
BF16 = mybir.dt.bfloat16
I32 = mybir.dt.int32
ALU = mybir.AluOpType
ACT = mybir.ActivationFunctionType
AX = mybir.AxisListType

P = 128
NB, T, M = 8, 1024, 256
KT = M // P
NT = NB * T // P
TB = T // P
UT = 4
UN = UT * P
NU = NT // UT
LN_EPS = 1e-5

HA, DA = 2, 128
ROT = DA // 2
HALF = ROT // 2
NQK = 3 * HA
WQK = NQK * P
QK_SCALE = 1.0 / DA
NEG = -1e30

FF = 768
NF = FF // P
W_SCALE = 1.0 / 127.0

HB, DK = 8, 64
HD = HB * DK
NP = HD // P
HG = 4
VA = DK + 1
DEN_EPS = 1e-6

CREDIT = 4


class Signal:

    def __init__(self, nc, ctx, name, per):
        self.sem = ctx.enter_context(nc.semaphore(name))
        self.per = per

    def at(self, turn, k):
        return turn * self.per + (CREDIT + k)


def open_signals(eng, *signals):
    for s in signals:
        eng.sem_inc(s.sem, CREDIT)


def wait_alone(eng, sem, value, passed):
    eng.wait_ge(sem, value)
    eng.sem_inc(passed, 1)


class Layernorm:

    def __init__(self, nc, ctx, name, tiles, X):
        sb = lambda n, shape: ctx.enter_context(nc.sbuf_tensor(f"{name}_{n}", shape, F32))
        self.nc, self.X, self.tiles = nc, X, tiles
        self.stats = sb("stats", [P, tiles, 6])
        self.mean_var = sb("mean_var", [P, tiles, 2])
        self.var_eps = sb("var_eps", [P, tiles])
        self.rstd = sb("rstd", [P, tiles])
        self.minus_half = sb("minus_half", [P, tiles])
        self.out = sb("xn", [P, tiles, M])
        self.stats_done = Signal(nc, ctx, f"{name}_stats_done", 1)
        self.mv_done = Signal(nc, ctx, f"{name}_mv_done", 1)
        self.ve_done = Signal(nc, ctx, f"{name}_ve_done", 1)
        self.rstd_done = Signal(nc, ctx, f"{name}_rstd_done", 1)
        self.dve_passed = ctx.enter_context(nc.semaphore(f"{name}_dve_passed"))
        self.pool_passed = ctx.enter_context(nc.semaphore(f"{name}_pool_passed"))
        self.consts = ctx.enter_context(nc.semaphore(f"{name}_consts"))
        self.ready = Signal(nc, ctx, f"{name}_ready", tiles // UT)

    def dve_open(self, dve):
        open_signals(dve, self.stats_done, self.mv_done, self.ready)

    def dve_stats(self, dve, turn):
        nc = self.nc
        for t in range(self.tiles):
            last = nc.vector.bn_stats(self.stats[:, t, :], self.X[:, bass.ds(turn * self.tiles + t, 1), :])
        last.then_inc(self.stats_done.sem, 1)
        wait_alone(dve, self.stats_done.sem, self.stats_done.at(turn, 1), self.dve_passed)
        for t in range(self.tiles):
            last = nc.vector.bn_aggr(self.mean_var[:, t, :], self.stats[:, t, :])
        last.then_inc(self.mv_done.sem, 1)

    def dve_normalise(self, dve, turn):
        nc = self.nc
        dve.wait_ge(self.rstd_done.sem, self.rstd_done.at(turn, 1))
        for t in range(self.tiles):
            last = nc.vector.tensor_scalar(self.out[:, t, :], self.X[:, bass.ds(turn * self.tiles + t, 1), :],
                                           self.mean_var[:, t, 0:1], self.rstd[:, t:t + 1],
                                           ALU.subtract, ALU.mult)
            if t % UT == UT - 1:
                last.then_inc(self.ready.sem, 1)

    def pool_open(self, pool):
        open_signals(pool, self.ve_done, self.rstd_done)
        self.nc.gpsimd.memset(self.minus_half[:], -0.5).then_inc(self.consts, 1)
        pool.wait_ge(self.consts, 1)

    def pool_rstd(self, pool, turn):
        nc = self.nc
        wait_alone(pool, self.mv_done.sem, self.mv_done.at(turn, 1), self.pool_passed)
        nc.gpsimd.tensor_scalar(self.var_eps[:], self.mean_var[:, :, 1], LN_EPS, None,
                                ALU.add).then_inc(self.ve_done.sem, 1)
        pool.wait_ge(self.ve_done.sem, self.ve_done.at(turn, 1))
        nc.gpsimd.tensor_tensor(self.rstd[:], self.var_eps[:], self.minus_half[:],
                                ALU.pow).then_inc(self.rstd_done.sem, 1)


class SplitTransposed:

    def __init__(self, nc, ctx, name, units, psum, ident, ln):
        sb = lambda n: ctx.enter_context(nc.sbuf_tensor(f"{name}_{n}", [P, KT, UN], F32R))
        self.nc, self.psum, self.ident, self.ln = nc, psum, ident, ln
        self.hi, self.lo = sb("xh"), sb("xl")
        self.transposed = Signal(nc, ctx, f"{name}_transposed", units)
        self.hi_done = Signal(nc, ctx, f"{name}_hi_done", units)
        self.lo_done = Signal(nc, ctx, f"{name}_lo_done", units)

    def pe(self, pe, turn, unit, tile0):
        ln = self.ln
        pe.wait_ge(ln.ready.sem, ln.ready.at(turn, unit + 1))
        for t in range(UT):
            for k in range(KT):
                last = self.nc.tensor.transpose(self.psum[:, k, t * P:(t + 1) * P],
                                                ln.out[:, tile0 + t, k * P:(k + 1) * P], self.ident[:])
        last.then_inc(self.transposed.sem, 1)

    def act(self, act, turn, unit):
        act.wait_ge(self.transposed.sem, self.transposed.at(turn, unit + 1))
        self.nc.scalar.activation(self.hi[:], self.psum, ACT.Copy).then_inc(self.hi_done.sem, 1)

    def dve(self, dve, turn, unit):
        dve.wait_ge(self.hi_done.sem, self.hi_done.at(turn, unit + 1))
        self.nc.vector.tensor_tensor(self.lo[:], self.psum, self.hi[:].bitcast(F32),
                                     ALU.subtract).then_inc(self.lo_done.sem, 1)

    def pe_wait(self, pe, turn, unit):
        pe.wait_ge(self.hi_done.sem, self.hi_done.at(turn, unit + 1))
        pe.wait_ge(self.lo_done.sem, self.lo_done.at(turn, unit + 1))

    def terms(self, w_hi, w_lo, k):
        return [(w_hi, self.hi[:, k, :]), (w_hi, self.lo[:, k, :]), (w_lo, self.hi[:, k, :]),
                (w_lo, self.lo[:, k, :])]


def project(nc, out, sx, w_hi, w_lo, cols):
    terms = [t for k in range(KT) for t in sx.terms(w_hi[:, k, cols], w_lo[:, k, cols], k)[:PROJ_TERMS]]
    for n, (w, x) in enumerate(terms):
        last = nc.tensor.matmul(out, w, x, start=n == 0, stop=n == len(terms) - 1)
    return last


def project_tokens(nc, out, sx, w_hi, w_lo, cols, tile):
    at = slice(tile * P, (tile + 1) * P)
    terms = [t for k in range(KT) for t in sx.terms(w_hi[:, k, cols], w_lo[:, k, cols], k)[:PROJ_TERMS]]
    for n, (w, x) in enumerate(terms):
        last = nc.tensor.matmul(out, x[:, at], w, start=n == 0, stop=n == len(terms) - 1)
    return last


PROJ_TERMS = 3


def attention_phase(nc, env, io):
    X, PS, ident = env["X"], env["PS"], env["ident"]
    with ExitStack() as ctx:
        sb = lambda n, shape, dt=F32: ctx.enter_context(nc.sbuf_tensor(n, shape, dt))
        sem = lambda n: ctx.enter_context(nc.semaphore(n))
        sig = lambda n, per: Signal(nc, ctx, n, per)

        wqkv_hi = sb("wqkv_hi", [P, KT, WQK + HA * DA], F32R)
        wqkv_lo = sb("wqkv_lo", [P, KT, WQK + HA * DA], F32R)
        wo = sb("wo_a", [P, HA, M])
        cos = sb("cos", [P, HA, T])
        sin = sb("sin", [P, T])
        mask_f = sb("mask_f", [P, P])
        mask_b = sb("mask_b", [P, P], BF16)
        ident_b = sb("ident_b", [P, P], BF16)
        ln = Layernorm(nc, ctx, "a_ln", TB, X)
        sx = SplitTransposed(nc, ctx, "a", 2, PS[:, 4:6, :], ident, ln)
        qk = sb("qk", [P, 2, HA, T])
        wqkv_raw = qk[:].rearrange("p s h t -> p (s h t)")[:, 0:KT * (WQK + HA * DA)].rearrange("p (k n) -> p k n", k=KT)
        swapped = sb("swapped", [P, 2, UN])
        V = sb("v_a", [P, TB, HA * DA])
        prob = sb("prob", [P, 2, T])
        neg_max = sb("neg_max", [P, 2])
        row_sum = sb("row_sum", [P, 2])
        row_inv = sb("row_inv", [P, 2])
        probT = [sb("probT_a", [P, UT, UN]), sb("probT_b", [P, TB, UN])]
        oT = sb("oT", [P, HA, T])

        NQB = T // UN
        steps = [(h, i) for h in range(HA) for i in range(TB)]
        NS = len(steps)
        groups = [(i + UT) // UT for _, i in steps]
        first_group = [sum(groups[:n]) for n in range(NS + 1)]
        NG = first_group[NS]

        const_loaded, w_loaded, x_loaded = sem("a_const_loaded"), sem("a_w_loaded"), sem("x_loaded")
        prep_hi, prep_done = sem("a_prep_hi"), sem("a_prep_done")
        proj_ready, proj_used = sig("a_proj_ready", 2 * NQK), sig("a_proj_used", 2 * NQK)
        rotated = sig("a_rotated", 4)
        v_ready, v_done = sig("a_v_ready", TB), sig("a_v_done", TB)
        s_ready, max_done, p_done = sig("s_ready", NS), sig("max_done", NS), sig("p_done", NS)
        inv_done, pn_done = sig("inv_done", NS), sig("pn_done", NS)
        pt_ready, pt_done = sig("pt_ready", NG), sig("pt_done", NG)
        o_ready, o_done = sig("a_o_ready", HA * NQB), sig("a_o_done", HA * NQB)
        y_ready, y_done = sig("a_y_ready", TB // 2), sig("a_y_done", TB // 2)

        x_v = io["x"].rearrange("b (n p) m -> p (b n) m", p=P)
        N_CONST = 4
        passed = sem("sp_passed")

        with nc.Block() as block:

            @block.sync
            def _(sp):
                with sp.Fori(0, NB) as b:
                    at = bass.ds(b * TB, TB)
                    sp.dma_start(X[:, at, :], x_v[:, at, :]).then_inc(x_loaded, 16)
                    wait_alone(sp, x_loaded, (b + 1) * 16, passed)
                load_ff_weights(sp, env, io)

            def rope_block(b_turn, half):
                return slice(half * UN, (half + 1) * UN)

            @block.gpsimd
            def _(pool):
                open_signals(pool, rotated)
                ln.pool_open(pool)

                def turn(b, last):
                    for half in range(2):
                        at = slice(half * UN, (half + 1) * UN)
                        for s in range(2):
                            pool.wait_ge(proj_used.sem, proj_used.at(b, NQK * half + 3 * (s + 1)))
                            r = (2 * half + s) % 2
                            for h in range(HA):
                                rows = slice(h * ROT, (h + 1) * ROT)
                                done = nc.gpsimd.tensor_tensor(qk[rows, s, h, at], qk[rows, s, h, at],
                                                               swapped[rows, r, :], ALU.add)
                            done.then_inc(rotated.sem, 1)
                    if not last:
                        ln.pool_rstd(pool, b + 1)

                ln.pool_rstd(pool, 0)
                with pool.Fori(0, NB - 1) as b:
                    turn(b, False)
                turn(NB - 1, True)

            @block.scalar
            def _(act):
                open_signals(act, sx.hi_done, v_done, p_done, pt_done, o_done)
                act.dma_start(wqkv_raw, io["w_qkv"].rearrange("(k p) n -> p k n", p=P)).then_inc(w_loaded, 16)
                act.dma_start(ident[:], io["ident"]).then_inc(const_loaded, 16)
                act.dma_start(mask_f[:], io["causal"]).then_inc(const_loaded, 16)
                act.dma_start(cos[:], io["cos"]).then_inc(const_loaded, 16)
                act.dma_start(sin[:], io["sin"]).then_inc(const_loaded, 16)
                act.dma_start(wo[:], io["wo_a"].rearrange("(h p) n -> p h n", p=P)).then_inc(w_loaded, 16)
                act.wait_ge(const_loaded, 16 * N_CONST)

                def exp_step(b, n):
                    i = steps[n][1]
                    act.wait_ge(max_done.sem, max_done.at(b, n + 1))
                    act.wait_ge(pt_ready.sem, pt_ready.at(b, first_group[n - 1] if n >= 2 else
                                                          first_group[NS - 1 + n] - NG))
                    nc.scalar.activation(prob[:, n % 2, 0:(i + 1) * P],
                                         PS[:, 2 * (n % 2):2 * (n % 2) + 2, :].rearrange("p a b -> p (a b)")[:, 0:(i + 1) * P],
                                         ACT.Exp, bias=neg_max[:, n % 2:n % 2 + 1],
                                         accum_out=row_sum[:, n % 2:n % 2 + 1]).then_inc(p_done.sem, 1)

                def evacuate_step(b, n):
                    i = steps[n][1]
                    for g in range(groups[n]):
                        c = first_group[n] + g
                        js = slice(g * UT, min((g + 1) * UT, i + 1))
                        act.wait_ge(pt_ready.sem, pt_ready.at(b, c + 1))
                        q = (i % UT) * P
                        nc.scalar.activation(probT[i // UT][:, js, q:q + P],
                                             PS[:, 4 + c % 2, 0:(js.stop - js.start) * P].rearrange("p (j q) -> p j q", q=P),
                                             ACT.Copy).then_inc(pt_done.sem, 1)

                def evacuate_out(b, k):
                    h, qb = k // NQB, k % NQB
                    act.wait_ge(o_ready.sem, o_ready.at(b, k + 1))
                    nc.scalar.activation(oT[:, h, qb * UN:(qb + 1) * UN], PS[:, 6, :], ACT.Copy).then_inc(o_done.sem, 1)

                def turn(b):
                    for half in range(2):
                        sx.act(act, b, half)
                        for t in range(UT * half, UT * (half + 1)):
                            act.wait_ge(v_ready.sem, v_ready.at(b, t + 1))
                            nc.scalar.activation(V[:, t, :], PS[:, 6 + t % 2, 0:HA * DA], ACT.Copy).then_inc(v_done.sem, 1)
                    exp_step(b, 0)
                    for n in range(NS):
                        if n + 1 < NS:
                            exp_step(b, n + 1)
                        evacuate_step(b, n)
                        if n % UT == 0 and n > 0:
                            evacuate_out(b, n // UT - 1)
                    evacuate_out(b, HA * NQB - 1)

                with act.Fori(0, NB) as b:
                    turn(b)

            @block.vector
            def _(dve):
                open_signals(dve, sx.lo_done, proj_used, max_done, inv_done, pn_done, y_done)
                ln.dve_open(dve)
                dve.wait_ge(w_loaded, 32)
                nq = WQK // 2
                nc.vector.tensor_scalar(wqkv_hi[:, :, 0:nq], wqkv_raw[:, :, 0:nq], QK_SCALE, None, ALU.mult).then_inc(prep_hi, 1)
                nc.vector.tensor_copy(wqkv_hi[:, :, nq:], wqkv_raw[:, :, nq:]).then_inc(prep_hi, 1)
                dve.wait_ge(prep_hi, 2)
                nc.vector.scalar_tensor_tensor(wqkv_lo[:, :, 0:nq], wqkv_raw[:, :, 0:nq], QK_SCALE,
                                               wqkv_hi[:, :, 0:nq].bitcast(F32), ALU.mult, ALU.subtract).then_inc(prep_done, 1)
                nc.vector.tensor_tensor(wqkv_lo[:, :, nq:], wqkv_raw[:, :, nq:], wqkv_hi[:, :, nq:].bitcast(F32),
                                        ALU.subtract).then_inc(prep_done, 1)
                dve.wait_ge(const_loaded, 16 * N_CONST)
                nc.vector.tensor_copy(ident_b[:], ident[:]).then_inc(prep_done, 1)
                nc.vector.tensor_copy(mask_b[:], mask_f[:]).then_inc(prep_done, 1)

                def stats(b):
                    dve.wait_ge(x_loaded, (b + 1) * 16)
                    ln.dve_stats(dve, b)

                def row_max(b, n):
                    i = steps[n][1]
                    dve.wait_ge(s_ready.sem, s_ready.at(b, n + 1))
                    nc.vector.tensor_reduce(neg_max[:, n % 2:n % 2 + 1],
                                            PS[:, 2 * (n % 2):2 * (n % 2) + 2, :].rearrange("p a b -> p (a b)")[:, 0:(i + 1) * P],
                                            AX.X, ALU.max, negate=True).then_inc(max_done.sem, 1)

                def normalise(b, n):
                    i = steps[n][1]
                    dve.wait_ge(p_done.sem, p_done.at(b, n + 1))
                    nc.vector.reciprocal(row_inv[:, n % 2:n % 2 + 1], row_sum[:, n % 2:n % 2 + 1]).then_inc(inv_done.sem, 1)
                    dve.wait_ge(inv_done.sem, inv_done.at(b, n + 1))
                    row = prob[:, n % 2, 0:(i + 1) * P]
                    nc.vector.tensor_scalar(row, row, row_inv[:, n % 2:n % 2 + 1], None, ALU.mult).then_inc(pn_done.sem, 1)

                def residual(b, pair):
                    dve.wait_ge(y_ready.sem, y_ready.at(b, pair + 1))
                    x = X[:, bass.ds(b * TB + 2 * pair, 2), :].rearrange("p a m -> p (a m)")
                    nc.vector.tensor_tensor(x, PS[:, 7, :], x, ALU.add).then_inc(y_done.sem, 1)

                def turn(b, last):
                    for half in range(2):
                        sx.dve(dve, b, half)
                        at = slice(half * UN, (half + 1) * UN)
                        for s in range(2):
                            for j in range(3):
                                m = NQK * half + 3 * s + j
                                dve.wait_ge(proj_ready.sem, proj_ready.at(b, m + 1))
                                if j < HA:
                                    dst, table = qk[:, s, j, at], cos[:, j, at]
                                else:
                                    r = (2 * half + s) % 2
                                    dve.wait_ge(rotated.sem, rotated.at(b, 2 * half + s - 1))
                                    dst, table = swapped[:, r, :], sin[:, at]
                                nc.vector.tensor_tensor(dst, PS[:, m % 4, :], table, ALU.mult).then_inc(proj_used.sem, 1)
                    row_max(b, 0)
                    for n in range(NS):
                        if n + 1 < NS:
                            row_max(b, n + 1)
                        normalise(b, n)
                        if n == 4 and not last:
                            stats(b + 1)
                        if n == 8 and not last:
                            ln.dve_normalise(dve, b + 1)
                        if n == 13:
                            for pair in range(TB // 4):
                                residual(b, pair)
                    for pair in range(TB // 4, TB // 2):
                        residual(b, pair)

                stats(0)
                ln.dve_normalise(dve, 0)
                with dve.Fori(0, NB - 1) as b:
                    turn(b, False)
                turn(NB - 1, True)

            @block.tensor
            def _(pe):
                open_signals(pe, sx.transposed, proj_ready, v_ready, s_ready, pt_ready, o_ready, y_ready)
                pe.wait_ge(prep_done, 4)

                def scores(b, n):
                    h, i = steps[n]
                    pe.wait_ge(p_done.sem, p_done.at(b, n - 1))
                    keys = (i + 1) * P
                    for c in range(0, keys, UN):
                        w = min(UN, keys - c)
                        diag = c + w == keys
                        bank = PS[:, 2 * (n % 2) + c // UN, :]
                        last = nc.tensor.matmul(bank[:, 0:w], qk[:, 0, h, i * P:(i + 1) * P], qk[:, 1, h, c:c + w],
                                                start=True, stop=not diag)
                        if diag:
                            last = nc.tensor.matmul(bank[:, w - P:w], ident_b[:], mask_b[:], start=False, stop=True)
                    last.then_inc(s_ready.sem, 1)

                def transpose_probs(b, n):
                    i = steps[n][1]
                    pe.wait_ge(pn_done.sem, pn_done.at(b, n + 1))
                    for g in range(groups[n]):
                        c = first_group[n] + g
                        pe.wait_ge(pt_done.sem, pt_done.at(b, c - 1))
                        for j in range(g * UT, min((g + 1) * UT, i + 1)):
                            last = nc.tensor.transpose(PS[:, 4 + c % 2, (j % UT) * P:(j % UT + 1) * P],
                                                       prob[:, n % 2, j * P:(j + 1) * P], ident[:])
                        last.then_inc(pt_ready.sem, 1)

                def weighted_values(b, k):
                    h, qb = k // NQB, k % NQB
                    pe.wait_ge(pt_done.sem, pt_done.at(b, first_group[UT * (k + 1)]))
                    pe.wait_ge(o_done.sem, o_done.at(b, k))
                    nj = UT * (qb + 1)
                    for j in range(nj):
                        q0 = max(0, j - UT * qb) * P
                        last = nc.tensor.matmul(PS[:, 6, q0:UN], V[:, j, h * DA:(h + 1) * DA], probT[qb][:, j, q0:UN],
                                                start=j == 0, stop=j == nj - 1)
                    last.then_inc(o_ready.sem, 1)

                def out_projection(b, qb):
                    pe.wait_ge(o_done.sem, o_done.at(b, NQB * (HA - 1) + qb + 1))
                    for pair in range(2 * qb, 2 * qb + 2):
                        pe.wait_ge(y_done.sem, y_done.at(b, pair))
                        for t in range(2):
                            at = slice((2 * pair + t) * P, (2 * pair + t + 1) * P)
                            for h in range(HA):
                                last = nc.tensor.matmul(PS[:, 7, t * M:(t + 1) * M], oT[:, h, at], wo[:, h, :],
                                                        start=h == 0, stop=h == HA - 1)
                        last.then_inc(y_ready.sem, 1)

                def turn(b):
                    pe.wait_ge(p_done.sem, p_done.at(b, 0))
                    pe.wait_ge(pt_done.sem, pt_done.at(b, 0))
                    pe.wait_ge(y_done.sem, y_done.at(b, 0))
                    for half in range(2):
                        sx.pe(pe, b, half, UT * half)
                        sx.pe_wait(pe, b, half)
                        for j in range(NQK):
                            m = NQK * half + j
                            pe.wait_ge(proj_used.sem, proj_used.at(b, m - 3))
                            project(nc, PS[:, m % 4, :], sx, wqkv_hi, wqkv_lo,
                                    slice(j * P, (j + 1) * P)).then_inc(proj_ready.sem, 1)
                        for t in range(UT):
                            tile = UT * half + t
                            pe.wait_ge(v_done.sem, v_done.at(b, tile - 1))
                            project_tokens(nc, PS[:, 6 + tile % 2, 0:HA * DA], sx, wqkv_hi, wqkv_lo,
                                           slice(WQK, WQK + HA * DA), t).then_inc(v_ready.sem, 1)
                    pe.wait_ge(proj_used.sem, proj_used.at(b, 2 * NQK))
                    pe.wait_ge(rotated.sem, rotated.at(b, 4))
                    pe.wait_ge(v_done.sem, v_done.at(b, TB))
                    scores(b, 0)
                    for n in range(NS):
                        if n + 1 < NS:
                            scores(b, n + 1)
                        transpose_probs(b, n)
                        if n % UT == 0 and n > 0:
                            weighted_values(b, n // UT - 1)
                        if n == NS - 3:
                            out_projection(b, 0)
                    weighted_values(b, HA * NQB - 1)
                    out_projection(b, 1)

                with pe.Fori(0, NB) as b:
                    turn(b)


def load_ff_weights(eng, env, io):
    stage = env["stage"].bitcast(I32)
    for n, name in enumerate(("w_gate", "w_up")):
        eng.dma_start(stage[:, n * KT * FF:(n + 1) * KT * FF].rearrange("p (k f) -> p k f", k=KT),
                      io[name].rearrange("(k p) f -> p k f", p=P)).then_inc(env["ff_loaded"], 16)
    eng.dma_start(stage[:, 2 * KT * FF:2 * KT * FF + NF * M].rearrange("p (k m) -> p k m", k=NF),
                  io["w_down"].rearrange("(k p) m -> p k m", p=P)).then_inc(env["ff_loaded"], 16)


LB_COLS = 4 * HD


def load_lin_weights(eng, env, io):
    stage = env["stage"]
    eng.dma_start(stage[:, 0:KT * LB_COLS].rearrange("p (k n) -> p k n", k=KT),
                  io["w_lin"].rearrange("(k p) n -> p k n", p=P)).then_inc(env["lin_loaded"], 16)
    eng.dma_start(stage[:, KT * LB_COLS:KT * LB_COLS + NP * M].rearrange("p (k m) -> p k m", k=NP),
                  io["w_o"].rearrange("(k p) m -> p k m", p=P)).then_inc(env["lin_loaded"], 16)


def feed_forward_phase(nc, env, io, name, nth, final):
    X, PS, ident, stage = env["X"], env["PS"], env["ident"], env["stage"]
    with ExitStack() as ctx:
        sb = lambda n, shape, dt=F32: ctx.enter_context(nc.sbuf_tensor(f"{name}_{n}", shape, dt))
        sem = lambda n: ctx.enter_context(nc.semaphore(f"{name}_{n}"))
        sig = lambda n, per: Signal(nc, ctx, f"{name}_{n}", per)

        NW = 2 * KT * FF + NF * M
        w_hi, w_lo = sb("w_hi", [P, NW], F32R), sb("w_lo", [P, NW], F32R)
        gu = lambda w, n: w[:, n * KT * FF:(n + 1) * KT * FF].rearrange("p (k f) -> p k f", k=KT)
        gate_hi, up_hi, gate_lo, up_lo = gu(w_hi, 0), gu(w_hi, 1), gu(w_lo, 0), gu(w_lo, 1)
        down_hi, down_lo = (w[:, 2 * KT * FF:].rearrange("p (k m) -> p k m", k=NF) for w in (w_hi, w_lo))
        low_max = sb("low_max", [P, 1])
        low_row = sb("low_row", [1, P])
        low_any = sb("low_any", [1, 1])
        ln = Layernorm(nc, ctx, f"{name}_ln", UT, X)
        sx = SplitTransposed(nc, ctx, name, 1, PS[:, 0:2, :], ident, ln)
        silu = sb("silu", [P, 2, UN])
        h = sb("h", [P, 2, UN])
        NH = 3
        h_hi, h_lo = sb("h_hi", [P, NH, UN], F32R), sb("h_lo", [P, NH, UN], F32R)

        prep = sem("prep")
        low_t, low_done = sem("low_t"), sem("low_done")
        gate_ready, up_ready = sig("gate_ready", NF), sig("up_ready", NF)
        silu_done, h_done = sig("silu_done", NF), sig("h_done", NF)
        hi_done, lo_done, down_done = sig("h_hi_done", NF), sig("h_lo_done", NF), sig("down_done", NF)
        x_done = sig("x_done", 1)
        stored = sem("stored")
        Y = PS[:, 6:8, :]
        out_v = io["out"].rearrange("b (n p) m -> p (b n) m", p=P)

        with nc.Block() as block:

            @block.sync
            def _(sp):
                if final:
                    with sp.Fori(0, NU) as u:
                        sp.wait_ge(x_done.sem, x_done.at(u, 1))
                        at = bass.ds(u * UT, UT)
                        sp.dma_start(out_v[:, at, :], X[:, at, :]).then_inc(stored, 16)
                    sp.wait_ge(stored, 16 * NU)
                else:
                    sp.wait_ge(prep, 3)
                    load_lin_weights(sp, env, io)

            @block.gpsimd
            def _(pool):
                ln.pool_open(pool)
                ln.pool_rstd(pool, 0)
                with pool.Fori(0, NU - 1) as u:
                    ln.pool_rstd(pool, u + 1)

            @block.scalar
            def _(act):
                open_signals(act, sx.hi_done, silu_done, hi_done)

                def high_part(u, f):
                    act.wait_ge(h_done.sem, h_done.at(u, f + 1))
                    act.wait_ge(down_done.sem, down_done.at(u, f - NH + 1))
                    nc.scalar.activation(h_hi[:, f % NH, :], h[:, f % 2, :], ACT.Copy).then_inc(hi_done.sem, 1)

                def turn(u):
                    sx.act(act, u, 0)
                    for f in range(NF):
                        act.wait_ge(gate_ready.sem, gate_ready.at(u, f + 1))
                        act.wait_ge(h_done.sem, h_done.at(u, f - 1))
                        nc.scalar.activation(silu[:, f % 2, :], PS[:, 2 + f % 2, :], ACT.Silu,
                                             scale=W_SCALE).then_inc(silu_done.sem, 1)
                        if f > 0:
                            high_part(u, f - 1)
                    high_part(u, NF - 1)

                with act.Fori(0, NU) as u:
                    turn(u)

            @block.vector
            def _(dve):
                open_signals(dve, sx.lo_done, h_done, lo_done, x_done)
                ln.dve_open(dve)
                dve.wait_ge(env["ff_loaded"], 48 * nth)
                raw = stage[:, 0:NW]
                nc.vector.tensor_copy(raw, raw.bitcast(I32)).then_inc(prep, 1)
                dve.wait_ge(prep, 1)
                nc.vector.tensor_copy(w_hi[:], raw).then_inc(prep, 1)
                dve.wait_ge(prep, 2)
                nc.vector.tensor_tensor(w_lo[:], raw, w_hi[:].bitcast(F32), ALU.subtract).then_inc(prep, 1)
                dve.wait_ge(prep, 3)
                nc.vector.tensor_reduce(low_max[:], w_lo[:].bitcast(F32), AX.X, ALU.max,
                                        apply_absolute_value=True).then_inc(prep, 1)
                dve.wait_ge(low_t, 1)
                nc.vector.tensor_reduce(low_any[:], PS[0:1, 7, 0:P], AX.X, ALU.max).then_inc(low_done, 1)

                def low_part(u, f):
                    dve.wait_ge(hi_done.sem, hi_done.at(u, f + 1))
                    dve.wait_ge(down_done.sem, down_done.at(u, f - NH + 1))
                    nc.vector.tensor_tensor(h_lo[:, f % NH, :], h[:, f % 2, :], h_hi[:, f % NH, :].bitcast(F32),
                                            ALU.subtract).then_inc(lo_done.sem, 1)

                def turn(u, last):
                    sx.dve(dve, u, 0)
                    for f in range(NF):
                        dve.wait_ge(up_ready.sem, up_ready.at(u, f + 1))
                        dve.wait_ge(silu_done.sem, silu_done.at(u, f + 1))
                        dve.wait_ge(lo_done.sem, lo_done.at(u, f - 1))
                        nc.vector.scalar_tensor_tensor(h[:, f % 2, :], PS[:, 4 + f % 2, :], W_SCALE, silu[:, f % 2, :],
                                                       ALU.mult, ALU.mult).then_inc(h_done.sem, 1)
                        if f > 0:
                            low_part(u, f - 1)
                        if f == 1 and not last:
                            ln.dve_stats(dve, u + 1)
                        if f == 3 and not last:
                            ln.dve_normalise(dve, u + 1)
                    low_part(u, NF - 1)
                    dve.wait_ge(down_done.sem, down_done.at(u, NF))
                    x = X[:, bass.ds(u * UT, UT), :].rearrange("p a m -> p (a m)")
                    nc.vector.scalar_tensor_tensor(x, Y.rearrange("p a b -> p (a b)"), W_SCALE, x,
                                                   ALU.mult, ALU.add).then_inc(x_done.sem, 1)

                ln.dve_stats(dve, 0)
                ln.dve_normalise(dve, 0)
                with dve.Fori(0, NU - 1) as u:
                    turn(u, False)
                turn(NU - 1, True)

            @block.tensor
            def _(pe):
                open_signals(pe, sx.transposed, gate_ready, up_ready, down_done)
                pe.wait_ge(prep, 4)
                nc.tensor.transpose(PS[0:1, 7, 0:P], low_max[:], ident[:]).then_inc(low_t, 1)
                pe.wait_ge(low_done, 1)
                wide = pe.value_load(low_any[:].bitcast(I32))

                def turn(u, last, terms):
                    def gate_or_up(bank, hi, lo, f, done):
                        at = slice(f * P, (f + 1) * P)
                        parts = [p for k in range(KT) for p in sx.terms(hi[:, k, at], lo[:, k, at], k)[:terms]]
                        for n, (w, x) in enumerate(parts):
                            ins = nc.tensor.matmul(PS[:, bank, :], w, x, start=n == 0, stop=n == len(parts) - 1)
                        ins.then_inc(done.sem, 1)

                    def down(f):
                        pe.wait_ge(hi_done.sem, hi_done.at(u, f + 1))
                        pe.wait_ge(lo_done.sem, lo_done.at(u, f + 1))
                        parts = [(a, w) for w in ((down_hi,) if terms == 2 else (down_hi, down_lo)) for a in (h_hi, h_lo)]
                        for t in range(UT):
                            for n, (a, w) in enumerate(parts):
                                ins = nc.tensor.matmul(Y[:, t // 2, (t % 2) * M:(t % 2 + 1) * M],
                                                       a[:, f % NH, t * P:(t + 1) * P], w[:, f, :],
                                                       start=f == 0 and n == 0 and t % 2 == 0,
                                                       stop=f == NF - 1 and n == len(parts) - 1, skip_group_check=True)
                        ins.then_inc(down_done.sem, 1)

                    sx.pe_wait(pe, u, 0)
                    for f in range(NF):
                        pe.wait_ge(silu_done.sem, silu_done.at(u, f - 1))
                        gate_or_up(2 + f % 2, gate_hi, gate_lo, f, gate_ready)
                        pe.wait_ge(h_done.sem, h_done.at(u, f - 1))
                        gate_or_up(4 + f % 2, up_hi, up_lo, f, up_ready)
                        if f == 2:
                            pe.wait_ge(x_done.sem, x_done.at(u, 0))
                        if f >= 2:
                            down(f - 2)
                    if not last:
                        sx.pe(pe, u + 1, 0, 0)
                    down(NF - 2)
                    down(NF - 1)

                def units(terms):
                    with pe.Fori(0, NU - 1) as u:
                        turn(u, False, terms)
                    turn(NU - 1, True, terms)

                sx.pe(pe, 0, 0, 0)
                with pe.If(wide == 0):
                    units(2)
                with pe.If(wide != 0):
                    units(4)


def linear_attention_phase(nc, env, io):
    X, PS, ident, stage = env["X"], env["PS"], env["ident"], env["stage"]
    with ExitStack() as ctx:
        sb = lambda n, shape, dt=F32: ctx.enter_context(nc.sbuf_tensor(f"lin_{n}", shape, dt))
        sem = lambda n: ctx.enter_context(nc.semaphore(f"lin_{n}"))
        sig = lambda n, per: Signal(nc, ctx, f"lin_{n}", per)

        NHALF = T // UN
        w_hi, w_lo = sb("w_hi", [P, KT, LB_COLS], F32R), sb("w_lo", [P, KT, LB_COLS], F32R)
        w_o = stage[:, KT * LB_COLS:KT * LB_COLS + NP * M].rearrange("p (k m) -> p k m", k=NP)
        w_o = sb("w_o", [P, NP, M])
        bias = sb("bias", [P, NP])
        decay_in = sb("decay_in", [P, HB + NP])
        log_g = sb("log_g", [P, HB + NP])
        tmp_a, tmp_b = sb("tmp_a", [P, HB + NP]), sb("tmp_b", [P, HB + NP])
        dist = sb("dist", [P, 3, P])
        rev = sb("rev", [P, 1])
        D = sb("decay", [P, HB, P])
        Gq = sb("decay_q", [P, NP, P])
        Gk = sb("decay_k", [P, HB])
        Gc = sb("decay_c", [P, NP])

        ln = Layernorm(nc, ctx, "lin_ln", UT, X)
        sx = SplitTransposed(nc, ctx, "lin", NHALF, PS[:, 0:2, :], ident, ln)
        e = sb("e", [P, 2, UN])
        qT, kT, qsT, gate = (sb(n, [P, NP, UN]) for n in ("qT", "kT", "qsT", "gate"))
        v = sb("v", [P, UT, HB, VA])
        AD = sb("AD", [P, 2, 2, NP, P])
        ks = sb("ks", [P, 2, HB, DK])
        S = sb("state", [P, NP, 2 * VA])
        den, inv = sb("den", [P, 2, HG]), sb("inv", [P, 2, HG])
        y = sb("y", [P, 2, HD])
        yg = sb("yg", [P, NP, P])

        NC = TB
        RING = (4, 5, 2, 3)
        NITEM = 3 * NP + UT

        const_loaded = sem("const_loaded")
        prep, prep_act, zeroed = sem("prep"), sem("prep_act"), sem("zeroed")
        proj_ready = sig("proj_ready", NHALF * NITEM)
        relu_done, exp_done, phi_done = (sig(n, NHALF * 2 * NP) for n in ("relu_done", "exp_done", "phi_done"))
        qs_done = sig("qs_done", NHALF * NP)
        gate_done, v_done = sig("gate_done", NHALF * NP), sig("v_done", NC)
        kt_ready, ks_done = sig("kt_ready", NC), sig("ks_done", NC)
        a_ready, ad_done = sig("a_ready", 2 * NC), sig("ad_done", 2 * NC)
        o_ready, den_done, inv_done, y_done = (sig(n, 2 * NC) for n in ("o_ready", "den_done", "inv_done", "y_done"))
        st_ready, s_done = sig("st_ready", 2 * NC), sig("s_done", 2 * NC)
        yt_ready, yg_done = sig("yt_ready", NC), sig("yg_done", NC)
        out_ready, x_done = sig("out_ready", NC), sig("x_done", NC)

        with nc.Block() as block:

            @block.sync
            def _(sp):
                sp.dma_start(bias[:], io["b_g"]).then_inc(const_loaded, 16)
                sp.dma_start(decay_in[:], io["decay"]).then_inc(const_loaded, 16)
                sp.dma_start(dist[:], io["dist"]).then_inc(const_loaded, 16)
                sp.dma_start(rev[:], io["rev"]).then_inc(const_loaded, 16)
                sp.wait_ge(prep, 4)
                load_ff_weights(sp, env, io)

            @block.gpsimd
            def _(pool):
                open_signals(pool, qs_done)
                nc.gpsimd.memset(S[:], 0.0).then_inc(zeroed, 1)
                nc.gpsimd.memset(v[:], 1.0).then_inc(zeroed, 1)
                ln.pool_open(pool)

                def turn(b, last):
                    for half in range(NHALF):
                        for j in range(NP):
                            pool.wait_ge(phi_done.sem, phi_done.at(b, 2 * NP * half + 2 * j + 1))
                            nc.gpsimd.tensor_tensor(qsT[:, j, :].rearrange("p (c t) -> p c t", t=P),
                                                    qT[:, j, :].rearrange("p (c t) -> p c t", t=P),
                                                    Gq[:, j, :].unsqueeze(1).to_broadcast([P, UT, P]),
                                                    ALU.mult).then_inc(qs_done.sem, 1)
                        if not (last and half == NHALF - 1):
                            ln.pool_rstd(pool, b * NHALF + half + 1)

                ln.pool_rstd(pool, 0)
                pool.wait_ge(prep_act, 4)
                with pool.Fori(0, NB - 1) as b:
                    turn(b, False)
                turn(NB - 1, True)

            @block.scalar
            def _(act):
                open_signals(act, sx.hi_done, relu_done, exp_done, gate_done, v_done)
                act.wait_ge(prep, 5)
                nc.scalar.activation(tmp_b[:], tmp_a[:], ACT.Exp, scale=-1.0).then_inc(prep_act, 1)
                act.wait_ge(prep_act, 1)
                nc.scalar.activation(tmp_a[:], tmp_b[:], ACT.Ln, bias=1.0).then_inc(prep_act, 1)
                act.wait_ge(prep, 8)
                for hd in range(HB):
                    nc.scalar.activation(D[:, hd, :], dist[:, 0, :], ACT.Exp, scale=log_g[:, hd:hd + 1])
                for j in range(NP):
                    nc.scalar.activation(Gq[:, j, :], dist[:, 2, :], ACT.Exp, scale=log_g[:, HB + j:HB + j + 1])
                nc.scalar.activation(Gc[:], log_g[:, HB:], ACT.Exp, scale=float(P)).then_inc(prep_act, 1)
                nc.scalar.activation(Gk[:], tmp_b[:, 0:HB], ACT.Exp).then_inc(prep_act, 1)
                nc.scalar.mul(bias[:], bias[:], 0.5).then_inc(prep_act, 1)
                act.wait_ge(prep_act, 5)
                act.wait_ge(zeroed, 2)

                def turn(b):
                    for half in range(NHALF):
                        sx.act(act, b, half)
                        for it in range(NITEM):
                            m = NITEM * half + it
                            src = PS[:, RING[m % 4], :]
                            act.wait_ge(proj_ready.sem, proj_ready.at(b, m + 1))
                            if it < 2 * NP:
                                n = 2 * NP * half + it
                                act.wait_ge(phi_done.sem, phi_done.at(b, n - 1))
                                nc.scalar.activation(e[:, it % 2, :], src, ACT.Relu, scale=-1.0).then_inc(relu_done.sem, 1)
                                act.wait_ge(relu_done.sem, relu_done.at(b, n + 1))
                                nc.scalar.activation(e[:, it % 2, :], e[:, it % 2, :], ACT.Exp,
                                                     scale=-1.0).then_inc(exp_done.sem, 1)
                            elif it < 3 * NP:
                                j = it - 2 * NP
                                nc.scalar.activation(gate[:, j, :], src, ACT.Tanh, bias=bias[:, j:j + 1],
                                                     scale=0.5).then_inc(gate_done.sem, 1)
                            else:
                                t = it - 3 * NP
                                nc.scalar.activation(v[:, t, :, 0:DK], src.rearrange("p (h d) -> p h d", d=DK),
                                                     ACT.Copy).then_inc(v_done.sem, 1)

                with act.Fori(0, NB) as b:
                    turn(b)

            @block.vector
            def _(dve):
                open_signals(dve, sx.lo_done, phi_done, ks_done, ad_done, den_done, inv_done, y_done, s_done, yg_done, x_done)
                ln.dve_open(dve)
                dve.wait_ge(env["lin_loaded"], 32)
                raw = stage[:, 0:KT * LB_COLS].rearrange("p (k n) -> p k n", k=KT)
                nc.vector.tensor_copy(w_hi[:], raw).then_inc(prep, 1)
                nc.vector.tensor_copy(w_o[:], stage[:, KT * LB_COLS:KT * LB_COLS + NP * M].rearrange(
                    "p (k m) -> p k m", k=NP)).then_inc(prep, 1)
                dve.wait_ge(prep, 2)
                nc.vector.tensor_tensor(w_lo[:], raw, w_hi[:].bitcast(F32), ALU.subtract).then_inc(prep, 1)
                dve.wait_ge(prep, 3)
                dve.wait_ge(const_loaded, 64)
                nc.vector.tensor_scalar(log_g[:], decay_in[:], 0.0, None, ALU.min).then_inc(prep, 1)
                nc.vector.scalar_tensor_tensor(tmp_a[:], decay_in[:], -1.0, decay_in[:], ALU.mult, ALU.max).then_inc(prep, 1)
                dve.wait_ge(prep_act, 2)
                nc.vector.tensor_tensor(log_g[:], log_g[:], tmp_a[:], ALU.subtract).then_inc(prep, 1)
                dve.wait_ge(prep, 6)
                nc.vector.tensor_scalar(log_g[:], log_g[:], -200.0, None, ALU.max).then_inc(prep, 1)
                dve.wait_ge(prep, 7)
                nc.vector.tensor_scalar(tmp_b[:], log_g[:], rev[:], None, ALU.mult).then_inc(prep, 1)
                dve.wait_ge(prep_act, 4)
                nc.vector.tensor_tensor(D[:], D[:], dist[:, 1, :].unsqueeze(1).to_broadcast([P, HB, P]),
                                        ALU.mult).then_inc(prep, 1)
                dve.wait_ge(prep, 9)
                dve.wait_ge(zeroed, 2)

                def phi_item(b, half, it):
                    n = 2 * NP * half + it
                    m = NITEM * half + it
                    dve.wait_ge(exp_done.sem, exp_done.at(b, n + 1))
                    dst = (qT, kT)[it % 2]
                    nc.vector.scalar_tensor_tensor(dst[:, it // 2, :], PS[:, RING[m % 4], :], 1.0, e[:, it % 2, :],
                                                   ALU.add, ALU.max).then_inc(phi_done.sem, 1)

                def scaled_keys(b, c):
                    dve.wait_ge(kt_ready.sem, kt_ready.at(b, c + 1))
                    nc.vector.tensor_tensor(ks[:, c % 2], PS[:, 4, :].rearrange("p (h d) -> p h d", d=DK),
                                            Gk[:].unsqueeze(2).to_broadcast([P, HB, DK]), ALU.mult).then_inc(ks_done.sem, 1)

                def decayed_scores(b, c, r):
                    dve.wait_ge(a_ready.sem, a_ready.at(b, 2 * c + r + 1))
                    nc.vector.tensor_tensor(AD[:, c % 2, r], PS[:, r, :].rearrange("p (j t) -> p j t", t=P),
                                            D[:].rearrange("p (j r) t -> p r j t", r=2)[:, r],
                                            ALU.mult).then_inc(ad_done.sem, 1)

                def quotient(b, c, g):
                    n = 2 * c + g
                    O = PS[:, 2 + g, 0:HG * VA].rearrange("p (h a) -> p h a", a=VA)
                    dve.wait_ge(o_ready.sem, o_ready.at(b, n + 1))
                    nc.vector.tensor_scalar(den[:, g, :], O[:, :, DK], DEN_EPS, 2.0, ALU.add, ALU.mult).then_inc(den_done.sem, 1)
                    dve.wait_ge(den_done.sem, den_done.at(b, n + 1))
                    nc.vector.reciprocal(inv[:, g, :], den[:, g, :]).then_inc(inv_done.sem, 1)
                    dve.wait_ge(inv_done.sem, inv_done.at(b, n + 1))
                    nc.vector.tensor_tensor(y[:, c % 2, HG * DK * g:HG * DK * (g + 1)].rearrange("p (h d) -> p h d", d=DK),
                                            O[:, :, 0:DK], inv[:, g, :].unsqueeze(2).to_broadcast([P, HG, DK]),
                                            ALU.mult).then_inc(y_done.sem, 1)

                def update_state(b, c, g):
                    n = 2 * c + g
                    dve.wait_ge(st_ready.sem, st_ready.at(b, n + 1))
                    for jj in range(2):
                        j = 2 * g + jj
                        for r in range(2):
                            rows, cols = slice(r * DK, (r + 1) * DK), slice(r * VA, (r + 1) * VA)
                            new = PS[rows, 5, jj * 2 * VA + r * VA:jj * 2 * VA + (r + 1) * VA]
                            if c == 0:
                                last = nc.vector.tensor_copy(S[rows, j, cols], new)
                            else:
                                last = nc.vector.scalar_tensor_tensor(S[rows, j, cols], S[rows, j, cols], Gc[rows, j:j + 1],
                                                                      new, ALU.mult, ALU.add)
                    last.then_inc(s_done.sem, 1)

                def gated(b, half, c):
                    ch = NC // NHALF * half + c
                    dve.wait_ge(yt_ready.sem, yt_ready.at(b, ch + 1))
                    dve.wait_ge(gate_done.sem, gate_done.at(b, NP * (half + 1)))
                    nc.vector.scalar_tensor_tensor(yg[:], gate[:, :, c * P:(c + 1) * P], 1.0,
                                                   PS[:, 6, :].rearrange("p (j t) -> p j t", t=P),
                                                   ALU.add, ALU.mult).then_inc(yg_done.sem, 1)

                def residual(b, ch):
                    dve.wait_ge(out_ready.sem, out_ready.at(b, ch + 1))
                    x = X[:, bass.ds(b * TB + ch, 1), :].rearrange("p a m -> p (a m)")
                    nc.vector.tensor_tensor(x, PS[:, 7, 0:M], x, ALU.add).then_inc(x_done.sem, 1)

                def turn(b, last):
                    for half in range(NHALF):
                        sx.dve(dve, b, half)
                        for it in range(2 * NP):
                            phi_item(b, half, it)
                        c0 = UT * half
                        scaled_keys(b, c0)
                        decayed_scores(b, c0, 0)
                        decayed_scores(b, c0, 1)
                        for c in range(UT):
                            more = c + 1 < UT
                            if more:
                                scaled_keys(b, c0 + c + 1)
                            for g in range(2):
                                quotient(b, c0 + c, g)
                                update_state(b, c0 + c, g)
                                if more:
                                    decayed_scores(b, c0 + c + 1, g)
                            if c > 0:
                                gated(b, half, c - 1)
                                residual(b, c0 + c - 1)
                            if not (last and half == NHALF - 1):
                                if c == 0:
                                    ln.dve_stats(dve, b * NHALF + half + 1)
                                if c == 1:
                                    ln.dve_normalise(dve, b * NHALF + half + 1)
                        gated(b, half, UT - 1)
                        residual(b, c0 + UT - 1)

                ln.dve_stats(dve, 0)
                ln.dve_normalise(dve, 0)
                with dve.Fori(0, NB - 1) as b:
                    turn(b, False)
                turn(NB - 1, True)

            @block.tensor
            def _(pe):
                open_signals(pe, sx.transposed, proj_ready, kt_ready, a_ready, o_ready, st_ready, yt_ready, out_ready)
                pe.wait_ge(prep, 9)

                def projections(b, half):
                    c0 = UT * half
                    sx.pe_wait(pe, b, half)
                    for it in range(NITEM):
                        m = NITEM * half + it
                        n = 2 * NP * half + it
                        if it == 0:
                            pe.wait_ge(ks_done.sem, ks_done.at(b, c0))
                            pe.wait_ge(s_done.sem, s_done.at(b, 2 * c0))
                            pe.wait_ge(y_done.sem, y_done.at(b, 2 * c0))
                        elif 4 <= it < 4 + 2 * NP:
                            pe.wait_ge(phi_done.sem, phi_done.at(b, n - 3))
                        elif it >= 4 + 2 * NP:
                            pe.wait_ge(gate_done.sem, gate_done.at(b, NP * half + it - 4 - 2 * NP + 1))
                        bank = PS[:, RING[m % 4], :]
                        if it < 2 * NP:
                            col = (it % 2) * HD + (it // 2) * P
                            ins = project(nc, bank, sx, w_hi, w_lo, slice(col, col + P))
                        elif it < 3 * NP:
                            col = 2 * HD + (it - 2 * NP) * P
                            ins = project(nc, bank, sx, w_hi, w_lo, slice(col, col + P))
                        else:
                            ins = project_tokens(nc, bank, sx, w_hi, w_lo, slice(3 * HD, 4 * HD), it - 3 * NP)
                        ins.then_inc(proj_ready.sem, 1)

                def keys(b, half, c):
                    ch = UT * half + c
                    pe.wait_ge(ks_done.sem, ks_done.at(b, ch))
                    for j in range(NP):
                        last = nc.tensor.transpose(PS[:, 4, j * P:(j + 1) * P], kT[:, j, c * P:(c + 1) * P], ident[:])
                    last.then_inc(kt_ready.sem, 1)

                def scores(b, half, c):
                    n = 2 * (UT * half + c)
                    at = slice(c * P, (c + 1) * P)
                    pe.wait_ge(ad_done.sem, ad_done.at(b, n))
                    for j in range(NP):
                        for r in range(2):
                            rows = slice(r * DK, (r + 1) * DK)
                            last = nc.tensor.matmul(PS[:, r, j * P:(j + 1) * P], kT[rows, j, at], qT[rows, j, at],
                                                    start=True, stop=True)
                            if j == NP - 1:
                                last.then_inc(a_ready.sem, 1)

                def outputs(b, half, c, g):
                    ch = UT * half + c
                    n = 2 * ch + g
                    pe.wait_ge(ad_done.sem, ad_done.at(b, 2 * ch + 2))
                    pe.wait_ge(y_done.sem, y_done.at(b, n - 1))
                    pe.wait_ge(s_done.sem, s_done.at(b, n - 1))
                    bank = PS[:, 2 + g, 0:HG * VA]
                    for hh in range(HG):
                        last = nc.tensor.matmul(bank[:, hh * VA:(hh + 1) * VA], AD[:, ch % 2, hh % 2, 2 * g + hh // 2, :], v[:, c, HG * g + hh, :],
                                                start=hh == 0, stop=ch == 0, skip_group_check=True)
                    if ch > 0:
                        for jj in range(2):
                            j = 2 * g + jj
                            last = nc.tensor.matmul(bank[:, jj * 2 * VA:(jj + 1) * 2 * VA], qsT[:, j, c * P:(c + 1) * P],
                                                    S[:, j, :], start=False, stop=True, skip_group_check=True)
                    last.then_inc(o_ready.sem, 1)

                def state(b, half, c, g):
                    ch = UT * half + c
                    n = 2 * ch + g
                    if g == 0:
                        pe.wait_ge(ks_done.sem, ks_done.at(b, ch + 1))
                    pe.wait_ge(s_done.sem, s_done.at(b, n))
                    for jj in range(2):
                        j = 2 * g + jj
                        last = nc.tensor.matmul(PS[:, 5, jj * 2 * VA:(jj + 1) * 2 * VA],
                                                ks[:, ch % 2, 2 * j:2 * j + 2, :].rearrange("p h d -> p (h d)"),
                                                v[:, c, 2 * j:2 * j + 2, :].rearrange("p h a -> p (h a)"),
                                                start=True, stop=True)
                    last.then_inc(st_ready.sem, 1)

                def out_projection(b, half, c):
                    ch = UT * half + c
                    pe.wait_ge(y_done.sem, y_done.at(b, 2 * ch + 2))
                    pe.wait_ge(yg_done.sem, yg_done.at(b, ch))
                    for j in range(NP):
                        last = nc.tensor.transpose(PS[:, 6, j * P:(j + 1) * P], y[:, ch % 2, j * P:(j + 1) * P], ident[:])
                    last.then_inc(yt_ready.sem, 1)
                    pe.wait_ge(yg_done.sem, yg_done.at(b, ch + 1))
                    pe.wait_ge(x_done.sem, x_done.at(b, ch))
                    for j in range(NP):
                        last = nc.tensor.matmul(PS[:, 7, 0:M], yg[:, j, :], w_o[:, j, :], start=j == 0, stop=j == NP - 1)
                    last.then_inc(out_ready.sem, 1)

                def turn(b, last):
                    for half in range(NHALF):
                        c0 = UT * half
                        projections(b, half)
                        pe.wait_ge(phi_done.sem, phi_done.at(b, 2 * NP * (half + 1)))
                        pe.wait_ge(v_done.sem, v_done.at(b, c0 + UT))
                        pe.wait_ge(qs_done.sem, qs_done.at(b, NP * (half + 1)))
                        keys(b, half, 0)
                        scores(b, half, 0)
                        for c in range(UT):
                            more = c + 1 < UT
                            if more:
                                keys(b, half, c + 1)
                            for g in range(2):
                                outputs(b, half, c, g)
                                state(b, half, c, g)
                                if more and g == 0:
                                    scores(b, half, c + 1)
                            if c > 0:
                                out_projection(b, half, c - 1)
                        if half + 1 < NHALF:
                            sx.pe(pe, b, half + 1, 0)
                        elif not last:
                            sx.pe(pe, b + 1, 0, 0)
                        out_projection(b, half, UT - 1)

                sx.pe(pe, 0, 0, 0)
                with pe.Fori(0, NB - 1) as b:
                    turn(b, False)
                turn(NB - 1, True)


def build(nc, io, phases=4):
    with ExitStack() as ctx:
        sb = lambda n, shape, dt=F32: ctx.enter_context(nc.sbuf_tensor(n, shape, dt))
        env = {
            "X": sb("X", [P, NT, M]),
            "ident": sb("ident", [P, P]),
            "stage": sb("stage", [P, KT * LB_COLS + NP * M]),
            "PS": ctx.enter_context(nc.psum_tensor("PS", [P, 8, UN], F32)),
            "ff_loaded": ctx.enter_context(nc.semaphore("ff_loaded")),
            "lin_loaded": ctx.enter_context(nc.semaphore("lin_loaded")),
        }
        env["stage"] = env["stage"][:, :]
        attention_phase(nc, env, io)
        if phases >= 2:
            feed_forward_phase(nc, env, io, "ff1", 1, phases == 2)
        if phases >= 3:
            linear_attention_phase(nc, env, io)
        if phases >= 4:
            feed_forward_phase(nc, env, io, "ff2", 2, True)
        if phases in (1, 3):
            with nc.Block() as block, nc.semaphore("dbg") as dbg:
                @block.sync
                def _(sp):
                    sp.dma_start(io["out"].rearrange("b (n p) m -> p (b n) m", p=P), env["X"][:]).then_inc(dbg, 16)
                    sp.wait_ge(dbg, 16)


PHASES = 4


def kernel(L0_attn_a_x, L0_attn_a_wq, L0_attn_a_wk, L0_attn_a_wv, L0_attn_a_wo, L0_attn_b_W_Q, L0_attn_b_W_K,
           L0_attn_b_W_V, L0_attn_b_W_g_w, L0_attn_b_W_g_b, L0_attn_b_W_O, L0_attn_b_decay_log, L0_ffn_w_gate,
           L0_ffn_w_up, L0_ffn_w_down):
    import concourse.bacc as bacc
    from concourse.bass_utils import run_bass_kernel_spmd as run

    a = lambda v: np.ascontiguousarray(np.asarray(v))

    def heads(w):
        w0, w1 = a(w)[:, 0, :], a(w)[:, 1, :]
        swap = lambda h: [h[:, HALF:ROT], h[:, 0:HALF]]
        return [w0, w1[:, ROT:], w1[:, :ROT]] + swap(w0) + swap(w1)

    w_qkv = np.concatenate(heads(L0_attn_a_wq) + heads(L0_attn_a_wk) + [a(L0_attn_a_wv).reshape(M, HA * DA)], axis=1)

    angle = np.power(np.float32(10000.0), -np.arange(HALF, dtype=np.float32) / np.float32(HALF)).astype(np.float32)
    rad = (angle[:, None] * np.arange(T, dtype=np.float32)[None, :]).astype(np.float32)
    c, s, one = np.cos(rad).astype(np.float32), np.sin(rad).astype(np.float32), np.ones((ROT, T), np.float32)
    cos = np.stack([np.concatenate([c, c, one]), np.concatenate([one, c, c])], axis=1)
    sin = np.concatenate([-s, s, -s, s])
    i = np.arange(P)
    causal = np.where(i[None, :] > i[:, None], np.float32(NEG), np.float32(0)).astype(np.float32)
    ahead = (i[None, :] - i[:, None]).astype(np.float32)
    dist = np.stack([np.maximum(ahead, 0), (ahead >= 0).astype(np.float32),
                     np.broadcast_to((i + 1).astype(np.float32), (P, P))], axis=1)

    d = a(L0_attn_b_decay_log)
    decay = np.concatenate([np.broadcast_to(d, (P, HB)), np.repeat(d.reshape(NP, 2).T, DK, axis=0)], axis=1)

    arrays = {
        "x": a(L0_attn_a_x), "w_qkv": a(w_qkv), "wo_a": a(L0_attn_a_wo).reshape(HA * DA, M),
        "ident": np.eye(P, dtype=np.float32), "causal": causal, "cos": a(cos), "sin": a(sin),
        "w_gate": a(a(L0_ffn_w_gate).T), "w_up": a(a(L0_ffn_w_up).T), "w_down": a(a(L0_ffn_w_down).T),
        "w_lin": a(np.concatenate([a(L0_attn_b_W_Q).T, a(L0_attn_b_W_K).T, a(L0_attn_b_W_g_w).T, a(L0_attn_b_W_V).T], axis=1)),
        "w_o": a(a(L0_attn_b_W_O).T), "b_g": a(a(L0_attn_b_W_g_b).reshape(NP, P).T), "decay": a(decay),
        "dist": a(dist), "rev": a((P - 1 - i).astype(np.float32)[:, None]),
    }
    nc = bacc.Bacc("TRN2", target_bir_lowering=False, num_devices=1)
    io = {}
    for name, v in arrays.items():
        io[name] = nc.dram_tensor(f"in_{name}", v.shape, mybir.dt.from_np(v.dtype), kind="ExternalInput").ap()
    io["out"] = nc.dram_tensor("out_x", (NB, T, M), F32, kind="ExternalOutput").ap()
    build(nc, io, PHASES)
    r = run(nc, [{f"in_{k}": v for k, v in arrays.items()}], core_ids=[0])
    return r.results[0]["out_x"]
```

```python
import concourse.bass as bass
from concourse import mybir
from contextlib import ExitStack
import numpy as np

F32 = mybir.dt.float32
F32R = mybir.dt.float32r
BF16 = mybir.dt.bfloat16
I32 = mybir.dt.int32
ALU = mybir.AluOpType
ACT = mybir.ActivationFunctionType
AX = mybir.AxisListType

P = 128
NB, T, M = 8, 1024, 256
KT = M // P
NT = NB * T // P
TB = T // P
UT = 4
UN = UT * P
NU = NT // UT
LN_EPS = 1e-5

HA, DA = 2, 128
ROT = DA // 2
HALF = ROT // 2
NQK = 3 * HA
WQK = NQK * P
QK_SCALE = 1.0 / DA
NEG = -1e30

FF = 768
NF = FF // P
W_SCALE = 1.0 / 127.0

HB, DK = 8, 64
HD = HB * DK
NP = HD // P
HG = 4
VA = DK + 1
DEN_EPS = 1e-6

CREDIT = 4


class Signal:

    def __init__(self, nc, ctx, name, per):
        self.sem = ctx.enter_context(nc.semaphore(name))
        self.per = per

    def at(self, turn, k):
        return turn * self.per + (CREDIT + k)


def open_signals(eng, *signals):
    for s in signals:
        eng.sem_inc(s.sem, CREDIT)


def wait_alone(eng, sem, value, passed):
    eng.wait_ge(sem, value)
    eng.sem_inc(passed, 1)


class Layernorm:

    def __init__(self, nc, ctx, name, tiles, X):
        sb = lambda n, shape: ctx.enter_context(nc.sbuf_tensor(f"{name}_{n}", shape, F32))
        self.nc, self.X, self.tiles = nc, X, tiles
        self.stats = sb("stats", [P, tiles, 6])
        self.mean_var = sb("mean_var", [P, tiles, 2])
        self.var_eps = sb("var_eps", [P, tiles])
        self.rstd = sb("rstd", [P, tiles])
        self.minus_half = sb("minus_half", [P, tiles])
        self.out = sb("xn", [P, tiles, M])
        self.stats_done = Signal(nc, ctx, f"{name}_stats_done", 1)
        self.mv_done = Signal(nc, ctx, f"{name}_mv_done", 1)
        self.ve_done = Signal(nc, ctx, f"{name}_ve_done", 1)
        self.rstd_done = Signal(nc, ctx, f"{name}_rstd_done", 1)
        self.dve_passed = ctx.enter_context(nc.semaphore(f"{name}_dve_passed"))
        self.pool_passed = ctx.enter_context(nc.semaphore(f"{name}_pool_passed"))
        self.consts = ctx.enter_context(nc.semaphore(f"{name}_consts"))
        self.ready = Signal(nc, ctx, f"{name}_ready", tiles // UT)

    def dve_open(self, dve):
        open_signals(dve, self.stats_done, self.mv_done, self.ready)

    def dve_tile_stats(self, dve, turn, some):
        for t in some:
            ins = self.nc.vector.bn_stats(self.stats[:, t, :], self.X[:, bass.ds(turn * self.tiles + t, 1), :])
            if t == self.tiles - 1:
                ins.then_inc(self.stats_done.sem, 1)

    def dve_aggregate(self, dve, turn):
        nc = self.nc
        wait_alone(dve, self.stats_done.sem, self.stats_done.at(turn, 1), self.dve_passed)
        for t in range(self.tiles):
            last = nc.vector.bn_aggr(self.mean_var[:, t, :], self.stats[:, t, :])
        last.then_inc(self.mv_done.sem, 1)

    def dve_stats(self, dve, turn):
        self.dve_tile_stats(dve, turn, range(self.tiles))
        self.dve_aggregate(dve, turn)

    def dve_normalise(self, dve, turn):
        nc = self.nc
        dve.wait_ge(self.rstd_done.sem, self.rstd_done.at(turn, 1))
        for t in range(self.tiles):
            last = nc.vector.tensor_scalar(self.out[:, t, :], self.X[:, bass.ds(turn * self.tiles + t, 1), :],
                                           self.mean_var[:, t, 0:1], self.rstd[:, t:t + 1],
                                           ALU.subtract, ALU.mult)
            if t % UT == UT - 1:
                last.then_inc(self.ready.sem, 1)

    def pool_open(self, pool):
        open_signals(pool, self.ve_done, self.rstd_done)
        self.nc.gpsimd.memset(self.minus_half[:], -0.5).then_inc(self.consts, 1)
        pool.wait_ge(self.consts, 1)

    def pool_rstd(self, pool, turn):
        nc = self.nc
        wait_alone(pool, self.mv_done.sem, self.mv_done.at(turn, 1), self.pool_passed)
        nc.gpsimd.tensor_scalar(self.var_eps[:], self.mean_var[:, :, 1], LN_EPS, None,
                                ALU.add).then_inc(self.ve_done.sem, 1)
        pool.wait_ge(self.ve_done.sem, self.ve_done.at(turn, 1))
        nc.gpsimd.tensor_tensor(self.rstd[:], self.var_eps[:], self.minus_half[:],
                                ALU.pow).then_inc(self.rstd_done.sem, 1)


class SplitTransposed:

    def __init__(self, nc, ctx, name, psum, ident, ln, unit=0):
        sb = lambda n: ctx.enter_context(nc.sbuf_tensor(f"{name}_{n}", [P, KT, UN], F32R))
        self.nc, self.psum, self.ident, self.ln, self.unit = nc, psum, ident, ln, unit
        self.hi, self.lo = sb("xh"), sb("xl")
        self.transposed = Signal(nc, ctx, f"{name}_transposed", 1)
        self.hi_done = Signal(nc, ctx, f"{name}_hi_done", 1)
        self.lo_done = Signal(nc, ctx, f"{name}_lo_done", 1)

    def pe_open(self, pe):
        open_signals(pe, self.transposed)

    def act_open(self, act):
        open_signals(act, self.hi_done)

    def dve_open(self, dve):
        open_signals(dve, self.lo_done)

    def pe(self, pe, turn, ln_turn):
        ln = self.ln
        pe.wait_ge(ln.ready.sem, ln.ready.at(ln_turn, self.unit + 1))
        for t in range(UT):
            for k in range(KT):
                last = self.nc.tensor.transpose(self.psum[:, k, t * P:(t + 1) * P],
                                                ln.out[:, self.unit * UT + t, k * P:(k + 1) * P], self.ident[:])
        last.then_inc(self.transposed.sem, 1)

    def act(self, act, turn):
        act.wait_ge(self.transposed.sem, self.transposed.at(turn, 1))
        self.nc.scalar.activation(self.hi[:], self.psum, ACT.Copy).then_inc(self.hi_done.sem, 1)

    def dve(self, dve, turn):
        dve.wait_ge(self.hi_done.sem, self.hi_done.at(turn, 1))
        self.nc.vector.tensor_tensor(self.lo[:], self.psum, self.hi[:].bitcast(F32),
                                     ALU.subtract).then_inc(self.lo_done.sem, 1)

    def pe_wait(self, pe, turn):
        pe.wait_ge(self.hi_done.sem, self.hi_done.at(turn, 1))
        pe.wait_ge(self.lo_done.sem, self.lo_done.at(turn, 1))

    def terms(self, w_hi, w_lo, k):
        return [(w_hi, self.hi[:, k, :]), (w_hi, self.lo[:, k, :]), (w_lo, self.hi[:, k, :]),
                (w_lo, self.lo[:, k, :])]


def project(nc, out, sx, w_hi, w_lo, cols):
    terms = [t for k in range(KT) for t in sx.terms(w_hi[:, k, cols], w_lo[:, k, cols], k)[:PROJ_TERMS]]
    for n, (w, x) in enumerate(terms):
        last = nc.tensor.matmul(out, w, x, start=n == 0, stop=n == len(terms) - 1)
    return last


def project_tokens(nc, out, sx, w_hi, w_lo, cols, tile):
    at = slice(tile * P, (tile + 1) * P)
    terms = [t for k in range(KT) for t in sx.terms(w_hi[:, k, cols], w_lo[:, k, cols], k)[:PROJ_TERMS]]
    for n, (w, x) in enumerate(terms):
        last = nc.tensor.matmul(out, x[:, at], w, start=n == 0, stop=n == len(terms) - 1)
    return last


PROJ_TERMS = 3


def attention_phase(nc, env, io):
    X, PS, ident = env["X"], env["PS"], env["ident"]
    with ExitStack() as ctx:
        sb = lambda n, shape, dt=F32: ctx.enter_context(nc.sbuf_tensor(n, shape, dt))
        sem = lambda n: ctx.enter_context(nc.semaphore(n))
        sig = lambda n, per: Signal(nc, ctx, n, per)

        wqkv_hi = sb("wqkv_hi", [P, KT, WQK + HA * DA], F32R)
        wqkv_lo = sb("wqkv_lo", [P, KT, WQK + HA * DA], F32R)
        wo = sb("wo_a", [P, HA, M])
        cos = sb("cos", [P, HA, T])
        sin = sb("sin", [P, T])
        mask_f = sb("mask_f", [P, P])
        mask_b = sb("mask_b", [P, P], BF16)
        ident_b = sb("ident_b", [P, P], BF16)
        NHALF = T // UN
        ln = Layernorm(nc, ctx, "a_ln", TB, X)
        sx = [SplitTransposed(nc, ctx, f"a{half}", PS[:, 2 * half:2 * half + 2, :], ident, ln, half)
              for half in range(NHALF)]
        qk = sb("qk", [P, 2, HA, T])
        wqkv_raw = qk[:].rearrange("p s h t -> p (s h t)")[:, 0:KT * (WQK + HA * DA)].rearrange("p (k n) -> p k n", k=KT)
        swapped = sb("swapped", [P, 2, UN])
        V = sb("v_a", [P, TB, HA * DA])

        steps = [(i, h) for i in range(TB) for h in range(HA)]
        NS = len(steps)
        prob = sb("prob", [P, 2, T])
        probT = sb("probT", [P, 2, TB, P])
        NO = 2
        oT = sb("oT", [P, NO, P])
        neg_max = sb("neg_max", [P, NS])
        row_sum = sb("row_sum", [P, NS])
        row_inv = sb("row_inv", [P, NS])

        groups = [(i + UT) // UT for i, _ in steps]
        first_group = [sum(groups[:n]) for n in range(NS + 1)]
        NG = first_group[NS]
        PROJ_RING = (4, 5, 0, 1)
        NPROJ = NHALF * NQK

        const_loaded, w_loaded, x_loaded = sem("a_const_loaded"), sem("a_w_loaded"), sem("x_loaded")
        prep_hi, prep_done = sem("a_prep_hi"), sem("a_prep_done")
        proj_ready, proj_used = sig("a_proj_ready", NPROJ), sig("a_proj_used", NPROJ)
        rotated = sig("a_rotated", 2 * NHALF)
        v_ready, v_done = sig("a_v_ready", TB), sig("a_v_done", TB)
        s_ready, max_done, p_done = sig("s_ready", NS), sig("max_done", NS), sig("p_done", NS)
        inv_done = sig("inv_done", NS)
        pt_ready, pt_done = sig("pt_ready", NG), sig("pt_done", NG)
        o_ready, o_done = sig("a_o_ready", NS), sig("a_o_done", NS)
        y_ready, y_done = sig("a_y_ready", NS), sig("a_y_done", NS)

        x_v = io["x"].rearrange("b (n p) m -> p (b n) m", p=P)
        N_CONST = 4
        passed = sem("sp_passed")

        def score_rows(n):
            return PS[:, 2 * (n % 2):2 * (n % 2) + 2, :].rearrange("p a b -> p (a b)")[:, 0:(steps[n][0] + 1) * P]

        O, Y = PS[:, 6, 0:P], PS[:, 7, 0:M]

        with nc.Block() as block:

            @block.sync
            def _(sp):
                with sp.Fori(0, NB) as b:
                    at = bass.ds(b * TB, TB)
                    sp.dma_start(X[:, at, :], x_v[:, at, :]).then_inc(x_loaded, 16)
                    wait_alone(sp, x_loaded, (b + 1) * 16, passed)
                load_ff_weights(sp, env, io)

            @block.gpsimd
            def _(pool):
                open_signals(pool, rotated)
                ln.pool_open(pool)

                def turn(b, last):
                    for half in range(NHALF):
                        at = slice(half * UN, (half + 1) * UN)
                        for s in range(2):
                            pool.wait_ge(proj_used.sem, proj_used.at(b, NQK * half + 3 * (s + 1)))
                            for h in range(HA):
                                rows = slice(h * ROT, (h + 1) * ROT)
                                done = nc.gpsimd.tensor_tensor(qk[rows, s, h, at], qk[rows, s, h, at],
                                                               swapped[rows, s, :], ALU.add)
                            done.then_inc(rotated.sem, 1)
                    if not last:
                        ln.pool_rstd(pool, b + 1)

                ln.pool_rstd(pool, 0)
                with pool.Fori(0, NB - 1) as b:
                    turn(b, False)
                turn(NB - 1, True)

            @block.scalar
            def _(act):
                for s in sx:
                    s.act_open(act)
                open_signals(act, v_done, p_done, pt_done, o_done)
                act.dma_start(wqkv_raw, io["w_qkv"].rearrange("(k p) n -> p k n", p=P)).then_inc(w_loaded, 16)
                act.dma_start(ident[:], io["ident"]).then_inc(const_loaded, 16)
                act.dma_start(mask_f[:], io["causal"]).then_inc(const_loaded, 16)
                act.dma_start(cos[:], io["cos"]).then_inc(const_loaded, 16)
                act.dma_start(sin[:], io["sin"]).then_inc(const_loaded, 16)
                act.dma_start(wo[:], io["wo_a"].rearrange("(h p) n -> p h n", p=P)).then_inc(w_loaded, 16)
                nq = WQK // 2
                act.wait_ge(w_loaded, 32)
                nc.scalar.activation(wqkv_hi[:, :, 0:nq], wqkv_raw[:, :, 0:nq], ACT.Copy, scale=QK_SCALE).then_inc(prep_hi, 1)
                nc.scalar.activation(wqkv_hi[:, :, nq:], wqkv_raw[:, :, nq:], ACT.Copy).then_inc(prep_hi, 1)

                def exp_step(b, n):
                    act.wait_ge(max_done.sem, max_done.at(b, n + 1))
                    act.wait_ge(pt_ready.sem, pt_ready.at(b, first_group[n - 1] if n >= 2 else
                                                          first_group[NS - 1 + n] - NG))
                    nc.scalar.activation(prob[:, n % 2, 0:(steps[n][0] + 1) * P], score_rows(n), ACT.Exp,
                                         bias=neg_max[:, n:n + 1], accum_out=row_sum[:, n:n + 1]).then_inc(p_done.sem, 1)

                def evacuate_probs(b, n):
                    i = steps[n][0]
                    act.wait_ge(o_ready.sem, o_ready.at(b, n - 1))
                    for g in range(groups[n]):
                        c = first_group[n] + g
                        js = slice(g * UT, min((g + 1) * UT, i + 1))
                        act.wait_ge(pt_ready.sem, pt_ready.at(b, c + 1))
                        nc.scalar.activation(probT[:, n % 2, js, :],
                                             PS[:, 4 + c % 2, 0:(js.stop - js.start) * P].rearrange("p (j q) -> p j q", q=P),
                                             ACT.Copy).then_inc(pt_done.sem, 1)

                def evacuate_out(b, n):
                    act.wait_ge(o_ready.sem, o_ready.at(b, n + 1))
                    act.wait_ge(y_ready.sem, y_ready.at(b, n - NO + 1))
                    nc.scalar.activation(oT[:, n % NO, :], O, ACT.Copy).then_inc(o_done.sem, 1)

                def turn(b, last):
                    for t in range(TB):
                        act.wait_ge(v_ready.sem, v_ready.at(b, t + 1))
                        nc.scalar.activation(V[:, t, :], PS[:, 2 + t % 2, 0:HA * DA], ACT.Copy).then_inc(v_done.sem, 1)
                    exp_step(b, 0)
                    for n in range(NS):
                        if n + 1 < NS:
                            exp_step(b, n + 1)
                        evacuate_probs(b, n)
                        if n >= NS - NHALF and not last:
                            sx[n - (NS - NHALF)].act(act, b + 1)
                        if n > 0:
                            evacuate_out(b, n - 1)
                    evacuate_out(b, NS - 1)

                for s in sx:
                    s.act(act, 0)
                with act.Fori(0, NB - 1) as b:
                    turn(b, False)
                turn(NB - 1, True)

            @block.vector
            def _(dve):
                for s in sx:
                    s.dve_open(dve)
                open_signals(dve, proj_used, max_done, inv_done, y_done)
                ln.dve_open(dve)

                def stats(b):
                    dve.wait_ge(x_loaded, (b + 1) * 16)
                    ln.dve_stats(dve, b)

                def row_max(b, n):
                    dve.wait_ge(s_ready.sem, s_ready.at(b, n + 1))
                    nc.vector.tensor_reduce(neg_max[:, n:n + 1], score_rows(n), AX.X, ALU.max,
                                            negate=True).then_inc(max_done.sem, 1)

                def inverse(b, n):
                    dve.wait_ge(p_done.sem, p_done.at(b, n + 1))
                    nc.vector.reciprocal(row_inv[:, n:n + 1], row_sum[:, n:n + 1]).then_inc(inv_done.sem, 1)

                def residual(b, n):
                    dve.wait_ge(y_ready.sem, y_ready.at(b, n + 1))
                    dve.wait_ge(inv_done.sem, inv_done.at(b, n + 1))
                    dve.wait_ge(y_done.sem, y_done.at(b, n))
                    x = X[:, bass.ds(b * TB + steps[n][0], 1), :].rearrange("p a m -> p (a m)")
                    nc.vector.scalar_tensor_tensor(x, Y, row_inv[:, n:n + 1], x,
                                                   ALU.mult, ALU.add).then_inc(y_done.sem, 1)

                def turn(b, last):
                    for half in range(NHALF):
                        at = slice(half * UN, (half + 1) * UN)
                        for s in range(2):
                            for j in range(3):
                                m = NQK * half + 3 * s + j
                                dve.wait_ge(proj_ready.sem, proj_ready.at(b, m + 1))
                                if j < HA:
                                    dst, table = qk[:, s, j, at], cos[:, j, at]
                                else:
                                    dve.wait_ge(rotated.sem, rotated.at(b, 2 * half + s - 1))
                                    dst, table = swapped[:, s, :], sin[:, at]
                                nc.vector.tensor_tensor(dst, PS[:, PROJ_RING[m % 4], :], table, ALU.mult).then_inc(proj_used.sem, 1)
                    row_max(b, 0)
                    row_max(b, 1)
                    for n in range(NS):
                        inverse(b, n)
                        if n + 2 < NS:
                            row_max(b, n + 2)
                        elif not last:
                            sx[n + 2 - NS].dve(dve, b + 1)
                        if n >= 2:
                            residual(b, n - 2)
                        if n == 4 and not last:
                            stats(b + 1)
                        if n == 7 and not last:
                            ln.dve_normalise(dve, b + 1)
                    residual(b, NS - 2)
                    residual(b, NS - 1)

                stats(0)
                nq = WQK // 2
                dve.wait_ge(prep_hi, 2)
                nc.vector.scalar_tensor_tensor(wqkv_lo[:, :, 0:nq], wqkv_raw[:, :, 0:nq], QK_SCALE,
                                               wqkv_hi[:, :, 0:nq].bitcast(F32), ALU.mult, ALU.subtract).then_inc(prep_done, 1)
                ln.dve_normalise(dve, 0)
                nc.vector.tensor_tensor(wqkv_lo[:, :, nq:], wqkv_raw[:, :, nq:], wqkv_hi[:, :, nq:].bitcast(F32),
                                        ALU.subtract).then_inc(prep_done, 1)
                dve.wait_ge(const_loaded, 16 * N_CONST)
                nc.vector.tensor_copy(ident_b[:], ident[:]).then_inc(prep_done, 1)
                nc.vector.tensor_copy(mask_b[:], mask_f[:]).then_inc(prep_done, 1)
                for s in sx:
                    s.dve(dve, 0)
                with dve.Fori(0, NB - 1) as b:
                    turn(b, False)
                turn(NB - 1, True)

            @block.tensor
            def _(pe):
                for s in sx:
                    s.pe_open(pe)
                open_signals(pe, proj_ready, v_ready, s_ready, pt_ready, o_ready, y_ready)

                def scores(b, n):
                    i, h = steps[n]
                    if n >= 2:
                        pe.wait_ge(p_done.sem, p_done.at(b, n - 1))
                    keys = (i + 1) * P
                    for c in range(0, keys, UN):
                        w = min(UN, keys - c)
                        diag = c + w == keys
                        bank = PS[:, 2 * (n % 2) + c // UN, :]
                        last = nc.tensor.matmul(bank[:, 0:w], qk[:, 0, h, i * P:(i + 1) * P], qk[:, 1, h, c:c + w],
                                                start=True, stop=not diag)
                        if diag:
                            last = nc.tensor.matmul(bank[:, w - P:w], ident_b[:], mask_b[:], start=False, stop=True)
                    last.then_inc(s_ready.sem, 1)

                def transpose_probs(b, n):
                    i = steps[n][0]
                    pe.wait_ge(p_done.sem, p_done.at(b, n + 1))
                    for g in range(groups[n]):
                        c = first_group[n] + g
                        pe.wait_ge(pt_done.sem, pt_done.at(b, c - 1))
                        for j in range(g * UT, min((g + 1) * UT, i + 1)):
                            last = nc.tensor.transpose(PS[:, 4 + c % 2, (j % UT) * P:(j % UT + 1) * P],
                                                       prob[:, n % 2, j * P:(j + 1) * P], ident[:])
                        last.then_inc(pt_ready.sem, 1)

                def weighted_values(b, n):
                    i, h = steps[n]
                    pe.wait_ge(pt_done.sem, pt_done.at(b, first_group[n + 1]))
                    pe.wait_ge(o_done.sem, o_done.at(b, n))
                    for j in range(i + 1):
                        last = nc.tensor.matmul(O, V[:, j, h * DA:(h + 1) * DA], probT[:, n % 2, j, :],
                                                start=j == 0, stop=j == i)
                    last.then_inc(o_ready.sem, 1)

                def out_projection(b, n):
                    pe.wait_ge(o_done.sem, o_done.at(b, n + 1))
                    pe.wait_ge(y_done.sem, y_done.at(b, n))
                    nc.tensor.matmul(Y, oT[:, n % NO, :], wo[:, steps[n][1], :], start=True,
                                     stop=True).then_inc(y_ready.sem, 1)

                def turn(b, last):
                    pe.wait_ge(pt_done.sem, pt_done.at(b, 0))
                    for half in range(NHALF):
                        sx[half].pe_wait(pe, b)
                        for j in range(NQK):
                            m = NQK * half + j
                            if m >= 4:
                                pe.wait_ge(proj_used.sem, proj_used.at(b, m - 3))
                            project(nc, PS[:, PROJ_RING[m % 4], :], sx[half], wqkv_hi, wqkv_lo,
                                    slice(j * P, (j + 1) * P)).then_inc(proj_ready.sem, 1)
                    for t in range(TB):
                        pe.wait_ge(v_done.sem, v_done.at(b, t - 1))
                        project_tokens(nc, PS[:, 2 + t % 2, 0:HA * DA], sx[t // UT], wqkv_hi, wqkv_lo,
                                       slice(WQK, WQK + HA * DA), t % UT).then_inc(v_ready.sem, 1)
                    pe.wait_ge(proj_used.sem, proj_used.at(b, NPROJ))
                    pe.wait_ge(rotated.sem, rotated.at(b, 2 * NHALF))
                    scores(b, 0)
                    pe.wait_ge(v_done.sem, v_done.at(b, TB))
                    scores(b, 1)
                    for n in range(NS):
                        transpose_probs(b, n)
                        if n + 2 < NS:
                            scores(b, n + 2)
                        elif not last:
                            sx[n + 2 - NS].pe(pe, b + 1, b + 1)
                        if n >= 1:
                            weighted_values(b, n - 1)
                        if n >= 2:
                            out_projection(b, n - 2)
                    weighted_values(b, NS - 1)
                    out_projection(b, NS - 2)
                    out_projection(b, NS - 1)

                pe.wait_ge(const_loaded, 16 * N_CONST)
                for s in sx:
                    s.pe(pe, 0, 0)
                pe.wait_ge(prep_done, 4)
                with pe.Fori(0, NB - 1) as b:
                    turn(b, False)
                turn(NB - 1, True)


def load_ff_weights(eng, env, io):
    stage = env["stage"].bitcast(I32)
    for n, name in enumerate(("w_gate", "w_up")):
        eng.dma_start(stage[:, n * KT * FF:(n + 1) * KT * FF].rearrange("p (k f) -> p k f", k=KT),
                      io[name].rearrange("(k p) f -> p k f", p=P)).then_inc(env["ff_loaded"], 16)
    eng.dma_start(stage[:, 2 * KT * FF:2 * KT * FF + NF * M].rearrange("p (k m) -> p k m", k=NF),
                  io["w_down"].rearrange("(k p) m -> p k m", p=P)).then_inc(env["ff_loaded"], 16)


LB_COLS = 4 * HD


def load_lin_weights(eng, env, io):
    stage = env["stage"]
    eng.dma_start(stage[:, 0:KT * LB_COLS].rearrange("p (k n) -> p k n", k=KT),
                  io["w_lin"].rearrange("(k p) n -> p k n", p=P)).then_inc(env["lin_loaded"], 16)
    eng.dma_start(stage[:, KT * LB_COLS:KT * LB_COLS + NP * M].rearrange("p (k m) -> p k m", k=NP),
                  io["w_o"].rearrange("(k p) m -> p k m", p=P)).then_inc(env["lin_loaded"], 16)


def feed_forward_phase(nc, env, io, name, nth, final):
    X, PS, ident, stage = env["X"], env["PS"], env["ident"], env["stage"]
    with ExitStack() as ctx:
        sb = lambda n, shape, dt=F32: ctx.enter_context(nc.sbuf_tensor(f"{name}_{n}", shape, dt))
        sem = lambda n: ctx.enter_context(nc.semaphore(f"{name}_{n}"))
        sig = lambda n, per: Signal(nc, ctx, f"{name}_{n}", per)

        NW = 2 * KT * FF + NF * M
        parts_of_w = [slice(0, KT * FF), slice(KT * FF, 2 * KT * FF), slice(2 * KT * FF, NW)]
        NPART = len(parts_of_w)
        w_hi, w_lo = sb("w_hi", [P, NW], F32R), sb("w_lo", [P, NW], F32R)
        gu = lambda w, n: w[:, parts_of_w[n]].rearrange("p (k f) -> p k f", k=KT)
        gate_hi, up_hi, gate_lo, up_lo = gu(w_hi, 0), gu(w_hi, 1), gu(w_lo, 0), gu(w_lo, 1)
        down_hi, down_lo = (w[:, parts_of_w[2]].rearrange("p (k m) -> p k m", k=NF) for w in (w_hi, w_lo))
        low_squares = sb("low_squares", [P, NPART])
        low_any = sb("low_any", [1, 1])
        ln = Layernorm(nc, ctx, f"{name}_ln", UT, X)
        sx = [SplitTransposed(nc, ctx, f"{name}_{par}", PS[:, 0:2, :], ident, ln) for par in range(2)]
        silu = sb("silu", [P, 2, UN])
        h = sb("h", [P, 2, UN])
        NH = 3
        h_hi, h_lo = sb("h_hi", [P, NH, UN], F32R), sb("h_lo", [P, NH, UN], F32R)
        LAG = 2

        prep_hi, prep_lo, prep_sq = sem("prep_hi"), sem("prep_lo"), sem("prep_sq")
        low_t, low_done = sem("low_t"), sem("low_done")
        gate_ready, up_ready = sig("gate_ready", NF), sig("up_ready", NF)
        silu_done, h_done = sig("silu_done", NF), sig("h_done", NF)
        hi_done, lo_done, down_done = sig("h_hi_done", NF), sig("h_lo_done", NF), sig("down_done", NF)
        x_done = sig("x_done", 1)
        stored = sem("stored")
        Y = PS[:, 6:8, :]
        out_v = io["out"].rearrange("b (n p) m -> p (b n) m", p=P)

        def run_units(eng, unit):
            unit(0, 0, 0, True, False)
            with eng.Fori(0, NU // 2 - 1) as p:
                unit(p * 2 + 1, 1, p, False, False)
                unit(p * 2 + 2, 0, p + 1, False, False)
            unit(NU - 1, 1, NU // 2 - 1, False, True)

        def next_of(par, turn):
            return 1 - par, turn + par

        with nc.Block() as block:

            @block.sync
            def _(sp):
                if final:
                    with sp.Fori(0, NU) as u:
                        sp.wait_ge(x_done.sem, x_done.at(u, 1))
                        at = bass.ds(u * UT, UT)
                        sp.dma_start(out_v[:, at, :], X[:, at, :]).then_inc(stored, 16)
                    sp.wait_ge(stored, 16 * NU)
                else:
                    sp.wait_ge(prep_sq, NPART)
                    load_lin_weights(sp, env, io)

            @block.gpsimd
            def _(pool):
                ln.pool_open(pool)
                ln.pool_rstd(pool, 0)
                with pool.Fori(0, NU - 1) as u:
                    ln.pool_rstd(pool, u + 1)

            @block.scalar
            def _(act):
                for s in sx:
                    s.act_open(act)
                open_signals(act, silu_done, hi_done)
                act.wait_ge(env["ff_loaded"], 48 * nth)
                for n, at in enumerate(parts_of_w):
                    nc.scalar.activation(w_hi[:, at], stage[:, at].bitcast(I32), ACT.Copy).then_inc(prep_hi, 1)
                sx[0].act(act, 0)
                for n, at in enumerate(parts_of_w):
                    act.wait_ge(prep_lo, n + 1)
                    nc.scalar.activation(stage[:, at], w_lo[:, at].bitcast(F32), ACT.Square,
                                         accum_out=low_squares[:, n:n + 1]).then_inc(prep_sq, 1)

                def high_part(u, f):
                    act.wait_ge(h_done.sem, h_done.at(u, f + 1))
                    act.wait_ge(down_done.sem, down_done.at(u, f - NH + 1))
                    nc.scalar.activation(h_hi[:, f % NH, :], h[:, f % 2, :], ACT.Copy).then_inc(hi_done.sem, 1)

                def unit(u, par, turn, first, last):
                    for f in range(NF):
                        act.wait_ge(gate_ready.sem, gate_ready.at(u, f + 1))
                        act.wait_ge(h_done.sem, h_done.at(u, f - 1))
                        nc.scalar.activation(silu[:, f % 2, :], PS[:, 2 + f % 2, :], ACT.Silu,
                                             scale=W_SCALE).then_inc(silu_done.sem, 1)
                        if f > 0 or not first:
                            high_part(u, f - 1)
                        if f == NF - 2 and not last:
                            npar, nturn = next_of(par, turn)
                            sx[npar].act(act, nturn)
                    if last:
                        high_part(u, NF - 1)

                run_units(act, unit)

            @block.vector
            def _(dve):
                for s in sx:
                    s.dve_open(dve)
                open_signals(dve, h_done, lo_done, x_done)
                ln.dve_open(dve)
                ln.dve_stats(dve, 0)
                for n, at in enumerate(parts_of_w):
                    dve.wait_ge(prep_hi, n + 1)
                    nc.vector.tensor_tensor(w_lo[:, at], stage[:, at].bitcast(I32), w_hi[:, at].bitcast(F32),
                                            ALU.subtract).then_inc(prep_lo, 1)
                    if n == 0:
                        ln.dve_normalise(dve, 0)
                sx[0].dve(dve, 0)
                dve.wait_ge(low_t, 1)
                nc.vector.tensor_reduce(low_any[:], PS[0:1, 7, 0:NPART * P], AX.X, ALU.max).then_inc(low_done, 1)

                def low_part(u, f):
                    dve.wait_ge(hi_done.sem, hi_done.at(u, f + 1))
                    dve.wait_ge(down_done.sem, down_done.at(u, f - NH + 1))
                    nc.vector.tensor_tensor(h_lo[:, f % NH, :], h[:, f % 2, :], h_hi[:, f % NH, :].bitcast(F32),
                                            ALU.subtract).then_inc(lo_done.sem, 1)

                def residual(u, done):
                    dve.wait_ge(down_done.sem, done)
                    x = X[:, bass.ds(u * UT, UT), :].rearrange("p a m -> p (a m)")
                    nc.vector.scalar_tensor_tensor(x, Y.rearrange("p a b -> p (a b)"), W_SCALE, x,
                                                   ALU.mult, ALU.add).then_inc(x_done.sem, 1)

                def unit(u, par, turn, first, last):
                    npar, nturn = next_of(par, turn)
                    for f in range(NF):
                        if f == NF - 1 and not last:
                            sx[npar].dve(dve, nturn)
                        dve.wait_ge(up_ready.sem, up_ready.at(u, f + 1))
                        dve.wait_ge(silu_done.sem, silu_done.at(u, f + 1))
                        dve.wait_ge(lo_done.sem, lo_done.at(u, f - 1))
                        nc.vector.scalar_tensor_tensor(h[:, f % 2, :], PS[:, 4 + f % 2, :], W_SCALE, silu[:, f % 2, :],
                                                       ALU.mult, ALU.mult).then_inc(h_done.sem, 1)
                        if f > 0 or not first:
                            low_part(u, f - 1)
                        if f == LAG - 1 and not first:
                            residual(u - 1, down_done.at(u, 0))
                        if not last:
                            if f == 0:
                                ln.dve_tile_stats(dve, u + 1, range(0, UT // 2))
                            if f == 2:
                                ln.dve_tile_stats(dve, u + 1, range(UT // 2, UT))
                                ln.dve_aggregate(dve, u + 1)
                            if f == 3:
                                ln.dve_normalise(dve, u + 1)
                    if last:
                        low_part(u, NF - 1)
                        residual(u, down_done.at(u, NF))

                run_units(dve, unit)

            @block.tensor
            def _(pe):
                for s in sx:
                    s.pe_open(pe)
                open_signals(pe, gate_ready, up_ready, down_done)
                sx[0].pe(pe, 0, 0)
                pe.wait_ge(prep_sq, NPART)
                for n in range(NPART):
                    ins = nc.tensor.transpose(PS[0:1, 7, n * P:(n + 1) * P], low_squares[:, n:n + 1], ident[:])
                ins.then_inc(low_t, 1)
                pe.wait_ge(low_done, 1)
                wide = pe.value_load(low_any[:].bitcast(I32))

                def gate_or_up(sxu, bank, hi, lo, f, terms, done):
                    at = slice(f * P, (f + 1) * P)
                    parts = [p for k in range(KT) for p in sxu.terms(hi[:, k, at], lo[:, k, at], k)[:terms]]
                    for n, (w, x) in enumerate(parts):
                        ins = nc.tensor.matmul(PS[:, bank, :], w, x, start=n == 0, stop=n == len(parts) - 1)
                    ins.then_inc(done.sem, 1)

                def down(u, f, terms):
                    pe.wait_ge(hi_done.sem, hi_done.at(u, f + 1))
                    pe.wait_ge(lo_done.sem, lo_done.at(u, f + 1))
                    parts = [(a, w) for w in ((down_hi,) if terms == 2 else (down_hi, down_lo)) for a in (h_hi, h_lo)]
                    for t in range(UT):
                        for n, (a, w) in enumerate(parts):
                            ins = nc.tensor.matmul(Y[:, t // 2, (t % 2) * M:(t % 2 + 1) * M],
                                                   a[:, f % NH, t * P:(t + 1) * P], w[:, f % NF, :],
                                                   start=f == 0 and n == 0 and t % 2 == 0,
                                                   stop=f % NF == NF - 1 and n == len(parts) - 1, skip_group_check=True)
                    ins.then_inc(down_done.sem, 1)

                def units(terms):
                    def unit(u, par, turn, first, last):
                        sx[par].pe_wait(pe, turn)
                        for f in range(NF):
                            pe.wait_ge(silu_done.sem, silu_done.at(u, f - 1))
                            gate_or_up(sx[par], 2 + f % 2, gate_hi, gate_lo, f, terms, gate_ready)
                            pe.wait_ge(h_done.sem, h_done.at(u, f - 1))
                            gate_or_up(sx[par], 4 + f % 2, up_hi, up_lo, f, terms, up_ready)
                            if f == NF - 2 and not last:
                                npar, nturn = next_of(par, turn)
                                sx[npar].pe(pe, nturn, u + 1)
                            if f == LAG:
                                pe.wait_ge(x_done.sem, x_done.at(u, 0))
                            if f >= LAG or not first:
                                down(u, f - LAG, terms)
                        if last:
                            for f in range(NF - LAG, NF):
                                down(u, f, terms)

                    run_units(pe, unit)

                with pe.If(wide == 0):
                    units(2)
                with pe.If(wide != 0):
                    units(4)


def linear_attention_phase(nc, env, io):
    X, PS, ident, stage = env["X"], env["PS"], env["ident"], env["stage"]
    with ExitStack() as ctx:
        sb = lambda n, shape, dt=F32: ctx.enter_context(nc.sbuf_tensor(f"lin_{n}", shape, dt))
        sem = lambda n: ctx.enter_context(nc.semaphore(f"lin_{n}"))
        sig = lambda n, per: Signal(nc, ctx, f"lin_{n}", per)

        NHALF = T // UN
        w_hi, w_lo = sb("w_hi", [P, KT, LB_COLS], F32R), sb("w_lo", [P, KT, LB_COLS], F32R)
        w_o = stage[:, KT * LB_COLS:KT * LB_COLS + NP * M].rearrange("p (k m) -> p k m", k=NP)
        w_o = sb("w_o", [P, NP, M])
        bias = sb("bias", [P, NP])
        decay_in = sb("decay_in", [P, HB + NP])
        log_g = sb("log_g", [P, HB + NP])
        tmp_a, tmp_b = sb("tmp_a", [P, HB + NP]), sb("tmp_b", [P, HB + NP])
        dist = sb("dist", [P, 3, P])
        rev = sb("rev", [P, 1])
        D = sb("decay", [P, HB, P])
        Gq = sb("decay_q", [P, NP, P])
        Gk = sb("decay_k", [P, HB])
        Gc = sb("decay_c", [P, NP])

        ln = Layernorm(nc, ctx, "lin_ln", UT, X)
        sx = SplitTransposed(nc, ctx, "lin", PS[:, 0:2, :], ident, ln)
        e = sb("e", [P, 2, UN])
        qT, kT, qsT, gate = (sb(n, [P, NP, UN]) for n in ("qT", "kT", "qsT", "gate"))
        v = sb("v", [P, UT, HB, VA])
        AD = sb("AD", [P, 2, 2, NP, P])
        ks = sb("ks", [P, 2, HB, DK])
        S = sb("state", [P, NP, 2 * VA])
        den, inv = sb("den", [P, 2, HG]), sb("inv", [P, 2, HG])
        y = sb("y", [P, 2, HD])
        yg = sb("yg", [P, NP, P])

        NC = TB
        RING = (4, 5, 2, 3)
        NITEM = 3 * NP + UT

        const_loaded = sem("const_loaded")
        prep, prep_act, zeroed = sem("prep"), sem("prep_act"), sem("zeroed")
        proj_ready = sig("proj_ready", NHALF * NITEM)
        relu_done, exp_done, phi_done = (sig(n, NHALF * 2 * NP) for n in ("relu_done", "exp_done", "phi_done"))
        qs_done = sig("qs_done", NHALF * NP)
        gate_done, v_done = sig("gate_done", NHALF * NP), sig("v_done", NC)
        kt_ready, ks_done = sig("kt_ready", NC), sig("ks_done", NC)
        a_ready, ad_done = sig("a_ready", 2 * NC), sig("ad_done", 2 * NC)
        o_ready, den_done, inv_done, y_done = (sig(n, 2 * NC) for n in ("o_ready", "den_done", "inv_done", "y_done"))
        st_ready, s_done = sig("st_ready", 2 * NC), sig("s_done", 2 * NC)
        yt_ready, yg_done = sig("yt_ready", NC), sig("yg_done", NC)
        out_ready, x_done = sig("out_ready", NC), sig("x_done", NC)

        with nc.Block() as block:

            @block.sync
            def _(sp):
                sp.dma_start(bias[:], io["b_g"]).then_inc(const_loaded, 16)
                sp.dma_start(decay_in[:], io["decay"]).then_inc(const_loaded, 16)
                sp.dma_start(dist[:], io["dist"]).then_inc(const_loaded, 16)
                sp.dma_start(rev[:], io["rev"]).then_inc(const_loaded, 16)
                sp.wait_ge(prep, 4)
                load_ff_weights(sp, env, io)

            @block.gpsimd
            def _(pool):
                open_signals(pool, qs_done)
                nc.gpsimd.memset(S[:], 0.0).then_inc(zeroed, 1)
                nc.gpsimd.memset(v[:], 1.0).then_inc(zeroed, 1)
                ln.pool_open(pool)

                def turn(b, last):
                    for half in range(NHALF):
                        for j in range(NP):
                            pool.wait_ge(phi_done.sem, phi_done.at(b, 2 * NP * half + 2 * j + 1))
                            nc.gpsimd.tensor_tensor(qsT[:, j, :].rearrange("p (c t) -> p c t", t=P),
                                                    qT[:, j, :].rearrange("p (c t) -> p c t", t=P),
                                                    Gq[:, j, :].unsqueeze(1).to_broadcast([P, UT, P]),
                                                    ALU.mult).then_inc(qs_done.sem, 1)
                        if not (last and half == NHALF - 1):
                            ln.pool_rstd(pool, b * NHALF + half + 1)

                ln.pool_rstd(pool, 0)
                pool.wait_ge(prep_act, 4)
                with pool.Fori(0, NB - 1) as b:
                    turn(b, False)
                turn(NB - 1, True)

            @block.scalar
            def _(act):
                open_signals(act, sx.hi_done, relu_done, exp_done, gate_done, v_done)
                act.wait_ge(prep, 5)
                nc.scalar.activation(tmp_b[:], tmp_a[:], ACT.Exp, scale=-1.0).then_inc(prep_act, 1)
                act.wait_ge(prep_act, 1)
                nc.scalar.activation(tmp_a[:], tmp_b[:], ACT.Ln, bias=1.0).then_inc(prep_act, 1)
                act.wait_ge(prep, 8)
                for hd in range(HB):
                    nc.scalar.activation(D[:, hd, :], dist[:, 0, :], ACT.Exp, scale=log_g[:, hd:hd + 1])
                for j in range(NP):
                    nc.scalar.activation(Gq[:, j, :], dist[:, 2, :], ACT.Exp, scale=log_g[:, HB + j:HB + j + 1])
                nc.scalar.activation(Gc[:], log_g[:, HB:], ACT.Exp, scale=float(P)).then_inc(prep_act, 1)
                nc.scalar.activation(Gk[:], tmp_b[:, 0:HB], ACT.Exp).then_inc(prep_act, 1)
                nc.scalar.mul(bias[:], bias[:], 0.5).then_inc(prep_act, 1)
                act.wait_ge(prep_act, 5)
                act.wait_ge(zeroed, 2)

                def turn(b):
                    for half in range(NHALF):
                        sx.act(act, b * NHALF + half)
                        for it in range(NITEM):
                            m = NITEM * half + it
                            src = PS[:, RING[m % 4], :]
                            act.wait_ge(proj_ready.sem, proj_ready.at(b, m + 1))
                            if it < 2 * NP:
                                n = 2 * NP * half + it
                                act.wait_ge(phi_done.sem, phi_done.at(b, n - 1))
                                nc.scalar.activation(e[:, it % 2, :], src, ACT.Relu, scale=-1.0).then_inc(relu_done.sem, 1)
                                act.wait_ge(relu_done.sem, relu_done.at(b, n + 1))
                                nc.scalar.activation(e[:, it % 2, :], e[:, it % 2, :], ACT.Exp,
                                                     scale=-1.0).then_inc(exp_done.sem, 1)
                            elif it < 3 * NP:
                                j = it - 2 * NP
                                nc.scalar.activation(gate[:, j, :], src, ACT.Tanh, bias=bias[:, j:j + 1],
                                                     scale=0.5).then_inc(gate_done.sem, 1)
                            else:
                                t = it - 3 * NP
                                nc.scalar.activation(v[:, t, :, 0:DK], src.rearrange("p (h d) -> p h d", d=DK),
                                                     ACT.Copy).then_inc(v_done.sem, 1)

                with act.Fori(0, NB) as b:
                    turn(b)

            @block.vector
            def _(dve):
                open_signals(dve, sx.lo_done, phi_done, ks_done, ad_done, den_done, inv_done, y_done, s_done, yg_done, x_done)
                ln.dve_open(dve)
                dve.wait_ge(env["lin_loaded"], 32)
                raw = stage[:, 0:KT * LB_COLS].rearrange("p (k n) -> p k n", k=KT)
                nc.vector.tensor_copy(w_hi[:], raw).then_inc(prep, 1)
                nc.vector.tensor_copy(w_o[:], stage[:, KT * LB_COLS:KT * LB_COLS + NP * M].rearrange(
                    "p (k m) -> p k m", k=NP)).then_inc(prep, 1)
                dve.wait_ge(prep, 2)
                nc.vector.tensor_tensor(w_lo[:], raw, w_hi[:].bitcast(F32), ALU.subtract).then_inc(prep, 1)
                dve.wait_ge(prep, 3)
                dve.wait_ge(const_loaded, 64)
                nc.vector.tensor_scalar(log_g[:], decay_in[:], 0.0, None, ALU.min).then_inc(prep, 1)
                nc.vector.scalar_tensor_tensor(tmp_a[:], decay_in[:], -1.0, decay_in[:], ALU.mult, ALU.max).then_inc(prep, 1)
                dve.wait_ge(prep_act, 2)
                nc.vector.tensor_tensor(log_g[:], log_g[:], tmp_a[:], ALU.subtract).then_inc(prep, 1)
                dve.wait_ge(prep, 6)
                nc.vector.tensor_scalar(log_g[:], log_g[:], -200.0, None, ALU.max).then_inc(prep, 1)
                dve.wait_ge(prep, 7)
                nc.vector.tensor_scalar(tmp_b[:], log_g[:], rev[:], None, ALU.mult).then_inc(prep, 1)
                dve.wait_ge(prep_act, 4)
                nc.vector.tensor_tensor(D[:], D[:], dist[:, 1, :].unsqueeze(1).to_broadcast([P, HB, P]),
                                        ALU.mult).then_inc(prep, 1)
                dve.wait_ge(prep, 9)
                dve.wait_ge(zeroed, 2)

                def phi_item(b, half, it):
                    n = 2 * NP * half + it
                    m = NITEM * half + it
                    dve.wait_ge(exp_done.sem, exp_done.at(b, n + 1))
                    dst = (qT, kT)[it % 2]
                    nc.vector.scalar_tensor_tensor(dst[:, it // 2, :], PS[:, RING[m % 4], :], 1.0, e[:, it % 2, :],
                                                   ALU.add, ALU.max).then_inc(phi_done.sem, 1)

                def scaled_keys(b, c):
                    dve.wait_ge(kt_ready.sem, kt_ready.at(b, c + 1))
                    nc.vector.tensor_tensor(ks[:, c % 2], PS[:, 4, :].rearrange("p (h d) -> p h d", d=DK),
                                            Gk[:].unsqueeze(2).to_broadcast([P, HB, DK]), ALU.mult).then_inc(ks_done.sem, 1)

                def decayed_scores(b, c, r):
                    dve.wait_ge(a_ready.sem, a_ready.at(b, 2 * c + r + 1))
                    nc.vector.tensor_tensor(AD[:, c % 2, r], PS[:, r, :].rearrange("p (j t) -> p j t", t=P),
                                            D[:].rearrange("p (j r) t -> p r j t", r=2)[:, r],
                                            ALU.mult).then_inc(ad_done.sem, 1)

                def quotient(b, c, g):
                    n = 2 * c + g
                    O = PS[:, 2 + g, 0:HG * VA].rearrange("p (h a) -> p h a", a=VA)
                    dve.wait_ge(o_ready.sem, o_ready.at(b, n + 1))
                    nc.vector.tensor_scalar(den[:, g, :], O[:, :, DK], DEN_EPS, 2.0, ALU.add, ALU.mult).then_inc(den_done.sem, 1)
                    dve.wait_ge(den_done.sem, den_done.at(b, n + 1))
                    nc.vector.reciprocal(inv[:, g, :], den[:, g, :]).then_inc(inv_done.sem, 1)
                    dve.wait_ge(inv_done.sem, inv_done.at(b, n + 1))
                    nc.vector.tensor_tensor(y[:, c % 2, HG * DK * g:HG * DK * (g + 1)].rearrange("p (h d) -> p h d", d=DK),
                                            O[:, :, 0:DK], inv[:, g, :].unsqueeze(2).to_broadcast([P, HG, DK]),
                                            ALU.mult).then_inc(y_done.sem, 1)

                def update_state(b, c, g):
                    n = 2 * c + g
                    dve.wait_ge(st_ready.sem, st_ready.at(b, n + 1))
                    for jj in range(2):
                        j = 2 * g + jj
                        for r in range(2):
                            rows, cols = slice(r * DK, (r + 1) * DK), slice(r * VA, (r + 1) * VA)
                            new = PS[rows, 5, jj * 2 * VA + r * VA:jj * 2 * VA + (r + 1) * VA]
                            if c == 0:
                                last = nc.vector.tensor_copy(S[rows, j, cols], new)
                            else:
                                last = nc.vector.scalar_tensor_tensor(S[rows, j, cols], S[rows, j, cols], Gc[rows, j:j + 1],
                                                                      new, ALU.mult, ALU.add)
                    last.then_inc(s_done.sem, 1)

                def gated(b, half, c):
                    ch = NC // NHALF * half + c
                    dve.wait_ge(yt_ready.sem, yt_ready.at(b, ch + 1))
                    dve.wait_ge(gate_done.sem, gate_done.at(b, NP * (half + 1)))
                    nc.vector.scalar_tensor_tensor(yg[:], gate[:, :, c * P:(c + 1) * P], 1.0,
                                                   PS[:, 6, :].rearrange("p (j t) -> p j t", t=P),
                                                   ALU.add, ALU.mult).then_inc(yg_done.sem, 1)

                def residual(b, ch):
                    dve.wait_ge(out_ready.sem, out_ready.at(b, ch + 1))
                    x = X[:, bass.ds(b * TB + ch, 1), :].rearrange("p a m -> p (a m)")
                    nc.vector.tensor_tensor(x, PS[:, 7, 0:M], x, ALU.add).then_inc(x_done.sem, 1)

                def turn(b, last):
                    for half in range(NHALF):
                        sx.dve(dve, b * NHALF + half)
                        for it in range(2 * NP):
                            phi_item(b, half, it)
                        c0 = UT * half
                        scaled_keys(b, c0)
                        decayed_scores(b, c0, 0)
                        decayed_scores(b, c0, 1)
                        for c in range(UT):
                            more = c + 1 < UT
                            if more:
                                scaled_keys(b, c0 + c + 1)
                            for g in range(2):
                                quotient(b, c0 + c, g)
                                update_state(b, c0 + c, g)
                                if more:
                                    decayed_scores(b, c0 + c + 1, g)
                            if c > 0:
                                gated(b, half, c - 1)
                                residual(b, c0 + c - 1)
                            if not (last and half == NHALF - 1):
                                if c == 0:
                                    ln.dve_stats(dve, b * NHALF + half + 1)
                                if c == 1:
                                    ln.dve_normalise(dve, b * NHALF + half + 1)
                        gated(b, half, UT - 1)
                        residual(b, c0 + UT - 1)

                ln.dve_stats(dve, 0)
                ln.dve_normalise(dve, 0)
                with dve.Fori(0, NB - 1) as b:
                    turn(b, False)
                turn(NB - 1, True)

            @block.tensor
            def _(pe):
                open_signals(pe, sx.transposed, proj_ready, kt_ready, a_ready, o_ready, st_ready, yt_ready, out_ready)
                pe.wait_ge(prep, 9)

                def projections(b, half):
                    c0 = UT * half
                    sx.pe_wait(pe, b * NHALF + half)
                    for it in range(NITEM):
                        m = NITEM * half + it
                        n = 2 * NP * half + it
                        if it == 0:
                            pe.wait_ge(ks_done.sem, ks_done.at(b, c0))
                            pe.wait_ge(s_done.sem, s_done.at(b, 2 * c0))
                            pe.wait_ge(y_done.sem, y_done.at(b, 2 * c0))
                        elif 4 <= it < 4 + 2 * NP:
                            pe.wait_ge(phi_done.sem, phi_done.at(b, n - 3))
                        elif it >= 4 + 2 * NP:
                            pe.wait_ge(gate_done.sem, gate_done.at(b, NP * half + it - 4 - 2 * NP + 1))
                        bank = PS[:, RING[m % 4], :]
                        if it < 2 * NP:
                            col = (it % 2) * HD + (it // 2) * P
                            ins = project(nc, bank, sx, w_hi, w_lo, slice(col, col + P))
                        elif it < 3 * NP:
                            col = 2 * HD + (it - 2 * NP) * P
                            ins = project(nc, bank, sx, w_hi, w_lo, slice(col, col + P))
                        else:
                            ins = project_tokens(nc, bank, sx, w_hi, w_lo, slice(3 * HD, 4 * HD), it - 3 * NP)
                        ins.then_inc(proj_ready.sem, 1)

                def keys(b, half, c):
                    ch = UT * half + c
                    pe.wait_ge(ks_done.sem, ks_done.at(b, ch))
                    for j in range(NP):
                        last = nc.tensor.transpose(PS[:, 4, j * P:(j + 1) * P], kT[:, j, c * P:(c + 1) * P], ident[:])
                    last.then_inc(kt_ready.sem, 1)

                def scores(b, half, c):
                    n = 2 * (UT * half + c)
                    at = slice(c * P, (c + 1) * P)
                    pe.wait_ge(ad_done.sem, ad_done.at(b, n))
                    for j in range(NP):
                        for r in range(2):
                            rows = slice(r * DK, (r + 1) * DK)
                            last = nc.tensor.matmul(PS[:, r, j * P:(j + 1) * P], kT[rows, j, at], qT[rows, j, at],
                                                    start=True, stop=True)
                            if j == NP - 1:
                                last.then_inc(a_ready.sem, 1)

                def outputs(b, half, c, g):
                    ch = UT * half + c
                    n = 2 * ch + g
                    pe.wait_ge(ad_done.sem, ad_done.at(b, 2 * ch + 2))
                    pe.wait_ge(y_done.sem, y_done.at(b, n - 1))
                    pe.wait_ge(s_done.sem, s_done.at(b, n - 1))
                    bank = PS[:, 2 + g, 0:HG * VA]
                    for hh in range(HG):
                        last = nc.tensor.matmul(bank[:, hh * VA:(hh + 1) * VA], AD[:, ch % 2, hh % 2, 2 * g + hh // 2, :], v[:, c, HG * g + hh, :],
                                                start=hh == 0, stop=ch == 0, skip_group_check=True)
                    if ch > 0:
                        for jj in range(2):
                            j = 2 * g + jj
                            last = nc.tensor.matmul(bank[:, jj * 2 * VA:(jj + 1) * 2 * VA], qsT[:, j, c * P:(c + 1) * P],
                                                    S[:, j, :], start=False, stop=True, skip_group_check=True)
                    last.then_inc(o_ready.sem, 1)

                def state(b, half, c, g):
                    ch = UT * half + c
                    n = 2 * ch + g
                    if g == 0:
                        pe.wait_ge(ks_done.sem, ks_done.at(b, ch + 1))
                    pe.wait_ge(s_done.sem, s_done.at(b, n))
                    for jj in range(2):
                        j = 2 * g + jj
                        last = nc.tensor.matmul(PS[:, 5, jj * 2 * VA:(jj + 1) * 2 * VA],
                                                ks[:, ch % 2, 2 * j:2 * j + 2, :].rearrange("p h d -> p (h d)"),
                                                v[:, c, 2 * j:2 * j + 2, :].rearrange("p h a -> p (h a)"),
                                                start=True, stop=True)
                    last.then_inc(st_ready.sem, 1)

                def out_projection(b, half, c):
                    ch = UT * half + c
                    pe.wait_ge(y_done.sem, y_done.at(b, 2 * ch + 2))
                    pe.wait_ge(yg_done.sem, yg_done.at(b, ch))
                    for j in range(NP):
                        last = nc.tensor.transpose(PS[:, 6, j * P:(j + 1) * P], y[:, ch % 2, j * P:(j + 1) * P], ident[:])
                    last.then_inc(yt_ready.sem, 1)
                    pe.wait_ge(yg_done.sem, yg_done.at(b, ch + 1))
                    pe.wait_ge(x_done.sem, x_done.at(b, ch))
                    for j in range(NP):
                        last = nc.tensor.matmul(PS[:, 7, 0:M], yg[:, j, :], w_o[:, j, :], start=j == 0, stop=j == NP - 1)
                    last.then_inc(out_ready.sem, 1)

                def turn(b, last):
                    for half in range(NHALF):
                        c0 = UT * half
                        projections(b, half)
                        pe.wait_ge(phi_done.sem, phi_done.at(b, 2 * NP * (half + 1)))
                        pe.wait_ge(v_done.sem, v_done.at(b, c0 + UT))
                        pe.wait_ge(qs_done.sem, qs_done.at(b, NP * (half + 1)))
                        keys(b, half, 0)
                        scores(b, half, 0)
                        for c in range(UT):
                            more = c + 1 < UT
                            if more:
                                keys(b, half, c + 1)
                            for g in range(2):
                                outputs(b, half, c, g)
                                state(b, half, c, g)
                                if more and g == 0:
                                    scores(b, half, c + 1)
                            if c > 0:
                                out_projection(b, half, c - 1)
                        if half + 1 < NHALF:
                            sx.pe(pe, b * NHALF + half + 1, b * NHALF + half + 1)
                        elif not last:
                            sx.pe(pe, (b + 1) * NHALF, (b + 1) * NHALF)
                        out_projection(b, half, UT - 1)

                sx.pe(pe, 0, 0)
                with pe.Fori(0, NB - 1) as b:
                    turn(b, False)
                turn(NB - 1, True)


def build(nc, io, phases=4):
    with ExitStack() as ctx:
        sb = lambda n, shape, dt=F32: ctx.enter_context(nc.sbuf_tensor(n, shape, dt))
        env = {
            "X": sb("X", [P, NT, M]),
            "ident": sb("ident", [P, P]),
            "stage": sb("stage", [P, KT * LB_COLS + NP * M]),
            "PS": ctx.enter_context(nc.psum_tensor("PS", [P, 8, UN], F32)),
            "ff_loaded": ctx.enter_context(nc.semaphore("ff_loaded")),
            "lin_loaded": ctx.enter_context(nc.semaphore("lin_loaded")),
        }
        env["stage"] = env["stage"][:, :]
        attention_phase(nc, env, io)
        if phases >= 2:
            feed_forward_phase(nc, env, io, "ff1", 1, phases == 2)
        if phases >= 3:
            linear_attention_phase(nc, env, io)
        if phases >= 4:
            feed_forward_phase(nc, env, io, "ff2", 2, True)
        if phases in (1, 3):
            with nc.Block() as block, nc.semaphore("dbg") as dbg:
                @block.sync
                def _(sp):
                    sp.dma_start(io["out"].rearrange("b (n p) m -> p (b n) m", p=P), env["X"][:]).then_inc(dbg, 16)
                    sp.wait_ge(dbg, 16)


PHASES = 4


def kernel(L0_attn_a_x, L0_attn_a_wq, L0_attn_a_wk, L0_attn_a_wv, L0_attn_a_wo, L0_attn_b_W_Q, L0_attn_b_W_K,
           L0_attn_b_W_V, L0_attn_b_W_g_w, L0_attn_b_W_g_b, L0_attn_b_W_O, L0_attn_b_decay_log, L0_ffn_w_gate,
           L0_ffn_w_up, L0_ffn_w_down):
    import concourse.bacc as bacc
    from concourse.bass_utils import run_bass_kernel_spmd as run

    a = lambda v: np.ascontiguousarray(np.asarray(v))

    def heads(w):
        w0, w1 = a(w)[:, 0, :], a(w)[:, 1, :]
        swap = lambda h: [h[:, HALF:ROT], h[:, 0:HALF]]
        return [w0, w1[:, ROT:], w1[:, :ROT]] + swap(w0) + swap(w1)

    w_qkv = np.concatenate(heads(L0_attn_a_wq) + heads(L0_attn_a_wk) + [a(L0_attn_a_wv).reshape(M, HA * DA)], axis=1)

    angle = np.power(np.float32(10000.0), -np.arange(HALF, dtype=np.float32) / np.float32(HALF)).astype(np.float32)
    rad = (angle[:, None] * np.arange(T, dtype=np.float32)[None, :]).astype(np.float32)
    c, s, one = np.cos(rad).astype(np.float32), np.sin(rad).astype(np.float32), np.ones((ROT, T), np.float32)
    cos = np.stack([np.concatenate([c, c, one]), np.concatenate([one, c, c])], axis=1)
    sin = np.concatenate([-s, s, -s, s])
    i = np.arange(P)
    causal = np.where(i[None, :] > i[:, None], np.float32(NEG), np.float32(0)).astype(np.float32)
    ahead = (i[None, :] - i[:, None]).astype(np.float32)
    dist = np.stack([np.maximum(ahead, 0), (ahead >= 0).astype(np.float32),
                     np.broadcast_to((i + 1).astype(np.float32), (P, P))], axis=1)

    d = a(L0_attn_b_decay_log)
    decay = np.concatenate([np.broadcast_to(d, (P, HB)), np.repeat(d.reshape(NP, 2).T, DK, axis=0)], axis=1)

    arrays = {
        "x": a(L0_attn_a_x), "w_qkv": a(w_qkv), "wo_a": a(L0_attn_a_wo).reshape(HA * DA, M),
        "ident": np.eye(P, dtype=np.float32), "causal": causal, "cos": a(cos), "sin": a(sin),
        "w_gate": a(a(L0_ffn_w_gate).T), "w_up": a(a(L0_ffn_w_up).T), "w_down": a(a(L0_ffn_w_down).T),
        "w_lin": a(np.concatenate([a(L0_attn_b_W_Q).T, a(L0_attn_b_W_K).T, a(L0_attn_b_W_g_w).T, a(L0_attn_b_W_V).T], axis=1)),
        "w_o": a(a(L0_attn_b_W_O).T), "b_g": a(a(L0_attn_b_W_g_b).reshape(NP, P).T), "decay": a(decay),
        "dist": a(dist), "rev": a((P - 1 - i).astype(np.float32)[:, None]),
    }
    nc = bacc.Bacc("TRN2", target_bir_lowering=False, num_devices=1)
    io = {}
    for name, v in arrays.items():
        io[name] = nc.dram_tensor(f"in_{name}", v.shape, mybir.dt.from_np(v.dtype), kind="ExternalInput").ap()
    io["out"] = nc.dram_tensor("out_x", (NB, T, M), F32, kind="ExternalOutput").ap()
    build(nc, io, PHASES)
    r = run(nc, [{f"in_{k}": v for k, v in arrays.items()}], core_ids=[0])
    return r.results[0]["out_x"]
```

```python
import concourse.bass as bass
from concourse import mybir
from contextlib import ExitStack
import numpy as np

F32 = mybir.dt.float32
F32R = mybir.dt.float32r
BF16 = mybir.dt.bfloat16
I32 = mybir.dt.int32
ALU = mybir.AluOpType
ACT = mybir.ActivationFunctionType
AX = mybir.AxisListType

P = 128
NB, T, M = 8, 1024, 256
KT = M // P
NT = NB * T // P
TB = T // P
UT = 4
UN = UT * P
NU = NT // UT
LN_EPS = 1e-5

HA, DA = 2, 128
ROT = DA // 2
HALF = ROT // 2
NQK = 2 * HA
WQK = NQK * P
QK_SCALE = 1.0 / DA
NEG = -1e30

FF = 768
NF = FF // P
W_SCALE = 1.0 / 127.0
NW = 2 * KT * FF + NF * M
NPART = 3
WPART = NW // NPART

HB, DK = 8, 64
HD = HB * DK
NP = HD // P
HG = 4
VA = DK + 1
DEN_EPS = 1e-6

CREDIT = 4


class Signal:

    def __init__(self, nc, ctx, name, per):
        self.sem = ctx.enter_context(nc.semaphore(name))
        self.per = per

    def at(self, turn, k):
        return turn * self.per + (CREDIT + k)


def open_signals(eng, *signals):
    for s in signals:
        eng.sem_inc(s.sem, CREDIT)


def wait_alone(eng, sem, value, passed):
    eng.wait_ge(sem, value)
    eng.sem_inc(passed, 1)


class NormBuffers:

    def __init__(self, nc, ctx):
        sb = lambda n, shape, dt=F32: ctx.enter_context(nc.sbuf_tensor(n, shape, dt))
        self.stats = sb("ln_stats", [P, TB, 6])
        self.mean_var = sb("ln_mean_var", [P, TB, 2])
        self.var_eps = sb("ln_var_eps", [P, TB])
        self.rstd = sb("ln_rstd", [P, TB])
        self.minus_half = sb("ln_minus_half", [P, TB])
        self.xn = sb("ln_xn", [P, TB, M])
        self.parts = sb("ln_xh", [P, KT, UN], F32R), sb("ln_xl", [P, KT, UN], F32R)


class Layernorm:

    def __init__(self, nc, ctx, name, tiles, X, bufs):
        self.nc, self.X, self.tiles = nc, X, tiles
        self.stats, self.mean_var, self.out = (t[:, 0:tiles, :] for t in (bufs.stats, bufs.mean_var, bufs.xn))
        self.var_eps, self.rstd, self.minus_half = (t[:, 0:tiles] for t in (bufs.var_eps, bufs.rstd, bufs.minus_half))
        self.stats_done = Signal(nc, ctx, f"{name}_stats_done", 1)
        self.mv_done = Signal(nc, ctx, f"{name}_mv_done", 1)
        self.ve_done = Signal(nc, ctx, f"{name}_ve_done", 1)
        self.rstd_done = Signal(nc, ctx, f"{name}_rstd_done", 1)
        self.dve_passed = ctx.enter_context(nc.semaphore(f"{name}_dve_passed"))
        self.pool_passed = ctx.enter_context(nc.semaphore(f"{name}_pool_passed"))
        self.ready = Signal(nc, ctx, f"{name}_ready", tiles // UT)

    def dve_open(self, dve):
        open_signals(dve, self.stats_done, self.mv_done, self.ready)

    def dve_tile_stats(self, dve, turn, some):
        for t in some:
            ins = self.nc.vector.bn_stats(self.stats[:, t, :], self.X[:, bass.ds(turn * self.tiles + t, 1), :])
            if t == self.tiles - 1:
                ins.then_inc(self.stats_done.sem, 1)

    def dve_aggregate(self, dve, turn):
        nc = self.nc
        wait_alone(dve, self.stats_done.sem, self.stats_done.at(turn, 1), self.dve_passed)
        for t in range(self.tiles):
            last = nc.vector.bn_aggr(self.mean_var[:, t, :], self.stats[:, t, :])
        last.then_inc(self.mv_done.sem, 1)

    def dve_stats(self, dve, turn):
        self.dve_tile_stats(dve, turn, range(self.tiles))
        self.dve_aggregate(dve, turn)

    def dve_normalise(self, dve, turn, some=None):
        nc = self.nc
        dve.wait_ge(self.rstd_done.sem, self.rstd_done.at(turn, 1))
        for t in some or range(self.tiles):
            last = nc.vector.tensor_scalar(self.out[:, t, :], self.X[:, bass.ds(turn * self.tiles + t, 1), :],
                                           self.mean_var[:, t, 0:1], self.rstd[:, t:t + 1],
                                           ALU.subtract, ALU.mult)
            if t % UT == UT - 1:
                last.then_inc(self.ready.sem, 1)

    def pool_open(self, pool):
        open_signals(pool, self.ve_done, self.rstd_done)

    def pool_rstd(self, pool, turn):
        nc = self.nc
        wait_alone(pool, self.mv_done.sem, self.mv_done.at(turn, 1), self.pool_passed)
        nc.gpsimd.tensor_scalar(self.var_eps, self.mean_var[:, :, 1], LN_EPS, None,
                                ALU.add).then_inc(self.ve_done.sem, 1)
        pool.wait_ge(self.ve_done.sem, self.ve_done.at(turn, 1))
        nc.gpsimd.tensor_tensor(self.rstd, self.var_eps, self.minus_half,
                                ALU.pow).then_inc(self.rstd_done.sem, 1)


class SplitTransposed:

    def __init__(self, nc, ctx, name, psum, ident, ln, unit=0, parts=None):
        sb = lambda n: ctx.enter_context(nc.sbuf_tensor(f"{name}_{n}", [P, KT, UN], F32R))
        self.nc, self.psum, self.ident, self.ln, self.unit = nc, psum, ident, ln, unit
        self.hi, self.lo = parts or (sb("xh"), sb("xl"))
        self.transposed = Signal(nc, ctx, f"{name}_transposed", 1)
        self.hi_done = Signal(nc, ctx, f"{name}_hi_done", 1)
        self.lo_done = Signal(nc, ctx, f"{name}_lo_done", 1)

    def pe_open(self, pe):
        open_signals(pe, self.transposed)

    def act_open(self, act):
        open_signals(act, self.hi_done)

    def dve_open(self, dve):
        open_signals(dve, self.lo_done)

    def pe(self, pe, turn, ln_turn):
        ln = self.ln
        pe.wait_ge(ln.ready.sem, ln.ready.at(ln_turn, self.unit + 1))
        for t in range(UT):
            for k in range(KT):
                last = self.nc.tensor.transpose(self.psum[:, k, t * P:(t + 1) * P],
                                                ln.out[:, self.unit * UT + t, k * P:(k + 1) * P], self.ident[:])
        last.then_inc(self.transposed.sem, 1)

    def act(self, act, turn):
        act.wait_ge(self.transposed.sem, self.transposed.at(turn, 1))
        self.nc.scalar.activation(self.hi[:], self.psum, ACT.Copy).then_inc(self.hi_done.sem, 1)

    def dve(self, dve, turn):
        dve.wait_ge(self.hi_done.sem, self.hi_done.at(turn, 1))
        self.nc.vector.tensor_tensor(self.lo[:], self.psum, self.hi[:].bitcast(F32),
                                     ALU.subtract).then_inc(self.lo_done.sem, 1)

    def pe_wait(self, pe, turn):
        pe.wait_ge(self.hi_done.sem, self.hi_done.at(turn, 1))
        pe.wait_ge(self.lo_done.sem, self.lo_done.at(turn, 1))

    def terms(self, w_hi, w_lo, k):
        return [(w_hi, self.hi[:, k, :]), (w_hi, self.lo[:, k, :]), (w_lo, self.hi[:, k, :]),
                (w_lo, self.lo[:, k, :])]


class Front:

    def __init__(self, nc, ctx, name, env):
        self.ln = Layernorm(nc, ctx, f"{name}_ln", UT, env["X"], env["norm"])
        self.sx = SplitTransposed(nc, ctx, name, env["PS"][:, 0:2, :], env["ident"], self.ln, parts=env["norm"].parts)

    def dve_open(self, dve):
        self.ln.dve_open(dve)
        self.sx.dve_open(dve)


def project(nc, out, sx, w_hi, w_lo, cols):
    terms = [t for k in range(KT) for t in sx.terms(w_hi[:, k, cols], w_lo[:, k, cols], k)[:PROJ_TERMS]]
    for n, (w, x) in enumerate(terms):
        last = nc.tensor.matmul(out, w, x, start=n == 0, stop=n == len(terms) - 1)
    return last


def project_tokens(nc, out, sx, w_hi, w_lo, cols, tile):
    at = slice(tile * P, (tile + 1) * P)
    terms = [t for k in range(KT) for t in sx.terms(w_hi[:, k, cols], w_lo[:, k, cols], k)[:PROJ_TERMS]]
    for n, (w, x) in enumerate(terms):
        last = nc.tensor.matmul(out, x[:, at], w, start=n == 0, stop=n == len(terms) - 1)
    return last


PROJ_TERMS = 3


def attention_phase(nc, env, io, following):
    X, PS, ident = env["X"], env["PS"], env["ident"]
    with ExitStack() as ctx:
        sb = lambda n, shape, dt=F32: ctx.enter_context(nc.sbuf_tensor(n, shape, dt))
        sem = lambda n: ctx.enter_context(nc.semaphore(n))
        sig = lambda n, per: Signal(nc, ctx, n, per)

        wqkv_hi = sb("wqkv_hi", [P, KT, WQK + HA * DA], F32R)
        wqkv_lo = sb("wqkv_lo", [P, KT, WQK + HA * DA], F32R)
        wo_hi, wo_lo = sb("wo_a_hi", [P, HA, M], F32R), sb("wo_a_lo", [P, HA, M], F32R)
        cos = sb("cos", [P, HA, T])
        sin = sb("sin", [P, T])
        mask_f = sb("mask_f", [P, P])
        mask_b = sb("mask_b", [P, P], BF16)
        ident_b = sb("ident_b", [P, P], BF16)
        NHALF = T // UN
        ln = Layernorm(nc, ctx, "a_ln", TB, X, env["norm"])
        sx = [SplitTransposed(nc, ctx, f"a{half}", PS[:, 2 * half:2 * half + 2, :], ident, ln, half,
                              parts=env["norm"].parts if half == 0 else None)
              for half in range(NHALF)]
        qk = sb("qk", [P, 2, HA, T])
        wqkv_raw = qk[:].rearrange("p s h t -> p (s h t)")[:, 0:KT * (WQK + HA * DA)].rearrange("p (k n) -> p k n", k=KT)
        swapped = sb("swapped", [P, NHALF * 2, UN])
        V = sb("v_a", [P, TB, HA * DA])

        steps = [(i, h) for i in range(TB) for h in range(HA)]
        NS = len(steps)
        prob = sb("prob", [P, 2, T])
        probT = sb("probT", [P, 2, TB, P])
        NO = 2
        oT_hi, oT_lo = sb("oT_hi", [P, NO, P], F32R), sb("oT_lo", [P, NO, P], F32R)
        wo_raw = prob[:, 0, 0:HA * M].rearrange("p (h m) -> p h m", h=HA)
        neg_max = sb("neg_max", [P, NS])
        row_sum = sb("row_sum", [P, NS])
        row_inv = sb("row_inv", [P, NS])

        groups = [(i + UT) // UT for i, _ in steps]
        first_group = [sum(groups[:n]) for n in range(NS + 1)]
        NG = first_group[NS]
        PROJ_RING = (0, 1, 4, 5)
        V_RING = (3, 1)
        NPROJ = NHALF * NQK

        const_loaded, w_loaded, x_loaded = sem("a_const_loaded"), sem("a_w_loaded"), sem("x_loaded")
        prep_hi, prep_done = sem("a_prep_hi"), sem("a_prep_done")
        proj_ready, cos_done, swap_done = (sig(f"a_{n}", NPROJ) for n in ("proj_ready", "cos_done", "swap_done"))
        sin_done = sig("a_sin_done", 2 * NHALF)
        rotated = sig("a_rotated", 2 * NHALF)
        v_ready, v_done = sig("a_v_ready", TB), sig("a_v_done", TB)
        s_ready, max_done, p_done = sig("s_ready", NS), sig("max_done", NS), sig("p_done", NS)
        inv_done = sig("inv_done", NS)
        pt_ready, pt_done = sig("pt_ready", NG), sig("pt_done", NG)
        o_ready, o_hi_done, o_lo_done = (sig(f"a_{n}", NS) for n in ("o_ready", "o_hi_done", "o_lo_done"))
        y_ready, y_done = sig("a_y_ready", NS), sig("a_y_done", NS)

        SPLIT_STEPS = (9, 10, 11)

        x_v = io["x"].rearrange("b (n p) m -> p (b n) m", p=P)
        N_CONST = 5
        passed = sem("sp_passed")

        def run_batches(eng, turn):
            turn(0, True, False)
            with eng.Fori(0, NB - 2) as p:
                turn(p + 1, False, False)
            turn(NB - 1, False, True)

        def score_rows(n):
            return PS[:, 2 * (n % 2):2 * (n % 2) + 2, :].rearrange("p a b -> p (a b)")[:, 0:(steps[n][0] + 1) * P]

        O, Y = PS[:, 6, 0:P], PS[:, 7, 0:M]

        with nc.Block() as block:

            @block.sync
            def _(sp):
                sp.dma_start(X[:, 0:TB, :], x_v[:, 0:TB, :]).then_inc(x_loaded, 16)
                sp.wait_ge(w_loaded, 16)
                sp.wait_ge(x_loaded, 16)
                with sp.Fori(0, NB - 1) as p:
                    at = bass.ds((p + 1) * TB, TB)
                    sp.dma_start(X[:, at, :], x_v[:, at, :]).then_inc(x_loaded, 16)
                    wait_alone(sp, x_loaded, (p + 2) * 16, passed)
                load_ff_weights(sp, env, io)

            @block.gpsimd
            def _(pool):
                open_signals(pool, rotated)
                ln.pool_open(pool)
                nc.gpsimd.memset(env["norm"].minus_half[:], -0.5).then_inc(env["norm_const"], 1)
                pool.wait_ge(env["norm_const"], 1)
                if following:
                    following.ln.pool_open(pool)

                def turn(b, first, last):
                    if last and following:
                        following.ln.pool_rstd(pool, 0)
                        pool.wait_ge(following.ln.rstd_done.sem, following.ln.rstd_done.at(0, 1))
                    for half in range(NHALF):
                        at = slice(half * UN, (half + 1) * UN)
                        for s in range(2):
                            pool.wait_ge(sin_done.sem, sin_done.at(b, 2 * half + s + 1))
                            for h in range(HA):
                                rows = slice(h * ROT, (h + 1) * ROT)
                                done = nc.gpsimd.tensor_tensor(qk[rows, s, h, at], qk[rows, s, h, at],
                                                               swapped[rows, 2 * half + s, :], ALU.add)
                            done.then_inc(rotated.sem, 1)
                    if not last:
                        pool.wait_ge(rotated.sem, rotated.at(b, 2 * NHALF))
                        ln.pool_rstd(pool, b + 1)
                    else:
                        pool.wait_ge(rotated.sem, rotated.at(b, 2 * NHALF))
                        pool.wait_ge(env["ff_loaded"], 16 * NPART)
                        nc.gpsimd.tensor_copy(env["ff_w_hi"][:], env["stage"][:, 0:NW].bitcast(I32)).then_inc(env["ff_high"], 1)

                ln.pool_rstd(pool, 0)
                run_batches(pool, turn)

            @block.scalar
            def _(act):
                for s in sx:
                    s.act_open(act)
                if following:
                    following.sx.act_open(act)
                open_signals(act, swap_done, v_done, p_done, pt_done, o_hi_done)
                act.dma_start(wqkv_raw, io["w_qkv"].rearrange("(k p) n -> p k n", p=P)).then_inc(w_loaded, 16)
                act.dma_start(ident[:], io["ident"]).then_inc(const_loaded, 16)
                act.dma_start(mask_f[:], io["causal"]).then_inc(const_loaded, 16)
                act.dma_start(cos[:], io["cos"]).then_inc(const_loaded, 16)
                act.dma_start(sin[:], io["sin"]).then_inc(const_loaded, 16)
                act.dma_start(wo_raw, io["wo_a"].rearrange("(h p) n -> p h n", p=P)).then_inc(const_loaded, 16)
                nq = WQK // 2
                act.wait_ge(w_loaded, 16)
                nc.scalar.activation(wqkv_hi[:, :, 0:nq], wqkv_raw[:, :, 0:nq], ACT.Copy, scale=QK_SCALE).then_inc(prep_hi, 1)
                nc.scalar.activation(wqkv_hi[:, :, nq:], wqkv_raw[:, :, nq:], ACT.Copy).then_inc(prep_hi, 1)
                act.wait_ge(const_loaded, 16 * N_CONST)
                nc.scalar.activation(wo_hi[:], wo_raw, ACT.Copy).then_inc(prep_hi, 1)

                def exp_step(b, n):
                    act.wait_ge(max_done.sem, max_done.at(b, n + 1))
                    act.wait_ge(pt_ready.sem, pt_ready.at(b, first_group[n - 1] if n >= 2 else
                                                          first_group[NS - 1 + n] - NG))
                    nc.scalar.activation(prob[:, n % 2, 0:(steps[n][0] + 1) * P], score_rows(n), ACT.Exp,
                                         bias=neg_max[:, n:n + 1], accum_out=row_sum[:, n:n + 1]).then_inc(p_done.sem, 1)

                def evacuate_probs(b, n):
                    i = steps[n][0]
                    act.wait_ge(o_ready.sem, o_ready.at(b, n - 1))
                    for g in range(groups[n]):
                        c = first_group[n] + g
                        js = slice(g * UT, min((g + 1) * UT, i + 1))
                        act.wait_ge(pt_ready.sem, pt_ready.at(b, c + 1))
                        nc.scalar.activation(probT[:, n % 2, js, :],
                                             PS[:, 4 + c % 2, 0:(js.stop - js.start) * P].rearrange("p (j q) -> p j q", q=P),
                                             ACT.Copy).then_inc(pt_done.sem, 1)

                def evacuate_out(b, n):
                    act.wait_ge(o_ready.sem, o_ready.at(b, n + 1))
                    act.wait_ge(y_ready.sem, y_ready.at(b, n - NO + 1))
                    nc.scalar.activation(oT_hi[:, n % NO, :], O, ACT.Copy).then_inc(o_hi_done.sem, 1)

                def swap_halves(b, m):
                    half, s, h = m // NQK, m % NQK // HA, m % HA
                    act.wait_ge(cos_done.sem, cos_done.at(b, m + 1))
                    act.wait_ge(rotated.sem, rotated.at(b, 2 * half + s - 3))
                    for r in range(2):
                        to, of = h * ROT + r * HALF, h * ROT + (1 - r) * HALF
                        last = nc.scalar.activation(swapped[to:to + HALF, 2 * half + s, :], PS[of:of + HALF, PROJ_RING[m % 4], :], ACT.Copy)
                    last.then_inc(swap_done.sem, 1)

                def values(b, t):
                    act.wait_ge(v_ready.sem, v_ready.at(b, t + 1))
                    nc.scalar.activation(V[:, t, :], PS[:, V_RING[t % 2], 0:HA * DA], ACT.Copy).then_inc(v_done.sem, 1)

                def turn(b, first, last):
                    for m in range(NPROJ - 1):
                        swap_halves(b, m)
                    values(b, 0)
                    swap_halves(b, NPROJ - 1)
                    values(b, 1)
                    exp_step(b, 0)
                    for n in range(NS):
                        if n + 1 < NS:
                            exp_step(b, n + 1)
                        if n == 0:
                            values(b, 2)
                        evacuate_probs(b, n)
                        if n + 3 < TB:
                            values(b, n + 3)
                        if n >= NS - NHALF and not last:
                            sx[n - (NS - NHALF)].act(act, b + 1)
                        if n == NS - 2 and last and following:
                            following.sx.act(act, 0)
                        if n > 0:
                            evacuate_out(b, n - 1)
                        if last and n in SPLIT_STEPS:
                            part = SPLIT_STEPS.index(n)
                            act.wait_ge(env["ff_low"], part + 1)
                            act.wait_ge(env["ff_squares"], part)
                            nc.scalar.activation(swapped[:].rearrange("p k t -> p (k t)")[:, 0:WPART],
                                                 env["stage"][:, part * WPART:(part + 1) * WPART], ACT.Square,
                                                 accum_out=env["low_squares"][:, part:part + 1]).then_inc(env["ff_squares"], 1)
                    evacuate_out(b, NS - 1)

                for s in sx:
                    s.act(act, 0)
                run_batches(act, turn)

            @block.vector
            def _(dve):
                for s in sx:
                    s.dve_open(dve)
                open_signals(dve, cos_done, sin_done, o_lo_done, max_done, inv_done, y_done)
                ln.dve_open(dve)
                if following:
                    following.dve_open(dve)

                def times_cos(b, m):
                    half, s, h = m // NQK, m % NQK // HA, m % HA
                    at = slice(half * UN, (half + 1) * UN)
                    dve.wait_ge(proj_ready.sem, proj_ready.at(b, m + 1))
                    nc.vector.tensor_tensor(qk[:, s, h, at], PS[:, PROJ_RING[m % 4], :], cos[:, h, at],
                                            ALU.mult).then_inc(cos_done.sem, 1)

                def times_sin(b, k):
                    half = k // 2
                    dve.wait_ge(swap_done.sem, swap_done.at(b, HA * (k + 1)))
                    nc.vector.tensor_tensor(swapped[:, k, :], swapped[:, k, :], sin[:, half * UN:(half + 1) * UN],
                                            ALU.mult).then_inc(sin_done.sem, 1)

                def out_low(b, n):
                    dve.wait_ge(o_hi_done.sem, o_hi_done.at(b, n + 1))
                    nc.vector.tensor_tensor(oT_lo[:, n % NO, :], O, oT_hi[:, n % NO, :].bitcast(F32),
                                            ALU.subtract).then_inc(o_lo_done.sem, 1)

                def row_max(b, n):
                    dve.wait_ge(s_ready.sem, s_ready.at(b, n + 1))
                    nc.vector.tensor_reduce(neg_max[:, n:n + 1], score_rows(n), AX.X, ALU.max,
                                            negate=True).then_inc(max_done.sem, 1)

                def inverse(b, n):
                    dve.wait_ge(p_done.sem, p_done.at(b, n + 1))
                    nc.vector.reciprocal(row_inv[:, n:n + 1], row_sum[:, n:n + 1]).then_inc(inv_done.sem, 1)

                def residual(b, n):
                    dve.wait_ge(y_ready.sem, y_ready.at(b, n + 1))
                    dve.wait_ge(inv_done.sem, inv_done.at(b, n + 1))
                    dve.wait_ge(y_done.sem, y_done.at(b, n))
                    x = X[:, bass.ds(b * TB + (steps[n][0] if n >= 0 else steps[n][0] - TB), 1), :].rearrange("p a m -> p (a m)")
                    nc.vector.scalar_tensor_tensor(x, Y, row_inv[:, n % NS:n % NS + 1], x,
                                                   ALU.mult, ALU.add).then_inc(y_done.sem, 1)

                def turn(b, first, last):
                    if last and following:
                        following.ln.dve_stats(dve, 0)
                    for m in range(NPROJ):
                        times_cos(b, m)
                        if m == 1 and not first:
                            residual(b, -1)
                        if m % HA == 0 and m > 0:
                            times_sin(b, m // HA - 1)
                    row_max(b, 0)
                    row_max(b, 1)
                    times_sin(b, NPROJ // HA - 1)
                    for n in range(NS):
                        inverse(b, n)
                        if n + 2 < NS:
                            row_max(b, n + 2)
                        elif not last:
                            sx[n + 2 - NS].dve(dve, b + 1)
                        elif n + 2 == NS and following:
                            following.sx.dve(dve, 0)
                        if n >= 1:
                            out_low(b, n - 1)
                        if n >= 2:
                            residual(b, n - 2)
                        if not last:
                            if n in (4, 6):
                                dve.wait_ge(x_loaded, (b + 2) * 16)
                                ln.dve_tile_stats(dve, b + 1, range(0, UT) if n == 4 else range(UT, TB))
                            if n == 6:
                                ln.dve_aggregate(dve, b + 1)
                            if n in (9, 11):
                                ln.dve_normalise(dve, b + 1, range(0, UT) if n == 9 else range(UT, TB))
                        if n == 7 and last and following:
                            following.ln.dve_normalise(dve, 0)
                        if n in SPLIT_STEPS and last:
                            part = SPLIT_STEPS.index(n)
                            raw = env["stage"][:, part * WPART:(part + 1) * WPART]
                            dve.wait_ge(env["ff_high"], 1)
                            nc.vector.tensor_tensor(raw, raw.bitcast(I32),
                                                    env["ff_w_hi"][:, part * WPART:(part + 1) * WPART].bitcast(F32),
                                                    ALU.subtract).then_inc(env["ff_low"], 1)
                    out_low(b, NS - 1)
                    residual(b, NS - 2)
                    if last:
                        dve.wait_ge(env["low_transposed"], 1)
                        nc.vector.tensor_reduce(env["low_any"][:], PS[0:1, 4, 0:NPART * P], AX.X,
                                                ALU.max).then_inc(env["low_done"], 1)
                        residual(b, NS - 1)

                dve.wait_ge(x_loaded, 16)
                ln.dve_stats(dve, 0)
                ln.dve_normalise(dve, 0)
                nq = WQK // 2
                dve.wait_ge(prep_hi, 2)
                nc.vector.scalar_tensor_tensor(wqkv_lo[:, :, 0:nq], wqkv_raw[:, :, 0:nq], QK_SCALE,
                                               wqkv_hi[:, :, 0:nq].bitcast(F32), ALU.mult, ALU.subtract).then_inc(prep_done, 1)
                nc.vector.tensor_tensor(wqkv_lo[:, :, nq:], wqkv_raw[:, :, nq:], wqkv_hi[:, :, nq:].bitcast(F32),
                                        ALU.subtract).then_inc(prep_done, 1)
                dve.wait_ge(const_loaded, 16 * N_CONST)
                dve.wait_ge(prep_hi, 3)
                nc.vector.tensor_tensor(wo_lo[:], wo_raw, wo_hi[:].bitcast(F32), ALU.subtract).then_inc(prep_done, 1)
                nc.vector.tensor_copy(ident_b[:], ident[:]).then_inc(prep_done, 1)
                nc.vector.tensor_copy(mask_b[:], mask_f[:]).then_inc(prep_done, 1)
                for s in sx:
                    s.dve(dve, 0)
                run_batches(dve, turn)

            @block.tensor
            def _(pe):
                for s in sx:
                    s.pe_open(pe)
                if following:
                    following.sx.pe_open(pe)
                open_signals(pe, proj_ready, v_ready, s_ready, pt_ready, o_ready, y_ready)

                def scores(b, n):
                    i, h = steps[n]
                    if n >= 2:
                        pe.wait_ge(p_done.sem, p_done.at(b, n - 1))
                    if i % UT == 0 and h == 0:
                        pe.wait_ge(rotated.sem, rotated.at(b, 2 * (i // UT + 1)))
                    keys = (i + 1) * P
                    for c in range(0, keys, UN):
                        w = min(UN, keys - c)
                        diag = c + w == keys
                        bank = PS[:, 2 * (n % 2) + c // UN, :]
                        last = nc.tensor.matmul(bank[:, 0:w], qk[:, 0, h, i * P:(i + 1) * P], qk[:, 1, h, c:c + w],
                                                start=True, stop=not diag)
                        if diag:
                            last = nc.tensor.matmul(bank[:, w - P:w], ident_b[:], mask_b[:], start=False, stop=True)
                    last.then_inc(s_ready.sem, 1)

                def values(b, t):
                    pe.wait_ge(v_done.sem, v_done.at(b, t - 1))
                    project_tokens(nc, PS[:, V_RING[t % 2], 0:HA * DA], sx[t // UT], wqkv_hi, wqkv_lo,
                                   slice(WQK, WQK + HA * DA), t % UT).then_inc(v_ready.sem, 1)

                def transpose_probs(b, n):
                    i = steps[n][0]
                    pe.wait_ge(p_done.sem, p_done.at(b, n + 1))
                    for g in range(groups[n]):
                        c = first_group[n] + g
                        pe.wait_ge(pt_done.sem, pt_done.at(b, c - 1))
                        for j in range(g * UT, min((g + 1) * UT, i + 1)):
                            last = nc.tensor.transpose(PS[:, 4 + c % 2, (j % UT) * P:(j % UT + 1) * P],
                                                       prob[:, n % 2, j * P:(j + 1) * P], ident[:])
                        last.then_inc(pt_ready.sem, 1)

                def weighted_values(b, n):
                    i, h = steps[n]
                    pe.wait_ge(pt_done.sem, pt_done.at(b, first_group[n + 1]))
                    pe.wait_ge(v_done.sem, v_done.at(b, i + 1))
                    pe.wait_ge(o_lo_done.sem, o_lo_done.at(b, n))
                    for j in range(i + 1):
                        last = nc.tensor.matmul(O, V[:, j, h * DA:(h + 1) * DA], probT[:, n % 2, j, :],
                                                start=j == 0, stop=j == i)
                    last.then_inc(o_ready.sem, 1)

                def out_projection(b, n):
                    pe.wait_ge(o_lo_done.sem, o_lo_done.at(b, n + 1))
                    pe.wait_ge(y_done.sem, y_done.at(b, n))
                    parts = ((oT_hi, wo_hi), (oT_hi, wo_lo), (oT_lo, wo_hi))
                    for k, (o, w) in enumerate(parts):
                        last = nc.tensor.matmul(Y, o[:, n % NO, :], w[:, steps[n][1], :], start=k == 0, stop=k == len(parts) - 1)
                    last.then_inc(y_ready.sem, 1)

                def turn(b, first, last):
                    pe.wait_ge(pt_done.sem, pt_done.at(b, 0))
                    for half in range(NHALF):
                        sx[half].pe_wait(pe, b)
                        for j in range(NQK):
                            m = NQK * half + j
                            if m >= 4:
                                pe.wait_ge(swap_done.sem, swap_done.at(b, m - 3))
                            project(nc, PS[:, PROJ_RING[m % 4], :], sx[half], wqkv_hi, wqkv_lo,
                                    slice(j * P, (j + 1) * P)).then_inc(proj_ready.sem, 1)
                            if m == 0 and not first:
                                out_projection(b, -1)
                    values(b, 0)
                    pe.wait_ge(swap_done.sem, swap_done.at(b, NPROJ - 2))
                    values(b, 1)
                    scores(b, 0)
                    scores(b, 1)
                    values(b, 2)
                    pe.wait_ge(swap_done.sem, swap_done.at(b, NPROJ))
                    for n in range(NS):
                        transpose_probs(b, n)
                        if n + 2 == HA * UT:
                            pe.wait_ge(v_done.sem, v_done.at(b, TB))
                        if n + 2 < NS:
                            scores(b, n + 2)
                        if n + 3 < TB:
                            values(b, n + 3)
                        if n + 2 >= NS and not last:
                            sx[n + 2 - NS].pe(pe, b + 1, b + 1)
                        if n + 2 == NS and last and following:
                            following.sx.pe(pe, 0, 0)
                        if n >= 1:
                            weighted_values(b, n - 1)
                        if n >= 2:
                            out_projection(b, n - 2)
                    weighted_values(b, NS - 1)
                    out_projection(b, NS - 2)
                    if last:
                        pe.wait_ge(env["ff_squares"], NPART)
                        for part in range(NPART):
                            ins = nc.tensor.transpose(PS[0:1, 4, part * P:(part + 1) * P],
                                                      env["low_squares"][:, part:part + 1], ident[:])
                        ins.then_inc(env["low_transposed"], 1)
                        out_projection(b, NS - 1)

                pe.wait_ge(const_loaded, 16 * N_CONST)
                for s in sx:
                    s.pe(pe, 0, 0)
                pe.wait_ge(prep_done, 5)
                run_batches(pe, turn)


def load_ff_weights(eng, env, io):
    stage = env["stage"].bitcast(I32)
    for n, name in enumerate(("w_gate", "w_up")):
        eng.dma_start(stage[:, n * KT * FF:(n + 1) * KT * FF].rearrange("p (k f) -> p k f", k=KT),
                      io[name].rearrange("(k p) f -> p k f", p=P)).then_inc(env["ff_loaded"], 16)
    eng.dma_start(stage[:, 2 * KT * FF:2 * KT * FF + NF * M].rearrange("p (k m) -> p k m", k=NF),
                  io["w_down"].rearrange("(k p) m -> p k m", p=P)).then_inc(env["ff_loaded"], 16)


LB_COLS = 4 * HD
STAGE = KT * LB_COLS + NP * M


def load_lin_weights(eng, env, io):
    stage = env["stage"]
    eng.dma_start(stage[:, 0:KT * LB_COLS].rearrange("p (k n) -> p k n", k=KT),
                  io["w_lin"].rearrange("(k p) n -> p k n", p=P)).then_inc(env["lin_loaded"], 16)
    eng.dma_start(stage[:, KT * LB_COLS:KT * LB_COLS + NP * M].rearrange("p (k m) -> p k m", k=NP),
                  io["w_o"].rearrange("(k p) m -> p k m", p=P)).then_inc(env["lin_loaded"], 16)


def feed_forward_phase(nc, env, io, name, nth, front, following):
    X, PS, ident, stage = env["X"], env["PS"], env["ident"], env["stage"]
    with ExitStack() as ctx:
        sb = lambda n, shape, dt=F32: ctx.enter_context(nc.sbuf_tensor(f"{name}_{n}", shape, dt))
        sem = lambda n: ctx.enter_context(nc.semaphore(f"{name}_{n}"))
        sig = lambda n, per: Signal(nc, ctx, f"{name}_{n}", per)

        parts_of_w = [slice(0, KT * FF), slice(KT * FF, 2 * KT * FF), slice(2 * KT * FF, NW)]
        split_before = nth == 1
        w_hi = env["ff_w_hi"] if split_before else sb("w_hi", [P, NW], F32R)
        w_lo = sb("w_lo", [P, NW], F32R)
        gu = lambda w, n: w[:, parts_of_w[n]].rearrange("p (k f) -> p k f", k=KT)
        gate_hi, up_hi, gate_lo, up_lo = gu(w_hi, 0), gu(w_hi, 1), gu(w_lo, 0), gu(w_lo, 1)
        down_hi, down_lo = (w[:, parts_of_w[2]].rearrange("p (k m) -> p k m", k=NF) for w in (w_hi, w_lo))
        ln = front.ln
        sx = [front.sx, SplitTransposed(nc, ctx, f"{name}_odd", PS[:, 0:2, :], ident, ln)]
        silu = sb("silu", [P, 2, UN])
        h = sb("h", [P, 2, UN])
        NH = 3
        h_hi, h_lo = sb("h_hi", [P, NH, UN], F32R), sb("h_lo", [P, NH, UN], F32R)
        LAG = 2

        prep_hi, prep_lo = sem("prep_hi"), sem("prep_lo")
        gate_ready, up_ready = sig("gate_ready", NF), sig("up_ready", NF)
        silu_done, h_done = sig("silu_done", NF), sig("h_done", NF)
        hi_done, lo_done, down_done = sig("h_hi_done", NF), sig("h_lo_done", NF), sig("down_done", NF)
        x_done = sig("x_done", 1)
        stored = sem("stored")
        Y = PS[:, 6:8, :]
        out_v = io["out"].rearrange("b (n p) m -> p (b n) m", p=P)

        def run_units(eng, unit):
            unit(0, 0, 0, True, False)
            with eng.Fori(0, NU // 2 - 1) as p:
                unit(p * 2 + 1, 1, p, False, False)
                unit(p * 2 + 2, 0, p + 1, False, False)
            unit(NU - 1, 1, NU // 2 - 1, False, True)

        def next_of(u, par, turn, last):
            if not last:
                return ln, u + 1, sx[1 - par], turn + par
            return (following.ln, 0, following.sx, 0) if following else None

        with nc.Block() as block:

            @block.sync
            def _(sp):
                if not following:
                    with sp.Fori(0, NU) as u:
                        sp.wait_ge(x_done.sem, x_done.at(u, 1))
                        at = bass.ds(u * UT, UT)
                        sp.dma_start(out_v[:, at, :], X[:, at, :]).then_inc(stored, 16)
                    sp.wait_ge(stored, 16 * NU)
                else:
                    sp.wait_ge(prep_lo, NPART)
                    load_lin_weights(sp, env, io)

            @block.gpsimd
            def _(pool):
                with pool.Fori(0, NU - 1) as u:
                    ln.pool_rstd(pool, u + 1)
                if following:
                    following.ln.pool_open(pool)
                    following.ln.pool_rstd(pool, 0)

            @block.scalar
            def _(act):
                sx[1].act_open(act)
                if following:
                    following.sx.act_open(act)
                open_signals(act, silu_done, hi_done)
                for at in parts_of_w:
                    if split_before:
                        nc.scalar.activation(w_lo[:, at], stage[:, at], ACT.Copy).then_inc(prep_lo, 1)
                    else:
                        act.wait_ge(env["ff_loaded"], 16 * NPART * nth)
                        nc.scalar.activation(w_hi[:, at], stage[:, at].bitcast(I32), ACT.Copy).then_inc(prep_hi, 1)

                def high_part(u, f):
                    act.wait_ge(h_done.sem, h_done.at(u, f + 1))
                    act.wait_ge(down_done.sem, down_done.at(u, f - NH + 1))
                    nc.scalar.activation(h_hi[:, f % NH, :], h[:, f % 2, :], ACT.Copy).then_inc(hi_done.sem, 1)

                def unit(u, par, turn, first, last):
                    upcoming = next_of(u, par, turn, last)
                    for f in range(NF):
                        act.wait_ge(gate_ready.sem, gate_ready.at(u, f + 1))
                        act.wait_ge(h_done.sem, h_done.at(u, f - 1))
                        nc.scalar.activation(silu[:, f % 2, :], PS[:, 2 + f % 2, :], ACT.Silu,
                                             scale=W_SCALE).then_inc(silu_done.sem, 1)
                        if f > 0 or not first:
                            high_part(u, f - 1)
                        if f == NF - 2 and upcoming:
                            _, _, nsx, nturn = upcoming
                            nsx.act(act, nturn)
                    if last:
                        high_part(u, NF - 1)

                run_units(act, unit)

            @block.vector
            def _(dve):
                sx[1].dve_open(dve)
                open_signals(dve, h_done, lo_done, x_done)
                if following:
                    following.dve_open(dve)
                if not split_before:
                    for n, at in enumerate(parts_of_w):
                        dve.wait_ge(prep_hi, n + 1)
                        nc.vector.tensor_tensor(w_lo[:, at], stage[:, at].bitcast(I32), w_hi[:, at].bitcast(F32),
                                                ALU.subtract).then_inc(prep_lo, 1)

                def low_part(u, f):
                    dve.wait_ge(hi_done.sem, hi_done.at(u, f + 1))
                    dve.wait_ge(down_done.sem, down_done.at(u, f - NH + 1))
                    nc.vector.tensor_tensor(h_lo[:, f % NH, :], h[:, f % 2, :], h_hi[:, f % NH, :].bitcast(F32),
                                            ALU.subtract).then_inc(lo_done.sem, 1)

                def residual(u, done):
                    dve.wait_ge(down_done.sem, done)
                    x = X[:, bass.ds(u * UT, UT), :].rearrange("p a m -> p (a m)")
                    nc.vector.scalar_tensor_tensor(x, Y.rearrange("p a b -> p (a b)"), W_SCALE, x,
                                                   ALU.mult, ALU.add).then_inc(x_done.sem, 1)

                def unit(u, par, turn, first, last):
                    upcoming = next_of(u, par, turn, last)
                    if upcoming:
                        nln, nln_turn, nsx, nturn = upcoming
                    for f in range(NF):
                        if f == NF - 1 and upcoming:
                            nsx.dve(dve, nturn)
                        dve.wait_ge(up_ready.sem, up_ready.at(u, f + 1))
                        dve.wait_ge(silu_done.sem, silu_done.at(u, f + 1))
                        dve.wait_ge(lo_done.sem, lo_done.at(u, f - 1))
                        nc.vector.scalar_tensor_tensor(h[:, f % 2, :], PS[:, 4 + f % 2, :], W_SCALE, silu[:, f % 2, :],
                                                       ALU.mult, ALU.mult).then_inc(h_done.sem, 1)
                        if f == 3 and upcoming:
                            nln.dve_normalise(dve, nln_turn)
                        if f > 0 or not first:
                            low_part(u, f - 1)
                        if f == LAG - 1 and not first:
                            residual(u - 1, down_done.at(u, 0))
                        if upcoming:
                            if f == 0:
                                nln.dve_tile_stats(dve, nln_turn, range(0, UT // 2))
                            if f == 2:
                                nln.dve_tile_stats(dve, nln_turn, range(UT // 2, UT))
                                nln.dve_aggregate(dve, nln_turn)
                    if last:
                        low_part(u, NF - 1)
                        residual(u, down_done.at(u, NF))

                run_units(dve, unit)

            @block.tensor
            def _(pe):
                sx[1].pe_open(pe)
                if following:
                    following.sx.pe_open(pe)
                open_signals(pe, gate_ready, up_ready, down_done)
                pe.wait_ge(env["low_done"], 1)
                wide = pe.value_load(env["low_any"][:].bitcast(I32))

                def wait_weights(parts):
                    if not split_before:
                        pe.wait_ge(prep_hi, parts)

                def gate_or_up(sxu, bank, hi, lo, f, terms, done):
                    at = slice(f * P, (f + 1) * P)
                    parts = [p for k in range(KT) for p in sxu.terms(hi[:, k, at], lo[:, k, at], k)[:terms]]
                    for n, (w, x) in enumerate(parts):
                        ins = nc.tensor.matmul(PS[:, bank, :], w, x, start=n == 0, stop=n == len(parts) - 1)
                    ins.then_inc(done.sem, 1)

                def down(u, f, terms):
                    pe.wait_ge(hi_done.sem, hi_done.at(u, f + 1))
                    pe.wait_ge(lo_done.sem, lo_done.at(u, f + 1))
                    parts = [(a, w) for w in ((down_hi,) if terms == 2 else (down_hi, down_lo)) for a in (h_hi, h_lo)]
                    for t in range(UT):
                        for n, (a, w) in enumerate(parts):
                            ins = nc.tensor.matmul(Y[:, t // 2, (t % 2) * M:(t % 2 + 1) * M],
                                                   a[:, f % NH, t * P:(t + 1) * P], w[:, f % NF, :],
                                                   start=f == 0 and n == 0 and t % 2 == 0,
                                                   stop=f % NF == NF - 1 and n == len(parts) - 1, skip_group_check=True)
                    ins.then_inc(down_done.sem, 1)

                def units(terms):
                    def unit(u, par, turn, first, last):
                        sx[par].pe_wait(pe, turn)
                        upcoming = next_of(u, par, turn, last)
                        for f in range(NF):
                            if first and f == 0:
                                wait_weights(1)
                            if first and f == LAG:
                                wait_weights(NPART)
                            pe.wait_ge(silu_done.sem, silu_done.at(u, f - 1))
                            gate_or_up(sx[par], 2 + f % 2, gate_hi, gate_lo, f, terms, gate_ready)
                            pe.wait_ge(h_done.sem, h_done.at(u, f - 1))
                            if first and f == 0:
                                wait_weights(2)
                            gate_or_up(sx[par], 4 + f % 2, up_hi, up_lo, f, terms, up_ready)
                            if f == NF - 2 and upcoming:
                                _, nln_turn, nsx, nturn = upcoming
                                nsx.pe(pe, nturn, nln_turn)
                            if f == LAG:
                                pe.wait_ge(x_done.sem, x_done.at(u, 0))
                            if f >= LAG or not first:
                                down(u, f - LAG, terms)
                        if last:
                            for f in range(NF - LAG, NF):
                                down(u, f, terms)

                    run_units(pe, unit)

                with pe.If(wide == 0):
                    units(2)
                with pe.If(wide != 0):
                    pe.wait_ge(prep_lo, NPART)
                    units(4)


def linear_attention_phase(nc, env, io, front, following):
    X, PS, ident, stage = env["X"], env["PS"], env["ident"], env["stage"]
    with ExitStack() as ctx:
        sb = lambda n, shape, dt=F32: ctx.enter_context(nc.sbuf_tensor(f"lin_{n}", shape, dt))
        sem = lambda n: ctx.enter_context(nc.semaphore(f"lin_{n}"))
        sig = lambda n, per: Signal(nc, ctx, f"lin_{n}", per)

        NHALF = T // UN
        w_hi, w_lo = sb("w_hi", [P, KT, LB_COLS], F32R), sb("w_lo", [P, KT, LB_COLS], F32R)
        w_o_hi, w_o_lo = sb("w_o_hi", [P, NP, M], F32R), sb("w_o_lo", [P, NP, M], F32R)
        bias = sb("bias", [P, NP])
        decay_in = sb("decay_in", [P, HB + NP])
        log_g = sb("log_g", [P, HB + NP])
        tmp_a, tmp_b = sb("tmp_a", [P, HB + NP]), sb("tmp_b", [P, HB + NP])
        rev = sb("rev", [P, 1])
        D = sb("decay", [P, HB, P])
        Gq = sb("decay_q", [P, NP, P])
        Gk = sb("decay_k", [P, HB])
        Gc = sb("decay_c", [P, NP])

        ln, sx = front.ln, front.sx
        e = env["norm"].xn[:, UT:TB, :].rearrange("p t m -> p (t m)").rearrange("p (r n) -> p r n", r=2)
        qT, kT, qsT, gate = (sb(n, [P, NP, UN]) for n in ("qT", "kT", "qsT", "gate"))
        v = sb("v", [P, UT, HB, VA])
        AD = sb("AD", [P, 2, 2, NP, P])
        dist = AD[:, 0, 0, 0:3, :]
        ks = sb("ks", [P, HB, DK])
        S = sb("state", [P, NP, 2 * VA])
        den, inv = sb("den", [P, 2, HG]), sb("inv", [P, 2, HG])
        y = sb("y", [P, 2, HD])
        yg = stage[:, STAGE - NP * P:STAGE].rearrange("p (j t) -> p j t", j=NP)
        yg_hi, yg_lo = sb("yg_hi", [P, NP, P], F32R), sb("yg_lo", [P, NP, P], F32R)

        NC = TB
        RING = (5, 2, 3, 4)
        ST_BANK = (5, 4)
        NITEM = 3 * NP + UT

        const_loaded = sem("const_loaded")
        prep_hi, prep_lo, prep_wo = sem("prep_hi"), sem("prep_lo"), sem("prep_wo")
        prep, prep_act, zeroed = sem("prep"), sem("prep_act"), sem("zeroed")
        proj_ready = sig("proj_ready", NHALF * NITEM)
        relu_done, exp_done, phi_done = (sig(n, NHALF * 2 * NP) for n in ("relu_done", "exp_done", "phi_done"))
        qs_done = sig("qs_done", NHALF * NP)
        gate_done, v_done = sig("gate_done", NHALF * NP), sig("v_done", NC)
        kt_ready, ks_done = sig("kt_ready", NC), sig("ks_done", NC)
        a_ready, ad_done = sig("a_ready", 2 * NC), sig("ad_done", 2 * NC)
        o_ready, den_done, inv_done, y_done = (sig(n, 2 * NC) for n in ("o_ready", "den_done", "inv_done", "y_done"))
        st_ready, s_done = sig("st_ready", 2 * NC), sig("s_done", 2 * NC)
        yt_ready, yg_done, yg_hi_done, yg_lo_done = (sig(n, NC) for n in ("yt_ready", "yg_done", "yg_hi_done", "yg_lo_done"))
        out_ready, x_done = sig("out_ready", NC), sig("x_done", NC)

        def next_of(b, half, last):
            if not (last and half == NHALF - 1):
                return ln, sx, b * NHALF + half + 1
            return (following.ln, following.sx, 0) if following else None

        raw = stage[:, 0:KT * LB_COLS].rearrange("p (k n) -> p k n", k=KT)
        qk_cols = lambda w, j: w[:, :, 0:2 * HD].rearrange("p k (s j c) -> p k s j c", s=2, j=NP)[:, :, :, j, :]
        w_second = slice(2 * HD, LB_COLS)
        w_o_raw = stage[:, KT * LB_COLS:KT * LB_COLS + NP * M].rearrange("p (k m) -> p k m", k=NP)

        def key_bank(ch):
            return (6, 7, 7, 4)[ch % UT]

        def run_batches(eng, turn):
            turn(0, True, False)
            with eng.Fori(0, NB - 2) as p:
                turn(p + 1, False, False)
            turn(NB - 1, False, True)

        with nc.Block() as block:

            @block.sync
            def _(sp):
                sp.dma_start(bias[:], io["b_g"]).then_inc(const_loaded, 16)
                sp.dma_start(decay_in[:], io["decay"]).then_inc(const_loaded, 16)
                sp.dma_start(dist, io["dist"]).then_inc(const_loaded, 16)
                sp.dma_start(rev[:], io["rev"]).then_inc(const_loaded, 16)
                sp.wait_ge(prep_lo, NP)
                sp.wait_ge(prep_wo, 2)
                load_ff_weights(sp, env, io)

            @block.gpsimd
            def _(pool):
                open_signals(pool, qs_done, yg_lo_done)
                if following:
                    following.ln.pool_open(pool)

                def turn(b, first, last):
                    for half in range(NHALF):
                        if half > 0 or not first:
                            gated_low(b, UT * half - 1)
                        for j in range(NP):
                            pool.wait_ge(phi_done.sem, phi_done.at(b, 2 * NP * half + 2 * j + 1))
                            nc.gpsimd.tensor_tensor(qsT[:, j, :].rearrange("p (c t) -> p c t", t=P),
                                                    qT[:, j, :].rearrange("p (c t) -> p c t", t=P),
                                                    Gq[:, j, :].unsqueeze(1).to_broadcast([P, UT, P]),
                                                    ALU.mult).then_inc(qs_done.sem, 1)
                        upcoming = next_of(b, half, last)
                        if upcoming:
                            upcoming[0].pool_rstd(pool, upcoming[2])
                        for c in range(UT - 1):
                            gated_low(b, UT * half + c)
                    if last:
                        gated_low(b, TB - 1)

                nc.gpsimd.memset(S[:], 0.0).then_inc(zeroed, 1)
                nc.gpsimd.memset(v[:], 1.0).then_inc(zeroed, 1)
                pool.wait_ge(prep_hi, NP + 1)
                nc.gpsimd.tensor_tensor(w_lo[:, :, w_second], raw[:, :, w_second], w_hi[:, :, w_second].bitcast(F32),
                                        ALU.subtract).then_inc(prep_wo, 1)
                pool.wait_ge(prep_hi, NP + 2)
                nc.gpsimd.tensor_tensor(w_o_lo[:], w_o_raw, w_o_hi[:].bitcast(F32), ALU.subtract).then_inc(prep_wo, 1)

                def gated_low(b, ch):
                    pool.wait_ge(yg_hi_done.sem, yg_hi_done.at(b, ch + 1))
                    pool.wait_ge(out_ready.sem, out_ready.at(b, ch))
                    nc.gpsimd.tensor_tensor(yg_lo[:], yg, yg_hi[:].bitcast(F32),
                                            ALU.subtract).then_inc(yg_lo_done.sem, 1)
                pool.wait_ge(prep_act, 4)
                run_batches(pool, turn)

            @block.scalar
            def _(act):
                if following:
                    following.sx.act_open(act)
                open_signals(act, relu_done, exp_done, gate_done, v_done, yg_hi_done)
                act.wait_ge(env["lin_loaded"], 32)
                for j in range(NP):
                    nc.scalar.activation(qk_cols(w_hi, j), qk_cols(raw, j), ACT.Copy).then_inc(prep_hi, 1)
                nc.scalar.activation(w_hi[:, :, w_second], raw[:, :, w_second], ACT.Copy).then_inc(prep_hi, 1)
                nc.scalar.activation(w_o_hi[:], w_o_raw, ACT.Copy).then_inc(prep_hi, 1)
                act.wait_ge(prep, 2)
                nc.scalar.activation(tmp_b[:], tmp_a[:], ACT.Exp, scale=-1.0).then_inc(prep_act, 1)
                act.wait_ge(prep_act, 1)
                nc.scalar.activation(tmp_a[:], tmp_b[:], ACT.Ln, bias=1.0).then_inc(prep_act, 1)
                act.wait_ge(prep, 5)
                for hd in range(HB):
                    nc.scalar.activation(D[:, hd, :], dist[:, 0, :], ACT.Exp, scale=log_g[:, hd:hd + 1])
                for j in range(NP):
                    nc.scalar.activation(Gq[:, j, :], dist[:, 2, :], ACT.Exp, scale=log_g[:, HB + j:HB + j + 1])
                nc.scalar.activation(Gc[:], log_g[:, HB:], ACT.Exp, scale=float(P)).then_inc(prep_act, 1)
                nc.scalar.activation(Gk[:], tmp_b[:, 0:HB], ACT.Exp).then_inc(prep_act, 1)
                nc.scalar.mul(bias[:], bias[:], 0.5).then_inc(prep_act, 1)
                act.wait_ge(prep_act, 5)
                act.wait_ge(zeroed, 2)

                def gated_high(b, ch):
                    act.wait_ge(yg_done.sem, yg_done.at(b, ch + 1))
                    act.wait_ge(out_ready.sem, out_ready.at(b, ch))
                    nc.scalar.activation(yg_hi[:], yg, ACT.Copy).then_inc(yg_hi_done.sem, 1)

                def turn(b, first, last):
                    for half in range(NHALF):
                        for it in range(NITEM):
                            if it == 2 and (half > 0 or not first):
                                gated_high(b, UT * half - 1)
                            m = NITEM * half + it
                            src = PS[:, RING[m % 4], :]
                            act.wait_ge(proj_ready.sem, proj_ready.at(b, m + 1))
                            if it < 2 * NP:
                                n = 2 * NP * half + it
                                act.wait_ge(phi_done.sem, phi_done.at(b, n - 1))
                                nc.scalar.activation(e[:, it % 2, :], src, ACT.Relu, scale=-1.0).then_inc(relu_done.sem, 1)
                                act.wait_ge(relu_done.sem, relu_done.at(b, n + 1))
                                nc.scalar.activation(e[:, it % 2, :], e[:, it % 2, :], ACT.Exp,
                                                     scale=-1.0).then_inc(exp_done.sem, 1)
                            elif it < 3 * NP:
                                j = it - 2 * NP
                                nc.scalar.activation(gate[:, j, :], src, ACT.Tanh, bias=bias[:, j:j + 1],
                                                     scale=0.5).then_inc(gate_done.sem, 1)
                            else:
                                t = it - 3 * NP
                                nc.scalar.activation(v[:, t, :, 0:DK], src.rearrange("p (h d) -> p h d", d=DK),
                                                     ACT.Copy).then_inc(v_done.sem, 1)
                        for c in range(UT - 1):
                            upcoming = next_of(b, half, last)
                            if c == UT - 2 and upcoming:
                                upcoming[1].act(act, upcoming[2])
                            gated_high(b, UT * half + c)
                    if last:
                        gated_high(b, TB - 1)

                run_batches(act, turn)

            @block.vector
            def _(dve):
                if following:
                    following.dve_open(dve)
                open_signals(dve, phi_done, ks_done, ad_done, den_done, inv_done, y_done, s_done, yg_done, x_done)
                dve.wait_ge(const_loaded, 64)
                nc.vector.tensor_scalar(log_g[:], decay_in[:], 0.0, None, ALU.min).then_inc(prep, 1)
                nc.vector.scalar_tensor_tensor(tmp_a[:], decay_in[:], -1.0, decay_in[:], ALU.mult, ALU.max).then_inc(prep, 1)
                for j in range(NP):
                    dve.wait_ge(prep_hi, j + 1)
                    nc.vector.tensor_tensor(qk_cols(w_lo, j), qk_cols(raw, j), qk_cols(w_hi, j).bitcast(F32),
                                            ALU.subtract).then_inc(prep_lo, 1)
                dve.wait_ge(prep_act, 2)
                nc.vector.tensor_tensor(log_g[:], log_g[:], tmp_a[:], ALU.subtract).then_inc(prep, 1)
                dve.wait_ge(prep, 3)
                nc.vector.tensor_scalar(log_g[:], log_g[:], -200.0, None, ALU.max).then_inc(prep, 1)
                dve.wait_ge(prep, 4)
                nc.vector.tensor_scalar(tmp_b[:], log_g[:], rev[:], None, ALU.mult).then_inc(prep, 1)
                dve.wait_ge(prep_act, 4)
                nc.vector.tensor_tensor(D[:], D[:], dist[:, 1, :].unsqueeze(1).to_broadcast([P, HB, P]),
                                        ALU.mult).then_inc(prep, 1)
                dve.wait_ge(prep, 6)
                dve.wait_ge(zeroed, 2)

                def phi_item(b, half, it):
                    n = 2 * NP * half + it
                    m = NITEM * half + it
                    dve.wait_ge(exp_done.sem, exp_done.at(b, n + 1))
                    dst = (qT, kT)[it % 2]
                    nc.vector.scalar_tensor_tensor(dst[:, it // 2, :], PS[:, RING[m % 4], :], 1.0, e[:, it % 2, :],
                                                   ALU.add, ALU.max).then_inc(phi_done.sem, 1)

                def scaled_keys(b, c):
                    dve.wait_ge(kt_ready.sem, kt_ready.at(b, c + 1))
                    nc.vector.tensor_tensor(ks[:], PS[:, key_bank(c), :].rearrange("p (h d) -> p h d", d=DK),
                                            Gk[:].unsqueeze(2).to_broadcast([P, HB, DK]), ALU.mult).then_inc(ks_done.sem, 1)

                def decayed_scores(b, c, r):
                    dve.wait_ge(a_ready.sem, a_ready.at(b, 2 * c + r + 1))
                    nc.vector.tensor_tensor(AD[:, c % 2, r], PS[:, r, :].rearrange("p (j t) -> p j t", t=P),
                                            D[:].rearrange("p (j r) t -> p r j t", r=2)[:, r],
                                            ALU.mult).then_inc(ad_done.sem, 1)

                def quotient(b, c, g):
                    n = 2 * c + g
                    O = PS[:, 2 + g, 0:HG * VA].rearrange("p (h a) -> p h a", a=VA)
                    dve.wait_ge(o_ready.sem, o_ready.at(b, n + 1))
                    nc.vector.tensor_scalar(den[:, g, :], O[:, :, DK], DEN_EPS, 2.0, ALU.add, ALU.mult).then_inc(den_done.sem, 1)
                    dve.wait_ge(den_done.sem, den_done.at(b, n + 1))
                    nc.vector.reciprocal(inv[:, g, :], den[:, g, :]).then_inc(inv_done.sem, 1)
                    dve.wait_ge(inv_done.sem, inv_done.at(b, n + 1))
                    nc.vector.tensor_tensor(y[:, c % 2, HG * DK * g:HG * DK * (g + 1)].rearrange("p (h d) -> p h d", d=DK),
                                            O[:, :, 0:DK], inv[:, g, :].unsqueeze(2).to_broadcast([P, HG, DK]),
                                            ALU.mult).then_inc(y_done.sem, 1)

                def update_state(b, c, g):
                    n = 2 * c + g
                    dve.wait_ge(st_ready.sem, st_ready.at(b, n + 1))
                    for jj in range(2):
                        j = 2 * g + jj
                        for r in range(2):
                            rows, cols = slice(r * DK, (r + 1) * DK), slice(r * VA, (r + 1) * VA)
                            new = PS[rows, ST_BANK[g], jj * 2 * VA + r * VA:jj * 2 * VA + (r + 1) * VA]
                            if c == 0:
                                last = nc.vector.tensor_copy(S[rows, j, cols], new)
                            else:
                                last = nc.vector.scalar_tensor_tensor(S[rows, j, cols], S[rows, j, cols], Gc[rows, j:j + 1],
                                                                      new, ALU.mult, ALU.add)
                    last.then_inc(s_done.sem, 1)

                def gated(b, ch):
                    c = ch % UT
                    dve.wait_ge(yt_ready.sem, yt_ready.at(b, ch + 1))
                    dve.wait_ge(gate_done.sem, gate_done.at(b, NP * (ch // UT + 1)))
                    dve.wait_ge(yg_lo_done.sem, yg_lo_done.at(b, ch))
                    nc.vector.scalar_tensor_tensor(yg, gate[:, :, c * P:(c + 1) * P], 1.0,
                                                   PS[:, 6, :].rearrange("p (j t) -> p j t", t=P),
                                                   ALU.add, ALU.mult).then_inc(yg_done.sem, 1)

                def residual(b, ch):
                    dve.wait_ge(out_ready.sem, out_ready.at(b, ch + 1))
                    x = X[:, bass.ds(b * TB + ch, 1), :].rearrange("p a m -> p (a m)")
                    nc.vector.tensor_tensor(x, PS[:, 7, 0:M], x, ALU.add).then_inc(x_done.sem, 1)

                def turn(b, first, last):
                    for half in range(NHALF):
                        c0 = UT * half
                        rest = half > 0 or not first
                        if rest:
                            gated(b, c0 - 1)
                        upcoming = next_of(b, half, last)
                        if upcoming:
                            nln, nsx, nturn = upcoming
                        for it in range(2 * NP):
                            phi_item(b, half, it)
                            if it >= UT - 1 and it < 2 * UT - 1 and upcoming:
                                nln.dve_tile_stats(dve, nturn, [it - (UT - 1)])
                            if rest and it in (1, 4):
                                residual(b, c0 - 2 + it // 4)
                        if upcoming:
                            nln.dve_aggregate(dve, nturn)
                        decayed_scores(b, c0, 0)
                        decayed_scores(b, c0, 1)
                        scaled_keys(b, c0)
                        if upcoming:
                            nln.dve_normalise(dve, nturn)
                        for c in range(UT):
                            ch = c0 + c
                            if c + 1 < UT:
                                decayed_scores(b, ch + 1, 0)
                                decayed_scores(b, ch + 1, 1)
                            elif upcoming:
                                nsx.dve(dve, nturn)
                            for g in range(2):
                                quotient(b, ch, g)
                                update_state(b, ch, g)
                            if c >= 1:
                                gated(b, ch - 1)
                            if c >= 2:
                                residual(b, ch - 2)
                            if c + 1 < UT:
                                scaled_keys(b, ch + 1)
                    if last:
                        gated(b, TB - 1)
                        residual(b, TB - 2)
                        residual(b, TB - 1)

                run_batches(dve, turn)

            @block.tensor
            def _(pe):
                if following:
                    following.sx.pe_open(pe)
                open_signals(pe, proj_ready, kt_ready, a_ready, o_ready, st_ready, yt_ready, out_ready)

                def projection(b, half, it):
                    c0 = UT * half
                    m = NITEM * half + it
                    n = 2 * NP * half + it
                    if it < 4:
                        freed = (s_done, y_done, y_done, s_done)[it]
                        pe.wait_ge(freed.sem, freed.at(b, 2 * c0 - 1 + it // 2))
                    elif it < 4 + 2 * NP:
                        pe.wait_ge(phi_done.sem, phi_done.at(b, n - 3))
                    else:
                        pe.wait_ge(gate_done.sem, gate_done.at(b, NP * half + it - 4 - 2 * NP + 1))
                    bank = PS[:, RING[m % 4], :]
                    if it < 2 * NP:
                        col = (it % 2) * HD + (it // 2) * P
                        ins = project(nc, bank, sx, w_hi, w_lo, slice(col, col + P))
                    elif it < 3 * NP:
                        col = 2 * HD + (it - 2 * NP) * P
                        ins = project(nc, bank, sx, w_hi, w_lo, slice(col, col + P))
                    else:
                        ins = project_tokens(nc, bank, sx, w_hi, w_lo, slice(3 * HD, 4 * HD), it - 3 * NP)
                    ins.then_inc(proj_ready.sem, 1)

                def keys(b, half, c):
                    ch = UT * half + c
                    if c == 0:
                        pe.wait_ge(yg_done.sem, yg_done.at(b, ch))
                    elif c == 1:
                        pe.wait_ge(x_done.sem, x_done.at(b, UT * half))
                    elif c == 2:
                        pe.wait_ge(ks_done.sem, ks_done.at(b, ch))
                    else:
                        pe.wait_ge(s_done.sem, s_done.at(b, 2 * ch))
                    for j in range(NP):
                        last = nc.tensor.transpose(PS[:, key_bank(ch), j * P:(j + 1) * P], kT[:, j, c * P:(c + 1) * P], ident[:])
                    last.then_inc(kt_ready.sem, 1)

                def scores(b, half, c):
                    n = 2 * (UT * half + c)
                    at = slice(c * P, (c + 1) * P)
                    pe.wait_ge(ad_done.sem, ad_done.at(b, n))
                    for j in range(NP):
                        for r in range(2):
                            rows = slice(r * DK, (r + 1) * DK)
                            last = nc.tensor.matmul(PS[:, r, j * P:(j + 1) * P], kT[rows, j, at], qT[rows, j, at],
                                                    start=True, stop=True)
                            if j == NP - 1:
                                last.then_inc(a_ready.sem, 1)

                def outputs(b, half, c, g):
                    ch = UT * half + c
                    n = 2 * ch + g
                    pe.wait_ge(ad_done.sem, ad_done.at(b, 2 * ch + 2))
                    pe.wait_ge(y_done.sem, y_done.at(b, n - 1))
                    pe.wait_ge(s_done.sem, s_done.at(b, n - 1))
                    bank = PS[:, 2 + g, 0:HG * VA]
                    for hh in range(HG):
                        last = nc.tensor.matmul(bank[:, hh * VA:(hh + 1) * VA], AD[:, ch % 2, hh % 2, 2 * g + hh // 2, :], v[:, c, HG * g + hh, :],
                                                start=hh == 0, stop=ch == 0, skip_group_check=True)
                    if ch > 0:
                        for jj in range(2):
                            j = 2 * g + jj
                            last = nc.tensor.matmul(bank[:, jj * 2 * VA:(jj + 1) * 2 * VA], qsT[:, j, c * P:(c + 1) * P],
                                                    S[:, j, :], start=False, stop=True, skip_group_check=True)
                    last.then_inc(o_ready.sem, 1)

                def state(b, half, c, g):
                    ch = UT * half + c
                    n = 2 * ch + g
                    pe.wait_ge(ks_done.sem, ks_done.at(b, ch + 1))
                    pe.wait_ge(s_done.sem, s_done.at(b, n - 1))
                    for jj in range(2):
                        j = 2 * g + jj
                        last = nc.tensor.matmul(PS[:, ST_BANK[g], jj * 2 * VA:(jj + 1) * 2 * VA],
                                                ks[:, 2 * j:2 * j + 2, :].rearrange("p h d -> p (h d)"),
                                                v[:, c, 2 * j:2 * j + 2, :].rearrange("p h a -> p (h a)"),
                                                start=True, stop=True)
                    last.then_inc(st_ready.sem, 1)

                def transposed_output(b, ch):
                    pe.wait_ge(y_done.sem, y_done.at(b, 2 * ch + 2))
                    pe.wait_ge(yg_done.sem, yg_done.at(b, ch))
                    for j in range(NP):
                        last = nc.tensor.transpose(PS[:, 6, j * P:(j + 1) * P], y[:, ch % 2, j * P:(j + 1) * P], ident[:])
                    last.then_inc(yt_ready.sem, 1)

                def out_projection(b, ch):
                    pe.wait_ge(yg_hi_done.sem, yg_hi_done.at(b, ch + 1))
                    pe.wait_ge(yg_lo_done.sem, yg_lo_done.at(b, ch + 1))
                    pe.wait_ge(x_done.sem, x_done.at(b, ch))
                    if ch >= 0 and ch % UT == 0:
                        pe.wait_ge(ks_done.sem, ks_done.at(b, ch + 3))
                    parts = [(g[:, j, :], w[:, j, :]) for j in range(NP)
                             for g, w in ((yg_hi, w_o_hi), (yg_hi, w_o_lo), (yg_lo, w_o_hi))]
                    for n, (g, w) in enumerate(parts):
                        last = nc.tensor.matmul(PS[:, 7, 0:M], g, w, start=n == 0, stop=n == len(parts) - 1)
                    last.then_inc(out_ready.sem, 1)

                def turn(b, first, last):
                    for half in range(NHALF):
                        c0 = UT * half
                        sx.pe_wait(pe, b * NHALF + half)
                        rest = half > 0 or not first
                        upcoming = next_of(b, half, last)
                        for it in range(NITEM):
                            if half == 0 and first and it < 2 * NP:
                                pe.wait_ge(prep_lo, it // 2 + 1)
                            if half == 0 and first and it == 2 * NP:
                                pe.wait_ge(prep_wo, 2)
                            projection(b, half, it)
                            if rest and it == 0:
                                transposed_output(b, c0 - 1)
                            if rest and it in (1, 4):
                                out_projection(b, c0 - 2 + it // 4)
                            if it == 3 * NP - 1:
                                pe.wait_ge(phi_done.sem, phi_done.at(b, 2 * NP * (half + 1)))
                                scores(b, half, 0)
                                keys(b, half, 0)
                        for c in range(UT):
                            ch = c0 + c
                            if c + 1 < UT:
                                scores(b, half, c + 1)
                            elif upcoming:
                                pe.wait_ge(ad_done.sem, ad_done.at(b, 2 * ch + 2))
                                upcoming[1].pe(pe, upcoming[2], upcoming[2])
                            if c == 0:
                                pe.wait_ge(v_done.sem, v_done.at(b, c0 + UT))
                                pe.wait_ge(qs_done.sem, qs_done.at(b, NP * (half + 1)))
                            for g in range(2):
                                outputs(b, half, c, g)
                                state(b, half, c, g)
                            if c >= 1:
                                transposed_output(b, ch - 1)
                            if c >= 2:
                                out_projection(b, ch - 2)
                            if c + 1 < UT:
                                keys(b, half, c + 1)
                    if last:
                        transposed_output(b, TB - 1)
                        out_projection(b, TB - 2)
                        out_projection(b, TB - 1)

                run_batches(pe, turn)


def build(nc, io):
    with ExitStack() as ctx:
        sb = lambda n, shape, dt=F32: ctx.enter_context(nc.sbuf_tensor(n, shape, dt))
        env = {
            "X": sb("X", [P, NT, M]),
            "ident": sb("ident", [P, P]),
            "stage": sb("stage", [P, STAGE]),
            "PS": ctx.enter_context(nc.psum_tensor("PS", [P, 8, UN], F32)),
            "ff_loaded": ctx.enter_context(nc.semaphore("ff_loaded")),
            "lin_loaded": ctx.enter_context(nc.semaphore("lin_loaded")),
        }
        env["stage"] = env["stage"][:, :]
        env["low_squares"], env["low_any"] = sb("low_squares", [P, NPART]), sb("low_any", [1, 1])
        for n in ("ff_high", "ff_low", "ff_squares", "low_transposed", "low_done", "norm_const"):
            env[n] = ctx.enter_context(nc.semaphore(n))
        env["norm"] = NormBuffers(nc, ctx)
        ff1, lin, ff2 = (Front(nc, ctx, n, env) for n in ("ff1", "lin", "ff2"))
        with nc.sbuf_tensor("ff_w_hi", [P, NW], F32R) as env["ff_w_hi"]:
            attention_phase(nc, env, io, ff1)
            feed_forward_phase(nc, env, io, "ff1", 1, ff1, lin)
        linear_attention_phase(nc, env, io, lin, ff2)
        feed_forward_phase(nc, env, io, "ff2", 2, ff2, None)


def kernel(L0_attn_a_x, L0_attn_a_wq, L0_attn_a_wk, L0_attn_a_wv, L0_attn_a_wo, L0_attn_b_W_Q, L0_attn_b_W_K,
           L0_attn_b_W_V, L0_attn_b_W_g_w, L0_attn_b_W_g_b, L0_attn_b_W_O, L0_attn_b_decay_log, L0_ffn_w_gate,
           L0_ffn_w_up, L0_ffn_w_down):
    import concourse.bacc as bacc
    from concourse.bass_utils import run_bass_kernel_spmd as run

    a = lambda v: np.ascontiguousarray(np.asarray(v))

    def heads(w):
        w0, w1 = a(w)[:, 0, :], a(w)[:, 1, :]
        return [w0, w1[:, ROT:], w1[:, :ROT]]

    w_qkv = np.concatenate(heads(L0_attn_a_wq) + heads(L0_attn_a_wk) + [a(L0_attn_a_wv).reshape(M, HA * DA)], axis=1)

    angle = np.power(np.float32(10000.0), -np.arange(HALF, dtype=np.float32) / np.float32(HALF)).astype(np.float32)
    rad = (angle[:, None] * np.arange(T, dtype=np.float32)[None, :]).astype(np.float32)
    c, s, one = np.cos(rad).astype(np.float32), np.sin(rad).astype(np.float32), np.ones((ROT, T), np.float32)
    cos = np.stack([np.concatenate([c, c, one]), np.concatenate([one, c, c])], axis=1)
    sin = np.concatenate([-s, s, -s, s])
    i = np.arange(P)
    causal = np.where(i[None, :] > i[:, None], np.float32(NEG), np.float32(0)).astype(np.float32)
    ahead = (i[None, :] - i[:, None]).astype(np.float32)
    dist = np.stack([np.maximum(ahead, 0), (ahead >= 0).astype(np.float32),
                     np.broadcast_to((i + 1).astype(np.float32), (P, P))], axis=1)

    d = a(L0_attn_b_decay_log)
    decay = np.concatenate([np.broadcast_to(d, (P, HB)), np.repeat(d.reshape(NP, 2).T, DK, axis=0)], axis=1)

    arrays = {
        "x": a(L0_attn_a_x), "w_qkv": a(w_qkv), "wo_a": a(L0_attn_a_wo).reshape(HA * DA, M),
        "ident": np.eye(P, dtype=np.float32), "causal": causal, "cos": a(cos), "sin": a(sin),
        "w_gate": a(a(L0_ffn_w_gate).T), "w_up": a(a(L0_ffn_w_up).T), "w_down": a(a(L0_ffn_w_down).T),
        "w_lin": a(np.concatenate([a(L0_attn_b_W_Q).T, a(L0_attn_b_W_K).T, a(L0_attn_b_W_g_w).T, a(L0_attn_b_W_V).T], axis=1)),
        "w_o": a(a(L0_attn_b_W_O).T), "b_g": a(a(L0_attn_b_W_g_b).reshape(NP, P).T), "decay": a(decay),
        "dist": a(dist), "rev": a((P - 1 - i).astype(np.float32)[:, None]),
    }
    nc = bacc.Bacc("TRN2", target_bir_lowering=False, num_devices=1)
    io = {}
    for name, v in arrays.items():
        io[name] = nc.dram_tensor(f"in_{name}", v.shape, mybir.dt.from_np(v.dtype), kind="ExternalInput").ap()
    io["out"] = nc.dram_tensor("out_x", (NB, T, M), F32, kind="ExternalOutput").ap()
    build(nc, io)
    r = run(nc, [{f"in_{k}": v for k, v in arrays.items()}], core_ids=[0])
    return r.results[0]["out_x"]
```
